# Optimizing a Trainium2 kernel written in Bass

```python
import numpy as np
import jax
import jax.numpy as jnp

def _softmax(x, axis=-1):
    return jax.nn.softmax(x, axis=axis)
def _gelu(x):
    return jax.nn.gelu(x, approximate=True)
def _silu(x):
    return jax.nn.silu(x)
def _sigmoid(x):
    return jax.nn.sigmoid(x)
def _layernorm(x, axis=-1, eps=1e-5):
    m = jnp.mean(x, axis=axis, keepdims=True)
    v = jnp.var(x, axis=axis, keepdims=True)
    return (x - m) / jnp.sqrt(v + eps)
def _scatter_add(tgt, idx, src, axis=0):
    return tgt.at[idx].add(src)
def _segment_sum(src, seg, n):
    return jax.ops.segment_sum(src, seg, n)

kernel_name = 'mk_conv_attn_hybrid_d2_conv_nchw256_ac2108'

def setup_inputs(seed: int = 0):
    np.random.seed(seed)
    _w = jnp.asarray
    def _rec_inputs():
        import jax
        import jax.numpy as jnp
        _gk = jax.random.key(seed)
        x = -0.0005207 + 1.001 * jax.random.normal(jax.random.fold_in(_gk, 1), (2, 256, 64, 64), jnp.float32)
        return x
    x = _rec_inputs()
    def _L0_conv_setup():
        import jax, jax.numpy as jnp
        import numpy as np
        CH = 256
        IN_C = CH // 2
        INTER_C = CH // 16
        NUM_POINTS = 32
        BN_EPS = 1e-05

        def conv1x1(x, W, b=None):
            y = jnp.einsum('oc,bchw->bohw', W, x)
            if b is not None:
                y = y + b[None, :, None, None]
            return y

        def bilinear_sample(feat, sx, sy):
            B, C, H, W = feat.shape
            x0f = jnp.floor(sx)
            y0f = jnp.floor(sy)
            wx = sx - x0f
            wy = sy - y0f
            x0 = jnp.clip(x0f.astype(jnp.int32), 0, W - 1)
            x1 = jnp.clip(x0f.astype(jnp.int32) + 1, 0, W - 1)
            y0 = jnp.clip(y0f.astype(jnp.int32), 0, H - 1)
            y1 = jnp.clip(y0f.astype(jnp.int32) + 1, 0, H - 1)
            feat_f = feat.reshape(B, C, H * W).transpose(0, 2, 1)

            def gather(yi, xi):
                idx = (yi * W + xi).reshape(B, -1)
                return jnp.take_along_axis(feat_f, idx[:, :, None], axis=1)
            wxf = wx.reshape(B, -1, 1)
            wyf = wy.reshape(B, -1, 1)
            out = gather(y0, x0) * (1 - wxf) * (1 - wyf) + gather(y0, x1) * wxf * (1 - wyf) + gather(y1, x0) * (1 - wxf) * wyf + gather(y1, x1) * wxf * wyf
            N, P = (sx.shape[1], sx.shape[2])
            return out.reshape(B, N, P, C)

        def multi_scale_attention(qf, vf, Wq, bq, Wk, bk, Wv, bv, Woff, boff):
            B, _, H, W = qf.shape
            N = H * W
            q = conv1x1(qf, Wq, bq).reshape(B, INTER_C, N).transpose(0, 2, 1)
            k = conv1x1(vf, Wk, bk)
            v = conv1x1(vf, Wv, bv)
            off = conv1x1(qf, Woff, boff).reshape(B, NUM_POINTS, 2, N)
            off = off.transpose(0, 3, 1, 2)
            ys, xs = jnp.meshgrid(jnp.arange(H, dtype=qf.dtype), jnp.arange(W, dtype=qf.dtype), indexing='ij')
            sx = xs.reshape(-1)[None, :, None] + off[..., 0]
            sy = ys.reshape(-1)[None, :, None] + off[..., 1]
            k_s = bilinear_sample(k, sx, sy)
            v_s = bilinear_sample(v, sx, sy)
            logits = jnp.einsum('bnc,bnpc->bnp', q, k_s) / jnp.sqrt(jnp.asarray(INTER_C, qf.dtype))
            attn = jax.nn.softmax(logits, axis=-1)
            out = jnp.einsum('bnp,bnpc->bnc', attn, v_s)
            return out.transpose(0, 2, 1).reshape(B, -1, H, W)
        key = jax.random.key(seed)
        ks = jax.random.split(key, 12)
        B, Hl, Wl, Hh, Wh = (2, 64, 64, 32, 32)
        s = 0.02
        return {'low_feature': jax.random.normal(ks[0], (B, CH, Hl, Wl), jnp.float32), 'high_feature': jax.random.normal(ks[1], (B, CH, Hh, Wh), jnp.float32), 'W1': jax.random.normal(ks[2], (IN_C, 2 * CH), jnp.float32) * s, 'b1': jnp.zeros((IN_C,), jnp.float32), 'W2': jax.random.normal(ks[3], (IN_C, CH), jnp.float32) * s, 'b2': jnp.zeros((IN_C,), jnp.float32), 'Wq': jax.random.normal(ks[4], (INTER_C, IN_C), jnp.float32) * s, 'bq': jnp.zeros((INTER_C,), jnp.float32), 'Wk': jax.random.normal(ks[5], (INTER_C, IN_C), jnp.float32) * s, 'bk': jnp.zeros((INTER_C,), jnp.float32), 'Wv': jax.random.normal(ks[6], (IN_C, IN_C), jnp.float32) * s, 'bv': jnp.zeros((IN_C,), jnp.float32), 'Woff': jax.random.normal(ks[7], (2 * NUM_POINTS, IN_C), jnp.float32) * 0.5, 'boff': jnp.zeros((2 * NUM_POINTS,), jnp.float32), 'Wb': jax.random.normal(ks[8], (CH, IN_C + CH), jnp.float32) * s, 'gamma': jnp.ones((CH,), jnp.float32), 'beta': jnp.zeros((CH,), jnp.float32), 'rmean': jnp.zeros((CH,), jnp.float32), 'rvar': jnp.ones((CH,), jnp.float32)}
    _L0_conv_all = _L0_conv_setup()
    _L0_conv_in = {k: v for k, v in _L0_conv_all.items() if k in ('high_feature', 'W1', 'b1', 'W2', 'b2', 'Wq', 'bq', 'Wk', 'bk', 'Wv', 'bv', 'Woff', 'boff', 'Wb', 'gamma', 'beta', 'rmean', 'rvar', )}
    del _L0_conv_all

    def _L1_attn_setup():
        import jax, jax.numpy as jnp
        import numpy as np
        EPS = 1e-05

        def _linear(x, w, b):
            return jnp.einsum('...i,oi->...o', x, w) + b

        def _l2_normalize(x, axis=-1):
            n = jnp.sqrt(jnp.sum(x * x, axis=axis, keepdims=True))
            return x / jnp.maximum(n, 1e-12)

        def _online_softmax_scan(sim):

            def combine(a, b):
                ma, sa = a
                mb, sb = b
                m = jnp.maximum(ma, mb)
                s = sa * jnp.exp(ma - m) + sb * jnp.exp(mb - m)
                return (m, s)
            m_scan, s_scan = jax.lax.associative_scan(combine, (sim, jnp.ones_like(sim)), axis=2)
            return (m_scan, s_scan)
        key = jax.random.key(seed)
        ks = jax.random.split(key, 8)
        B, L, D = (2, 2048, 256)
        H, h = (8, 32)
        s = 1.0 / np.sqrt(D)
        inp = {'x': jax.random.normal(ks[0], (B, L, D), jnp.float32), 'wq_w': jax.random.normal(ks[1], (D, D), jnp.float32) * s, 'wq_b': jnp.zeros((D,), jnp.float32), 'wk_w': jax.random.normal(ks[2], (D, D), jnp.float32) * s, 'wk_b': jnp.zeros((D,), jnp.float32), 'wv_w': jax.random.normal(ks[3], (D, D), jnp.float32) * s, 'wv_b': jnp.zeros((D,), jnp.float32), 'wo_w': jax.random.normal(ks[4], (D, D), jnp.float32) * s, 'wo_b': jnp.zeros((D,), jnp.float32), 'wg_w': jax.random.normal(ks[5], (1, h * h), jnp.float32) * (1.0 / np.sqrt(h * h)), 'wg_b': jnp.zeros((1,), jnp.float32), 'kv_norm_scale': jnp.ones((1, H, 1, h, h), jnp.float32), 'qk_norm_scale': jnp.full((1, H, 1), 1.0 / np.sqrt(h), jnp.float32)}
        return inp
    _L1_attn_all = _L1_attn_setup()
    _L1_attn_in = {k: v for k, v in _L1_attn_all.items() if k in ('wq_w', 'wq_b', 'wk_w', 'wk_b', 'wv_w', 'wv_b', 'wo_w', 'wo_b', 'wg_w', 'wg_b', 'kv_norm_scale', 'qk_norm_scale', )}
    del _L1_attn_all

    def _L1_ffn_setup():
        import jax, jax.numpy as jnp
        import numpy as np
        B, T, D, H, E = (16, 4096, 256, 512, 8)
        key = jax.random.key(seed)
        ks = jax.random.split(key, 5)
        x = jax.random.normal(ks[0], (B, T, D), dtype=jnp.float32)
        gate_w = jax.random.normal(ks[1], (D, E), dtype=jnp.float32) * 0.02
        gate_b = jnp.zeros((E,), dtype=jnp.float32)
        W1 = jax.random.normal(ks[2], (E, D, H), dtype=jnp.float32) * 0.02
        b1 = jnp.zeros((E, H), dtype=jnp.float32)
        W2 = jax.random.normal(ks[3], (E, H, D), dtype=jnp.float32) * 0.02
        b2 = jnp.zeros((E, D), dtype=jnp.float32)
        return {'x': x, 'gate_w': gate_w, 'gate_b': gate_b, 'W1': W1, 'b1': b1, 'W2': W2, 'b2': b2}
    _L1_ffn_all = _L1_ffn_setup()
    _L1_ffn_in = {k: v for k, v in _L1_ffn_all.items() if k in ('gate_w', 'gate_b', 'W1', 'b1', 'W2', 'b2', )}
    del _L1_ffn_all

    return {
        "x": x,
        "L0_conv_high_feature": _L0_conv_in["high_feature"],
        "L0_conv_W1": _L0_conv_in["W1"],
        "L0_conv_b1": _L0_conv_in["b1"],
        "L0_conv_W2": _L0_conv_in["W2"],
        "L0_conv_b2": _L0_conv_in["b2"],
        "L0_conv_Wq": _L0_conv_in["Wq"],
        "L0_conv_bq": _L0_conv_in["bq"],
        "L0_conv_Wk": _L0_conv_in["Wk"],
        "L0_conv_bk": _L0_conv_in["bk"],
        "L0_conv_Wv": _L0_conv_in["Wv"],
        "L0_conv_bv": _L0_conv_in["bv"],
        "L0_conv_Woff": _L0_conv_in["Woff"],
        "L0_conv_boff": _L0_conv_in["boff"],
        "L0_conv_Wb": _L0_conv_in["Wb"],
        "L0_conv_gamma": _L0_conv_in["gamma"],
        "L0_conv_beta": _L0_conv_in["beta"],
        "L0_conv_rmean": _L0_conv_in["rmean"],
        "L0_conv_rvar": _L0_conv_in["rvar"],
        "L1_attn_wq_w": _L1_attn_in["wq_w"],
        "L1_attn_wq_b": _L1_attn_in["wq_b"],
        "L1_attn_wk_w": _L1_attn_in["wk_w"],
        "L1_attn_wk_b": _L1_attn_in["wk_b"],
        "L1_attn_wv_w": _L1_attn_in["wv_w"],
        "L1_attn_wv_b": _L1_attn_in["wv_b"],
        "L1_attn_wo_w": _L1_attn_in["wo_w"],
        "L1_attn_wo_b": _L1_attn_in["wo_b"],
        "L1_attn_wg_w": _L1_attn_in["wg_w"],
        "L1_attn_wg_b": _L1_attn_in["wg_b"],
        "L1_attn_kv_norm_scale": _L1_attn_in["kv_norm_scale"],
        "L1_attn_qk_norm_scale": _L1_attn_in["qk_norm_scale"],
        "L1_ffn_gate_w": _L1_ffn_in["gate_w"],
        "L1_ffn_gate_b": _L1_ffn_in["gate_b"],
        "L1_ffn_W1": _L1_ffn_in["W1"],
        "L1_ffn_b1": _L1_ffn_in["b1"],
        "L1_ffn_W2": _L1_ffn_in["W2"],
        "L1_ffn_b2": _L1_ffn_in["b2"],
    }

def reference(x, L0_conv_high_feature, L0_conv_W1, L0_conv_b1, L0_conv_W2, L0_conv_b2, L0_conv_Wq, L0_conv_bq, L0_conv_Wk, L0_conv_bk, L0_conv_Wv, L0_conv_bv, L0_conv_Woff, L0_conv_boff, L0_conv_Wb, L0_conv_gamma, L0_conv_beta, L0_conv_rmean, L0_conv_rvar, L1_attn_wq_w, L1_attn_wq_b, L1_attn_wk_w, L1_attn_wk_b, L1_attn_wv_w, L1_attn_wv_b, L1_attn_wo_w, L1_attn_wo_b, L1_attn_wg_w, L1_attn_wg_b, L1_attn_kv_norm_scale, L1_attn_qk_norm_scale, L1_ffn_gate_w, L1_ffn_gate_b, L1_ffn_W1, L1_ffn_b1, L1_ffn_W2, L1_ffn_b2):
    import jax
    import jax.numpy as jnp
    def _L0_conv_ref(low_feature, high_feature, W1, b1, W2, b2, Wq, bq, Wk, bk, Wv, bv, Woff, boff, Wb, gamma, beta, rmean, rvar):
        import jax, jax.numpy as jnp
        import numpy as np
        CH = 256
        IN_C = CH // 2
        INTER_C = CH // 16
        NUM_POINTS = 32
        BN_EPS = 1e-05

        def conv1x1(x, W, b=None):
            y = jnp.einsum('oc,bchw->bohw', W, x)
            if b is not None:
                y = y + b[None, :, None, None]
            return y

        def bilinear_sample(feat, sx, sy):
            B, C, H, W = feat.shape
            x0f = jnp.floor(sx)
            y0f = jnp.floor(sy)
            wx = sx - x0f
            wy = sy - y0f
            x0 = jnp.clip(x0f.astype(jnp.int32), 0, W - 1)
            x1 = jnp.clip(x0f.astype(jnp.int32) + 1, 0, W - 1)
            y0 = jnp.clip(y0f.astype(jnp.int32), 0, H - 1)
            y1 = jnp.clip(y0f.astype(jnp.int32) + 1, 0, H - 1)
            feat_f = feat.reshape(B, C, H * W).transpose(0, 2, 1)

            def gather(yi, xi):
                idx = (yi * W + xi).reshape(B, -1)
                return jnp.take_along_axis(feat_f, idx[:, :, None], axis=1)
            wxf = wx.reshape(B, -1, 1)
            wyf = wy.reshape(B, -1, 1)
            out = gather(y0, x0) * (1 - wxf) * (1 - wyf) + gather(y0, x1) * wxf * (1 - wyf) + gather(y1, x0) * (1 - wxf) * wyf + gather(y1, x1) * wxf * wyf
            N, P = (sx.shape[1], sx.shape[2])
            return out.reshape(B, N, P, C)

        def multi_scale_attention(qf, vf, Wq, bq, Wk, bk, Wv, bv, Woff, boff):
            B, _, H, W = qf.shape
            N = H * W
            q = conv1x1(qf, Wq, bq).reshape(B, INTER_C, N).transpose(0, 2, 1)
            k = conv1x1(vf, Wk, bk)
            v = conv1x1(vf, Wv, bv)
            off = conv1x1(qf, Woff, boff).reshape(B, NUM_POINTS, 2, N)
            off = off.transpose(0, 3, 1, 2)
            ys, xs = jnp.meshgrid(jnp.arange(H, dtype=qf.dtype), jnp.arange(W, dtype=qf.dtype), indexing='ij')
            sx = xs.reshape(-1)[None, :, None] + off[..., 0]
            sy = ys.reshape(-1)[None, :, None] + off[..., 1]
            k_s = bilinear_sample(k, sx, sy)
            v_s = bilinear_sample(v, sx, sy)
            logits = jnp.einsum('bnc,bnpc->bnp', q, k_s) / jnp.sqrt(jnp.asarray(INTER_C, qf.dtype))
            attn = jax.nn.softmax(logits, axis=-1)
            out = jnp.einsum('bnp,bnpc->bnc', attn, v_s)
            return out.transpose(0, 2, 1).reshape(B, -1, H, W)
        B, _, Hl, Wl = low_feature.shape
        high_up = jax.image.resize(high_feature, (B, CH, Hl, Wl), method='bilinear')
        query_feature = conv1x1(jnp.concatenate([high_up, low_feature], axis=1), W1, b1)
        value_feature = conv1x1(high_up, W2, b2)
        value_feature = multi_scale_attention(query_feature, value_feature, Wq, bq, Wk, bk, Wv, bv, Woff, boff)
        x = conv1x1(jnp.concatenate([value_feature, high_up], axis=1), Wb)
        x = (x - rmean[None, :, None, None]) * jax.lax.rsqrt(rvar + BN_EPS)[None, :, None, None]
        x = x * gamma[None, :, None, None] + beta[None, :, None, None]
        return jax.nn.relu(x)

    def _L1_attn_ref(x, wq_w, wq_b, wk_w, wk_b, wv_w, wv_b, wo_w, wo_b, wg_w, wg_b, kv_norm_scale, qk_norm_scale):
        import jax, jax.numpy as jnp
        import numpy as np
        EPS = 1e-05

        def _linear(x, w, b):
            return jnp.einsum('...i,oi->...o', x, w) + b

        def _l2_normalize(x, axis=-1):
            n = jnp.sqrt(jnp.sum(x * x, axis=axis, keepdims=True))
            return x / jnp.maximum(n, 1e-12)

        def _online_softmax_scan(sim):

            def combine(a, b):
                ma, sa = a
                mb, sb = b
                m = jnp.maximum(ma, mb)
                s = sa * jnp.exp(ma - m) + sb * jnp.exp(mb - m)
                return (m, s)
            m_scan, s_scan = jax.lax.associative_scan(combine, (sim, jnp.ones_like(sim)), axis=2)
            return (m_scan, s_scan)
        B, L, D = x.shape
        H, h = (kv_norm_scale.shape[1], kv_norm_scale.shape[3])
        q = _linear(x, wq_w, wq_b).reshape(B, L, H, h).transpose(0, 2, 1, 3)
        k = _linear(x, wk_w, wk_b).reshape(B, L, H, h).transpose(0, 2, 1, 3)
        v = _linear(x, wv_w, wv_b).reshape(B, L, H, h).transpose(0, 2, 1, 3)
        sim = jnp.einsum('bhld,bhld->bhl', q, k) * qk_norm_scale
        k = _l2_normalize(k)
        v = _l2_normalize(v)
        Z = jnp.einsum('bhld,bhle->bhlde', v, k) * kv_norm_scale
        gate_inputs = Z.reshape(B, H, L, h * h)
        gates_logits = jnp.einsum('bhli,oi->bhlo', gate_inputs, wg_w) + wg_b
        gates = jnp.square(jax.nn.relu(gates_logits)) + EPS
        gates = gates[..., None]
        gated_Z = gates * Z
        m_scan, s_scan = _online_softmax_scan(sim)
        Z_scan = jnp.cumsum(gated_Z, axis=2)
        g_scan = jnp.cumsum(gates, axis=2)
        softmax_weights = (jnp.exp(sim - m_scan) / (s_scan + EPS))[..., None, None]
        gated_weights = Z_scan / (g_scan + EPS)
        attn_weights = gated_weights * (1.0 + jax.nn.silu(softmax_weights))
        ctxt = jnp.einsum('bhld,bhlde->bhle', q, attn_weights)
        ctxt = ctxt.transpose(0, 2, 1, 3).reshape(B, L, D)
        return _linear(ctxt, wo_w, wo_b)

    def _L1_ffn_ref(x, gate_w, gate_b, W1, b1, W2, b2):
        import jax, jax.numpy as jnp
        import numpy as np
        B, T, D, H, E = (16, 4096, 256, 512, 8)
        Bb, Tt, Dd = x.shape
        Ee = gate_w.shape[1]
        xf = x.reshape(-1, Dd)
        N = xf.shape[0]
        logits = xf @ gate_w + gate_b
        probs = jax.nn.softmax(logits, axis=-1)
        top2_vals, top2_idx = jax.lax.top_k(probs, 2)
        cw = jnp.zeros((N, Ee), dtype=xf.dtype).at[jnp.arange(N)[:, None], top2_idx].add(top2_vals)

        def step(acc, params):
            w1, bb1, w2, bb2, we = params
            h = jax.nn.gelu(xf @ w1 + bb1, approximate=False)
            y = h @ w2 + bb2
            return (acc + we[:, None] * y, None)
        out, _ = jax.lax.scan(step, jnp.zeros_like(xf), (W1, b1, W2, b2, cw.T))
        return out.reshape(Bb, Tt, Dd)

    def _gn(v, G=32, eps=1e-5):
        B_, C_, H_, W_ = v.shape
        g = v.reshape(B_, G, C_ // G, H_, W_)
        m = jnp.mean(g, axis=(2, 3, 4), keepdims=True)
        s = jnp.var(g, axis=(2, 3, 4), keepdims=True)
        return ((g - m) / jnp.sqrt(s + eps)).reshape(v.shape)

    def _ln_c(v, eps=1e-6):
        m = jnp.mean(v, axis=1, keepdims=True)
        s = jnp.var(v, axis=1, keepdims=True)
        return (v - m) / jnp.sqrt(s + eps)

    def _ln_t(v, eps=1e-5):
        m = jnp.mean(v, axis=-1, keepdims=True)
        s = jnp.var(v, axis=-1, keepdims=True)
        return (v - m) / jnp.sqrt(s + eps)

    def _to_tokens(v):
        B_, C_, H_, W_ = v.shape
        return v.reshape(B_, C_, H_ * W_).transpose(0, 2, 1)
    def _from_tokens(t, like):
        B_, C_, H_, W_ = like.shape
        return t.transpose(0, 2, 1).reshape(B_, C_, H_, W_)

    x = x + _L0_conv_ref(_gn(x), L0_conv_high_feature, L0_conv_W1, L0_conv_b1, L0_conv_W2, L0_conv_b2, L0_conv_Wq, L0_conv_bq, L0_conv_Wk, L0_conv_bk, L0_conv_Wv, L0_conv_bv, L0_conv_Woff, L0_conv_boff, L0_conv_Wb, L0_conv_gamma, L0_conv_beta, L0_conv_rmean, L0_conv_rvar)
    t = _to_tokens(x)
    t = t + _L1_attn_ref(_ln_t(t), L1_attn_wq_w, L1_attn_wq_b, L1_attn_wk_w, L1_attn_wk_b, L1_attn_wv_w, L1_attn_wv_b, L1_attn_wo_w, L1_attn_wo_b, L1_attn_wg_w, L1_attn_wg_b, L1_attn_kv_norm_scale, L1_attn_qk_norm_scale)
    t = t + _L1_ffn_ref(_ln_t(t), L1_ffn_gate_w, L1_ffn_gate_b, L1_ffn_W1, L1_ffn_b1, L1_ffn_W2, L1_ffn_b2)
    x = _from_tokens(t, x)
    return x


_drawn_inputs = setup_inputs


def setup_inputs(seed=0):
    import zlib

    import numpy as np

    out = dict(_drawn_inputs(seed))
    spreads = {'L0_conv_b1': (0.0, 0.8),
     'L0_conv_b2': (0.0, 0.8),
     'L0_conv_bq': (0.0, 0.8),
     'L0_conv_bk': (0.0, 0.8),
     'L0_conv_bv': (0.0, 0.464),
     'L0_conv_boff': (0.0, 0.8),
     'L0_conv_gamma': (1.0, 0.2),
     'L0_conv_beta': (0.0, 0.1),
     'L0_conv_rmean': (0.0, 0.1),
     'L0_conv_rvar': (1.0, 0.6),
     'L1_attn_wq_b': (0.0, 0.8),
     'L1_attn_wk_b': (0.0, 0.8),
     'L1_attn_wv_b': (0.0, 0.8),
     'L1_attn_wo_b': (0.0, 0.1),
     'L1_attn_kv_norm_scale': (1.0, 0.6),
     'L1_attn_qk_norm_scale': (0.1767766922712326, 0.6),
     'L1_ffn_gate_b': (0.0, 0.579),
     'L1_ffn_b1': (0.0, 0.8),
     'L1_ffn_b2': (0.0, 0.322)}
    factors = {'L0_conv_W1': 8.0,
     'L0_conv_W2': 8.0,
     'L0_conv_Wq': 8.0,
     'L0_conv_Wk': 8.0,
     'L0_conv_Wv': 8.0,
     'L0_conv_Woff': 8.0,
     'L1_attn_wg_w': 2.834,
     'L1_ffn_W1': 2.968,
     'L1_ffn_W2': 2.765}
    for name, (base, spread) in spreads.items():
        noise = np.random.default_rng([zlib.crc32(name.encode()), seed]).standard_normal(out[name].shape)
        drawn = base * np.exp(spread * noise) if base else spread * noise
        out[name] = jnp.asarray(drawn.astype(out[name].dtype))
    for name, factor in factors.items():
        out[name] = (out[name] * factor).astype(out[name].dtype)
    return out
```

```python
from contextlib import ExitStack

import numpy as np
import concourse.bass as bass
from concourse import mybir

ALU = mybir.AluOpType
ACT = mybir.ActivationFunctionType
AX = mybir.AxisListType
F32 = mybir.dt.float32

P = 128
BATCH = 2
HALVES = 2
CHUNK = 512
CHUNKS = 8
TOKENS = CHUNK * CHUNKS
HEADS = 8
EXPERTS = 8
LN_EPS = 1e-5


class Track:

    def __init__(self, ctx, nc, name, steps):
        self.sem = ctx.enter_context(nc.semaphore(name))
        self.steps = steps
        self.place = {s: i + 1 for i, s in enumerate(steps)}
        assert len(self.place) == len(steps), name
        self.per = len(steps)
        self.emitted = 0

    def credit(self, eng):
        eng.sem_inc(self.sem, self.per)

    def done(self, step):
        assert self.steps[self.emitted % self.per] == step, (step, self.steps[self.emitted % self.per])
        self.emitted += 1
        return self.sem

    def upto(self, t, step):
        return t * self.per + (self.per + self.place[step])

    def last_turn(self, t, step):
        return t * self.per + self.place[step]

    def so_far(self, t):
        return t * self.per + (self.per + self.emitted % self.per)


class Loads:

    def __init__(self, ctx, nc, name, per=1):
        self.sem = ctx.enter_context(nc.semaphore(name))
        self.per = per

    def upto(self, t):
        return t * (16 * self.per) + 16 * self.per


def chunk_of(dram, index):
    return dram[bass.ds(index, 1)].rearrange("o p k n -> (o p) k n")


SIDE = 64
POINTS = 32
ROWPAIRS = SIDE // 2
LANES = 4
CELLS = SIDE // 2
QC = 16


def norm_phase(nc, x_dram, group_mean, gamma, beta, rmean, rvar, gn, bn):
    n = BATCH * HALVES
    with ExitStack() as ctx:
        def sb(name, shape):
            return ctx.enter_context(nc.sbuf_tensor("gn_" + name, shape, F32))
        x_sb = sb("x", [P, BATCH * CHUNKS, HALVES, CHUNK])
        avg = sb("avg", [P, P])
        stats = sb("stats", [P, n, CHUNKS, 6])
        mv = sb("mv", [P, n, 2])
        off = sb("off", [P, n])
        spread = sb("spread", [P, n])
        par = sb("par", [P, 4, HALVES])
        means = ctx.enter_context(nc.psum_tensor("gn_means", [P, n], F32))
        variances = ctx.enter_context(nc.psum_tensor("gn_vars", [P, n], F32))
        ready = ctx.enter_context(nc.semaphore("gn_constants"))
        parts = [Loads(ctx, nc, f"gn_x_loaded{i}") for i in range(4)]
        dve_t = Track(ctx, nc, "gn_dve", [f"stats{i}" for i in range(n * CHUNKS)] + [f"mv{i}" for i in range(n)]
                      + "off offsq spread eps inv shift rv_eps rv_inv scale bias0 bias".split())
        pe_t = Track(ctx, nc, "gn_pe", ["mean", "var"])
        act_t = Track(ctx, nc, "gn_act", ["std", "rv_std"])
        block = ctx.enter_context(nc.Block())

        @block.sync
        def _(sp):
            for i in range(4):
                sp.dma_start(x_sb[:, 4 * i:4 * i + 4], x_dram[4 * i:4 * i + 4].rearrange("c p k n -> p c k n")).then_inc(parts[i].sem, 16)
            sp.dma_start(avg[:], group_mean).then_inc(ready, 16)
            for i, src in enumerate((gamma, beta, rmean, rvar)):
                sp.dma_start(par[:, i], src).then_inc(ready, 16)

        @block.tensor
        def _(pe):
            pe_t.credit(pe)
            pe.wait_ge(ready, 80)
            pe.wait_ge(dve_t.sem, dve_t.upto(0, f"mv{n - 1}"))
            nc.tensor.matmul(means[:], avg[:], mv[:, :, 0], start=True, stop=True).then_inc(pe_t.done("mean"), 1)
            pe.wait_ge(dve_t.sem, dve_t.upto(0, "spread"))
            nc.tensor.matmul(variances[:], avg[:], spread[:], start=True, stop=True).then_inc(pe_t.done("var"), 1)

        @block.scalar
        def _(act):
            act_t.credit(act)
            act.wait_ge(dve_t.sem, dve_t.upto(0, "eps"))
            nc.scalar.activation(gn[:, :, 0], gn[:, :, 0], ACT.Sqrt).then_inc(act_t.done("std"), 1)
            act.wait_ge(dve_t.sem, dve_t.upto(0, "rv_eps"))
            nc.scalar.activation(bn[:, :, 0], bn[:, :, 0], ACT.Sqrt).then_inc(act_t.done("rv_std"), 1)

        @block.vector
        def _(v):
            dve_t.credit(v)

            def own():
                v.wait_ge(dve_t.sem, dve_t.so_far(0))
            i = 0
            for c in range(BATCH * CHUNKS):
                if c % 4 == 0:
                    v.wait_ge(parts[c // 4].sem, 16)
                for h in range(HALVES):
                    nc.vector.bn_stats(stats[:, c // CHUNKS * HALVES + h, c % CHUNKS], x_sb[:, c, h]).then_inc(dve_t.done(f"stats{i}"), 1)
                    i += 1
            own()
            for i in range(n):
                nc.vector.bn_aggr(mv[:, i], stats[:, i].rearrange("p c s -> p (c s)")).then_inc(dve_t.done(f"mv{i}"), 1)
            v.wait_ge(pe_t.sem, pe_t.upto(0, "mean"))
            own()
            nc.vector.tensor_tensor(off[:], mv[:, :, 0], means[:], ALU.subtract).then_inc(dve_t.done("off"), 1)
            own()
            nc.vector.tensor_tensor(off[:], off[:], off[:], ALU.mult).then_inc(dve_t.done("offsq"), 1)
            own()
            nc.vector.tensor_tensor(spread[:], off[:], mv[:, :, 1], ALU.add).then_inc(dve_t.done("spread"), 1)
            v.wait_ge(pe_t.sem, pe_t.upto(0, "var"))
            nc.vector.tensor_scalar_add(gn[:, :, 0], variances[:], LN_EPS).then_inc(dve_t.done("eps"), 1)
            v.wait_ge(act_t.sem, act_t.upto(0, "std"))
            nc.vector.reciprocal(gn[:, :, 0], gn[:, :, 0]).then_inc(dve_t.done("inv"), 1)
            own()
            nc.vector.scalar_tensor_tensor(gn[:, :, 1], means[:], -1.0, gn[:, :, 0], ALU.mult, ALU.mult).then_inc(dve_t.done("shift"), 1)
            v.wait_ge(ready, 80)
            nc.vector.tensor_scalar_add(bn[:, :, 0], par[:, 3], LN_EPS).then_inc(dve_t.done("rv_eps"), 1)
            v.wait_ge(act_t.sem, act_t.upto(0, "rv_std"))
            nc.vector.reciprocal(bn[:, :, 0], bn[:, :, 0]).then_inc(dve_t.done("rv_inv"), 1)
            own()
            nc.vector.tensor_tensor(bn[:, :, 0], bn[:, :, 0], par[:, 0], ALU.mult).then_inc(dve_t.done("scale"), 1)
            own()
            nc.vector.tensor_tensor(bn[:, :, 1], par[:, 2], bn[:, :, 0], ALU.mult).then_inc(dve_t.done("bias0"), 1)
            own()
            nc.vector.tensor_tensor(bn[:, :, 1], par[:, 1], bn[:, :, 1], ALU.subtract).then_inc(dve_t.done("bias"), 1)


def upsample_phase(nc, b, high, up):
    S = SIDE // 2
    with ExitStack() as ctx:
        bufs = []
        for h in range(HALVES):
            def sb(name, shape):
                return ctx.enter_context(nc.sbuf_tensor(f"up{b}{h}_{name}", shape, F32))
            bufs.append((sb("in", [P, S, S]), sb("q", [P, S, S + 2]), sb("t", [P, S, S]), sb("wide", [P, S, S, 2])))
        tall_q = ctx.enter_context(nc.sbuf_tensor(f"up{b}_tq", [P, S + 2, SIDE], F32))
        tall_t = ctx.enter_context(nc.sbuf_tensor(f"up{b}_tt", [P, S, SIDE], F32))
        loaded = [ctx.enter_context(nc.semaphore(f"up{b}_loaded{h}")) for h in range(HALVES)]
        wide_steps = "q q_left q_right t even odd".split()
        tall_steps = "tq tq_top tq_bottom tt rows_even rows_odd".split()
        wide_t = [Track(ctx, nc, f"up{b}_wide{h}", wide_steps) for h in range(HALVES)]
        tall_t_ = Track(ctx, nc, f"up{b}_tall", [f"{s}{h}" for h in range(HALVES) for s in tall_steps])
        block = ctx.enter_context(nc.Block())

        def widen(eng, ops, h):
            tr = wide_t[h]
            tr.credit(eng)
            src, q, t, wide = bufs[h]
            eng.wait_ge(loaded[h], 16)
            ops.tensor_scalar(q[:, :, 1:S + 1], src[:], 0.25, None, ALU.mult).then_inc(tr.done("q"), 1)
            ops.tensor_scalar(q[:, :, 0:1], src[:, :, 0:1], 0.25, None, ALU.mult).then_inc(tr.done("q_left"), 1)
            ops.tensor_scalar(q[:, :, S + 1:], src[:, :, S - 1:], 0.25, None, ALU.mult).then_inc(tr.done("q_right"), 1)
            ops.tensor_scalar(t[:], src[:], 0.75, None, ALU.mult).then_inc(tr.done("t"), 1)
            eng.wait_ge(tr.sem, tr.upto(0, "t"))
            ops.tensor_tensor(wide[:, :, :, 0], q[:, :, 0:S], t[:], ALU.add).then_inc(tr.done("even"), 1)
            ops.tensor_tensor(wide[:, :, :, 1], q[:, :, 2:], t[:], ALU.add).then_inc(tr.done("odd"), 1)

        @block.sync
        def _(sp):
            for h in range(HALVES):
                sp.dma_start(bufs[h][0][:], high[b, :, h].rearrange("p (y x) -> p y x", x=S)).then_inc(loaded[h], 16)

        @block.gpsimd
        def _(pool):
            widen(pool, nc.gpsimd, 1)

        @block.vector
        def _(v):
            widen(v, nc.vector, 0)
            tr = tall_t_
            tr.credit(v)
            for h in range(HALVES):
                wide = bufs[h][3][:].rearrange("p y x e -> p y (x e)")
                rows = up[:, h].rearrange("p (y e x) -> p y e x", e=2, x=SIDE)
                v.wait_ge(wide_t[h].sem, wide_t[h].upto(0, "odd"))
                v.wait_ge(tr.sem, tr.so_far(0))
                nc.vector.tensor_scalar(tall_q[:, 1:S + 1], wide, 0.25, None, ALU.mult).then_inc(tr.done(f"tq{h}"), 1)
                nc.vector.tensor_scalar(tall_q[:, 0:1], wide[:, 0:1], 0.25, None, ALU.mult).then_inc(tr.done(f"tq_top{h}"), 1)
                nc.vector.tensor_scalar(tall_q[:, S + 1:], wide[:, S - 1:], 0.25, None, ALU.mult).then_inc(tr.done(f"tq_bottom{h}"), 1)
                nc.vector.tensor_scalar(tall_t[:], wide, 0.75, None, ALU.mult).then_inc(tr.done(f"tt{h}"), 1)
                v.wait_ge(tr.sem, tr.so_far(0))
                nc.vector.tensor_tensor(rows[:, :, 0], tall_q[:, 0:S], tall_t[:], ALU.add).then_inc(tr.done(f"rows_even{h}"), 1)
                nc.vector.tensor_tensor(rows[:, :, 1], tall_q[:, 2:], tall_t[:], ALU.add).then_inc(tr.done(f"rows_odd{h}"), 1)


def features_phase(nc, b, x_dram, base_dram, w, gn, up, qf, vf):
    with ExitStack() as ctx:
        def sb(name, shape):
            return ctx.enter_context(nc.sbuf_tensor(f"fe{b}_{name}", shape, F32))
        w1 = sb("w1", [P, 4, P])
        w2 = sb("w2", [P, HALVES, P])
        wb = sb("wb", [P, HALVES, 256])
        b1 = sb("b1", [P, 1])
        b2 = sb("b2", [P, 1])
        x_sb = sb("x", [P, HALVES, CHUNK])
        xg = sb("xg", [P, HALVES, CHUNK])
        base = sb("base", [P, HALVES, CHUNK])
        ps = ctx.enter_context(nc.psum_tensor(f"fe{b}_ps", [P, 2, 512], F32))
        ps_base = ctx.enter_context(nc.psum_tensor(f"fe{b}_psb", [P, HALVES, 512], F32))
        ready = ctx.enter_context(nc.semaphore(f"fe{b}_constants"))
        loads = Loads(ctx, nc, f"fe{b}_x_loaded")
        stores = Loads(ctx, nc, f"fe{b}_stored")
        pe_t = Track(ctx, nc, f"fe{b}_pe", ["vf", "base", "qf"])
        act_t = Track(ctx, nc, f"fe{b}_act", ["gn0", "gn1", "qf"])
        dve_t = Track(ctx, nc, f"fe{b}_dve", ["vf", "base"])
        stored_t = Track(ctx, nc, f"fe{b}_base_stored", ["stored"])
        consts = [(w1, w["w1"]), (w2, w["w2"]), (wb, w["wbh"]), (b1, w["b1"]), (b2, w["b2"])]
        block = ctx.enter_context(nc.Block())

        @block.sync
        def _(sp):
            for dst, src in consts:
                sp.dma_start(dst[:], src).then_inc(ready, 16)
            with sp.Fori(0, CHUNKS) as t:
                sp.wait_ge(act_t.sem, act_t.last_turn(t, "gn1"))
                sp.dma_start(x_sb[:], chunk_of(x_dram, t + b * CHUNKS)).then_inc(loads.sem, 16)

        @block.gpsimd
        def _(pool):
            stored_t.credit(pool)
            with pool.Fori(0, CHUNKS) as t:
                pool.wait_ge(dve_t.sem, dve_t.upto(t, "base"))
                pool.dma_start(chunk_of(base_dram, t + b * CHUNKS), base[:]).then_inc(stores.sem, 16)
                pool.wait_ge(stores.sem, stores.upto(t))
                pool.sem_inc(stored_t.done("stored"), 1)

        @block.tensor
        def _(pe):
            pe_t.credit(pe)
            pe.wait_ge(ready, 16 * len(consts))
            with pe.Fori(0, CHUNKS) as t:
                u = [up[:, k, bass.ds(t * CHUNK, CHUNK)] for k in range(HALVES)]
                pe.wait_ge(dve_t.sem, dve_t.last_turn(t, "vf"))
                for k in range(HALVES):
                    mm = nc.tensor.matmul(ps[:, 1], w2[:, k], u[k], start=(k == 0), stop=(k == 1))
                mm.then_inc(pe_t.done("vf"), 1)
                pe.wait_ge(dve_t.sem, dve_t.last_turn(t, "base"))
                for h in range(HALVES):
                    for k in range(HALVES):
                        mm = nc.tensor.matmul(ps_base[:, h], wb[:, k, h * P:(h + 1) * P], u[k], start=(k == 0), stop=(k == 1))
                mm.then_inc(pe_t.done("base"), 1)
                pe.wait_ge(act_t.sem, act_t.upto(t, "gn1"))
                for k in range(4):
                    mm = nc.tensor.matmul(ps[:, 0], w1[:, k], u[k] if k < 2 else xg[:, k - 2], start=(k == 0), stop=(k == 3))
                mm.then_inc(pe_t.done("qf"), 1)

        @block.scalar
        def _(act):
            act_t.credit(act)
            act.wait_ge(ready, 16 * len(consts))
            with act.Fori(0, CHUNKS) as t:
                act.wait_ge(loads.sem, loads.upto(t))
                act.wait_ge(pe_t.sem, pe_t.last_turn(t, "qf"))
                for h in range(HALVES):
                    g = b * HALVES + h
                    nc.scalar.activation(xg[:, h], x_sb[:, h], ACT.Identity, bias=gn[:, g, 1:2], scale=gn[:, g, 0:1]).then_inc(act_t.done(f"gn{h}"), 1)
                act.wait_ge(pe_t.sem, pe_t.upto(t, "qf"))
                nc.scalar.activation(qf[:, bass.ds(t * CHUNK, CHUNK)], ps[:, 0], ACT.Identity, bias=b1[:]).then_inc(act_t.done("qf"), 1)

        @block.vector
        def _(v):
            dve_t.credit(v)
            v.wait_ge(ready, 16 * len(consts))
            with v.Fori(0, CHUNKS) as t:
                v.wait_ge(pe_t.sem, pe_t.upto(t, "vf"))
                nc.vector.tensor_scalar(vf[:, bass.ds(t * CHUNK, CHUNK)], ps[:, 1], b2[:], None, ALU.add).then_inc(dve_t.done("vf"), 1)
                v.wait_ge(pe_t.sem, pe_t.upto(t, "base"))
                v.wait_ge(stored_t.sem, stored_t.last_turn(t, "stored"))
                nc.vector.tensor_copy(base[:], ps_base[:]).then_inc(dve_t.done("base"), 1)


def tables_phase(nc, b, w, coords, qf, vf, q_rows, k_table, v_table, where):
    with ExitStack() as ctx:
        def sb(name, shape):
            return ctx.enter_context(nc.sbuf_tensor(f"ta{b}_{name}", shape, F32))
        wq, wk, wv, woff = sb("wq", [P, QC]), sb("wk", [P, QC]), sb("wv", [P, P]), sb("woff", [P, 2, POINTS])
        bq, bk, bv, boff = sb("bq", [64, 1]), sb("bk", [QC, 1]), sb("bv", [P, P]), sb("boff", [P, 2])
        xy = sb("xy", [P, 2, ROWPAIRS * CELLS])
        ring = ctx.enter_context(nc.psum_tensor(f"ta{b}_ring", [P, 4, 512], F32))
        ready = ctx.enter_context(nc.semaphore(f"ta{b}_constants"))
        zeroed = ctx.enter_context(nc.semaphore(f"ta{b}_zeroed"))
        doubled = ctx.enter_context(nc.semaphore(f"ta{b}_doubled"))
        groups = [f"q{c}" for c in range(8)] + [f"k{c}" for c in range(8)] + [f"v{g}" for g in range(16)] + \
                 [f"off{i}" for i in range(4)]
        pe_t = Track(ctx, nc, f"ta{b}_pe", groups)
        act_t = Track(ctx, nc, f"ta{b}_act", [f"q{c}{r}" for c in range(8) for r in "ab"] + [f"k{c}" for c in range(8)])
        dve_t = Track(ctx, nc, f"ta{b}_dve", [f"v{g}" for g in range(16)] + [f"{s}{i}" for i in range(4) for s in ("off", "clamp")])
        consts = [(wq[:], w["wq"]), (wk[:], w["wk"]), (wv[:], w["wv"]), (woff[:], w["woff"]), (bq[0:QC], w["bq"]),
                  (bq[32:32 + QC], w["bq"]), (bk[:], w["bk"]), (bv[:], w["bv"]), (boff[:], w["boff"]), (xy[:], coords)]
        block = ctx.enter_context(nc.Block())

        @block.sync
        def _(sp):
            for dst, src in consts:
                sp.dma_start(dst, src).then_inc(ready, 16)
            sp.wait_ge(act_t.sem, act_t.upto(0, "k7"))
            sp.dma_start(k_table[32:32 + QC, :, SIDE:], k_table[0:QC, :, 0:SIDE]).then_inc(doubled, 16)
            sp.wait_ge(dve_t.sem, dve_t.upto(0, "v15"))
            sp.dma_start(v_table[SIDE:], v_table[0:SIDE]).then_inc(doubled, 16)
            sp.wait_ge(doubled, 32)

        @block.gpsimd
        def _(pool):
            nc.gpsimd.memset(q_rows[:], 0.0).then_inc(zeroed, 1)
            nc.gpsimd.memset(k_table[:], 0.0).then_inc(zeroed, 1)

        @block.tensor
        def _(pe):
            pe_t.credit(pe)
            pe.wait_ge(ready, 16 * len(consts))
            for i, name in enumerate(groups):
                kind, n = name.rstrip("0123456789"), int(name.lstrip("qkvof"))
                dst = ring[:, i % 4]
                if i >= 4:
                    last = groups[i - 4]
                    if last[0] == "q":
                        pe.wait_ge(act_t.sem, act_t.upto(0, last + "b"))
                    elif last[0] == "k":
                        pe.wait_ge(act_t.sem, act_t.upto(0, last))
                    else:
                        pe.wait_ge(dve_t.sem, dve_t.upto(0, last))
                if kind == "q":
                    rows = qf[:, n * CHUNK:(n + 1) * CHUNK].rearrange("p (t r x) -> p t r x", r=2, x=SIDE)
                    for r in range(2):
                        mm = nc.tensor.matmul(dst[32 * r:32 * r + QC, 0:256], wq[:], rows[:, :, r], start=True, stop=True)
                elif kind == "k":
                    mm = nc.tensor.matmul(dst[0:QC], wk[:], vf[:, n * CHUNK:(n + 1) * CHUNK], start=True, stop=True)
                elif kind == "v":
                    cols = vf[:].rearrange("p (y x) -> p x y", x=SIDE)
                    for j in range(4):
                        mm = nc.tensor.matmul(dst[0:SIDE, j * P:(j + 1) * P], cols[:, 4 * n + j], wv[:], start=True, stop=True)
                else:
                    cells = qf[:].rearrange("p (t r h a) -> p t r h a", r=2, h=2, a=CELLS)
                    half = slice(n % 2 * 16, n % 2 * 16 + 16)
                    for lane in range(LANES):
                        mm = nc.tensor.matmul(dst[32 * lane:32 * lane + 32], woff[:, n // 2], cells[:, half, lane % 2, lane // 2],
                                              start=True, stop=True)
                mm.then_inc(pe_t.done(name), 1)

        @block.scalar
        def _(act):
            act_t.credit(act)
            act.wait_ge(ready, 16 * len(consts))
            act.wait_ge(zeroed, 2)
            for c in range(8):
                act.wait_ge(pe_t.sem, pe_t.upto(0, f"q{c}"))
                for r in range(2):
                    s = slice(32 * r, 32 * r + QC)
                    nc.scalar.activation(q_rows[s, c * 256:(c + 1) * 256], ring[s, c % 4, 0:256], ACT.Identity,
                                         bias=bq[s]).then_inc(act_t.done(f"q{c}{'ab'[r]}"), 1)
            for c in range(8):
                act.wait_ge(pe_t.sem, pe_t.upto(0, f"k{c}"))
                nc.scalar.activation(k_table[0:QC, :, 8 * c:8 * c + 8], ring[0:QC, c % 4].rearrange("p (y x) -> p x y", x=SIDE),
                                     ACT.Identity, bias=bk[:]).then_inc(act_t.done(f"k{c}"), 1)

        @block.vector
        def _(v):
            dve_t.credit(v)
            v.wait_ge(ready, 16 * len(consts))
            for g in range(16):
                v.wait_ge(pe_t.sem, pe_t.upto(0, f"v{g}"))
                nc.vector.tensor_tensor(v_table[0:SIDE, 4 * g:4 * g + 4], ring[0:SIDE, g % 4].rearrange("p (x c) -> p x c", c=P),
                                        bv[0:SIDE].unsqueeze(1).to_broadcast([SIDE, 4, P]), ALU.add).then_inc(dve_t.done(f"v{g}"), 1)
            for i in range(4):
                v.wait_ge(pe_t.sem, pe_t.upto(0, f"off{i}"))
                part = where[:, i // 2, i % 2 * 512:i % 2 * 512 + 512]
                nc.vector.scalar_tensor_tensor(part, ring[:, i % 4], boff[:, i // 2:i // 2 + 1], xy[:, i // 2, i % 2 * 512:i % 2 * 512 + 512],
                                               ALU.add, ALU.add).then_inc(dve_t.done(f"off{i}"), 1)
                v.wait_ge(dve_t.sem, dve_t.upto(0, f"off{i}"))
                nc.vector.tensor_scalar(part, part, 0.0, float(SIDE - 1), ALU.max, ALU.min).then_inc(dve_t.done(f"clamp{i}"), 1)


def sample_phase(nc, b, ramp, identity, q_rows, k_table, v_table, where, val):
    C, G8 = CELLS, 8
    with ExitStack() as ctx:
        def sb(name, shape):
            return ctx.enter_context(nc.sbuf_tensor(f"sa{b}_{name}", shape, F32))
        ramp_sb = sb("ramp", [P, SIDE])
        ident = sb("ident", [P, P])
        qt = sb("qt", [64, SIDE])
        scores = sb("scores", [P, SIDE, SIDE])
        hx = sb("hx", [P, C, SIDE])
        hy = sb("hy", [P, C, SIDE])
        ahy = sb("ahy", [P, C, SIDE])
        hy_t = sb("hy_t", [P, C, P])
        prod = sb("prod", [P, C, SIDE])
        A = sb("A", [P, SIDE, SIDE])
        logit, logit_t, probs, attn_t, attn = (sb(n, [P, 32]) for n in ("logit", "logit_t", "probs", "attn_t", "attn"))
        most, total = sb("most", [P, 1]), sb("total", [P, 1])
        ring = ctx.enter_context(nc.psum_tensor(f"sa{b}_ring", [P, 4, 512], F32))
        out_ps = ctx.enter_context(nc.psum_tensor(f"sa{b}_out", [P, 2, 512], F32))
        ready = ctx.enter_context(nc.semaphore(f"sa{b}_constants"))
        zeroed = ctx.enter_context(nc.semaphore(f"sa{b}_zeroed"))
        passed = ctx.enter_context(nc.semaphore(f"sa{b}_passed"))
        banks = [f"tr{g}" for g in range(8)] + [f"s{k}" for k in range(8)] + [f"l{k}" for k in range(4)] + [f"a{k}" for k in range(8)]
        pe_t = Track(ctx, nc, f"sa{b}_pe", banks[:20] + ["out"] + banks[20:])
        act_t = Track(ctx, nc, f"sa{b}_act", ["abs_y", "hat_y"] + [f"tr{g}{r}" for g in range(8) for r in "ab"] + ["qt"]
                      + [f"s{k}" for k in range(8)] + "abs_x hat_x exp o0 o1".split())
        dve_t = Track(ctx, nc, f"sa{b}_dve", [f"l{k}" for k in range(4)] + "logit logit_t most neg inv attn_t attn ahy".split()
                      + [f"a{k}" for k in range(8)])
        pool_t = Track(ctx, nc, f"sa{b}_pool", ["dist_y", "dist_x"])
        tail_pe = Track(ctx, nc, f"sa{b}_tail_pe", ["out"])
        tail_act = Track(ctx, nc, f"sa{b}_tail_act", ["o0", "o1"])
        block = ctx.enter_context(nc.Block())

        @block.sync
        def _(sp):
            sp.dma_start(ramp_sb[:], ramp).then_inc(ready, 16)
            sp.dma_start(ident[:], identity).then_inc(ready, 16)

        @block.gpsimd
        def _(pool):
            pool_t.credit(pool)
            nc.gpsimd.memset(hy_t[:], 0.0).then_inc(zeroed, 1)
            nc.gpsimd.memset(A[:], 0.0).then_inc(zeroed, 1)
            pool.wait_ge(ready, 32)
            grid = ramp_sb[:].unsqueeze(1).to_broadcast([P, C, SIDE])
            with pool.Fori(0, ROWPAIRS) as t:
                place = where[:, :, bass.ds(t * C, C)]
                pool.wait_ge(dve_t.sem, dve_t.last_turn(t, "ahy"))
                nc.gpsimd.tensor_tensor(hy[:], grid, place[:, 1].unsqueeze(2).to_broadcast([P, C, SIDE]),
                                        ALU.subtract).then_inc(pool_t.done("dist_y"), 1)
                pool.wait_ge(pe_t.sem, pe_t.last_turn(t, "a7"))
                nc.gpsimd.tensor_tensor(hx[:], grid, place[:, 0].unsqueeze(2).to_broadcast([P, C, SIDE]),
                                        ALU.subtract).then_inc(pool_t.done("dist_x"), 1)

        @block.tensor
        def _(pe):
            pe_t.credit(pe)
            pe.wait_ge(ready, 32)
            pe.wait_ge(zeroed, 2)

            def reader(t, name, last_turn):
                tr, step = (act_t, name + "b") if name[0] == "t" else (act_t, name) if name[0] == "s" else (dve_t, name)
                pe.wait_ge(tr.sem, tr.last_turn(t, step) if last_turn else tr.upto(t, step))

            def weighted_values(tr):
                for x in range(SIDE):
                    for c in range(2):
                        s = slice(64 * c, 64 * c + 64)
                        mm = nc.tensor.matmul(out_ps[:, c, 0:64], v_table[s, x], A[s, x], start=(x == 0), stop=(x == SIDE - 1))
                mm.then_inc(tr.done("out"), 1)

            with pe.Fori(0, ROWPAIRS) as t:
                pe.wait_ge(act_t.sem, act_t.upto(t, "hat_y"))
                for i, name in enumerate(banks):
                    bank = ring[:, i % 4]
                    n = int(name.lstrip("trsla"))
                    if name == "s0":
                        pe.wait_ge(act_t.sem, act_t.upto(t, "qt"))
                    if name == "l0":
                        pe.wait_ge(act_t.sem, act_t.upto(t, "s7"))
                    if name == "a0":
                        pe.wait_ge(dve_t.sem, dve_t.last_turn(t, "a7"))
                        pe.wait_ge(act_t.sem, act_t.last_turn(t, "o1"))
                        weighted_values(pe_t)
                        pe.wait_ge(dve_t.sem, dve_t.upto(t, "ahy"))
                    reader(t, banks[i - 4], i < 4)
                    if name[0] == "t":
                        pe.sem_inc(passed, 1)
                        for j in range(4):
                            mm = nc.tensor.transpose(bank[0:64, j * P:(j + 1) * P], hy[:, 4 * n + j], ident[:])
                    elif name[0] == "s":
                        for j in range(G8):
                            mm = nc.tensor.matmul(bank[:, j * 64:(j + 1) * 64], k_table[:, n * G8 + j], qt[:], start=True, stop=True)
                    elif name[0] == "l":
                        for j in range(G8):
                            for h in range(2):
                                a = n * G8 + j
                                mm = nc.tensor.matmul(bank[64 * h:64 * h + 64, j * 64:(j + 1) * 64], hy_t[:, a, 64 * h:64 * h + 64],
                                                      scores[:, h * C + a], start=True, stop=True)
                    else:
                        lane = slice(32 * (n // 2), 32 * (n // 2) + 32)
                        for j in range(G8):
                            for c in range(2):
                                a = n % 2 * 16 + 2 * j + c
                                mm = nc.tensor.matmul(bank[64 * c:64 * c + 64, j * 64:(j + 1) * 64], ahy[lane, a], hx[lane, a],
                                                      start=True, stop=True)
                    mm.then_inc(pe_t.done(name), 1)
            tail_pe.credit(pe)
            pe.wait_ge(dve_t.sem, dve_t.last_turn(ROWPAIRS, "a7"))
            pe.wait_ge(act_t.sem, act_t.last_turn(ROWPAIRS, "o1"))
            weighted_values(tail_pe)

        @block.scalar
        def _(act):
            act_t.credit(act)
            act.wait_ge(zeroed, 2)

            def keep_values(slot, tr):
                for c in range(2):
                    dst = slot.rearrange("p (r h a c) -> p c h r a", r=2, h=2, c=2)[:, c]
                    nc.scalar.copy(dst, out_ps[:, c, 0:64].rearrange("p (h r a) -> p h r a", h=2, r=2)).then_inc(tr.done(f"o{c}"), 1)

            with act.Fori(0, ROWPAIRS) as t:
                act.wait_ge(pool_t.sem, pool_t.upto(t, "dist_y"))
                nc.scalar.activation(hy[:], hy[:], ACT.Abs).then_inc(act_t.done("abs_y"), 1)
                act.wait_ge(act_t.sem, act_t.so_far(t))
                nc.scalar.activation(hy[:], hy[:], ACT.Relu, bias=1.0, scale=-1.0).then_inc(act_t.done("hat_y"), 1)
                act.wait_ge(pe_t.sem, pe_t.last_turn(t, "l3"))
                for g in range(8):
                    act.wait_ge(pe_t.sem, pe_t.upto(t, f"tr{g}"))
                    src = ring[0:64, g % 4].rearrange("q (i r p) -> q i r p", r=2, p=POINTS)
                    for r in range(2):
                        dst = hy_t[64 * r:64 * r + 64, 4 * g:4 * g + 4].rearrange("q a (h r p) -> q (a h) r p", h=2, r=2)
                        nc.scalar.copy(dst[:, :, r], src[:, :, r]).then_inc(act_t.done(f"tr{g}{'ab'[r]}"), 1)
                nc.scalar.copy(qt[:], q_rows[:, bass.ds(t * SIDE, SIDE)]).then_inc(act_t.done("qt"), 1)
                for k in range(8):
                    act.wait_ge(pe_t.sem, pe_t.upto(t, f"s{k}"))
                    nc.scalar.copy(scores[:, :, k * G8:(k + 1) * G8].rearrange("q n x -> q x n"),
                                   ring[:, (8 + k) % 4].rearrange("q (x n) -> q x n", n=SIDE)).then_inc(act_t.done(f"s{k}"), 1)
                act.wait_ge(pool_t.sem, pool_t.upto(t, "dist_x"))
                nc.scalar.activation(hx[:], hx[:], ACT.Abs).then_inc(act_t.done("abs_x"), 1)
                act.wait_ge(act_t.sem, act_t.so_far(t))
                nc.scalar.activation(hx[:], hx[:], ACT.Relu, bias=1.0, scale=-1.0).then_inc(act_t.done("hat_x"), 1)
                act.wait_ge(dve_t.sem, dve_t.upto(t, "neg"))
                nc.scalar.activation(probs[:], logit_t[:], ACT.Exp, bias=most[:], scale=0.25, accum_out=total[:]).then_inc(act_t.done("exp"), 1)
                act.wait_ge(pe_t.sem, pe_t.upto(t, "out"))
                keep_values(val[:, bass.ds(t * P, P)], act_t)
            tail_act.credit(act)
            act.wait_ge(tail_pe.sem, tail_pe.upto(0, "out"))
            keep_values(val[:, ROWPAIRS * P:], tail_act)

        @block.vector
        def _(v):
            dve_t.credit(v)
            with v.Fori(0, ROWPAIRS) as t:
                def own():
                    v.wait_ge(dve_t.sem, dve_t.so_far(t))
                v.wait_ge(act_t.sem, act_t.upto(t, "hat_x"))
                own()
                for k in range(4):
                    v.wait_ge(pe_t.sem, pe_t.upto(t, f"l{k}"))
                    s = slice(k * G8, (k + 1) * G8)
                    nc.vector.tensor_tensor(prod[:, s], hx[:, s], ring[:, k % 4].rearrange("p (a x) -> p a x", x=SIDE),
                                            ALU.mult).then_inc(dve_t.done(f"l{k}"), 1)
                own()
                nc.vector.tensor_reduce(logit[:], prod[:], AX.X, ALU.add).then_inc(dve_t.done("logit"), 1)
                own()
                nc.vector.transpose(logit_t[:], logit[:]).then_inc(dve_t.done("logit_t"), 1)
                own()
                nc.vector.tensor_reduce(most[:], logit_t[:], AX.X, ALU.max).then_inc(dve_t.done("most"), 1)
                own()
                nc.vector.tensor_scalar(most[:], most[:], -0.25, None, ALU.mult).then_inc(dve_t.done("neg"), 1)
                v.wait_ge(act_t.sem, act_t.upto(t, "exp"))
                nc.vector.reciprocal(total[:], total[:]).then_inc(dve_t.done("inv"), 1)
                own()
                nc.vector.tensor_scalar(attn_t[:], probs[:], total[:], None, ALU.mult).then_inc(dve_t.done("attn_t"), 1)
                own()
                nc.vector.transpose(attn[:], attn_t[:]).then_inc(dve_t.done("attn"), 1)
                own()
                v.wait_ge(pe_t.sem, pe_t.last_turn(t, "a7"))
                nc.vector.tensor_tensor(ahy[:], hy[:], attn[:].unsqueeze(2).to_broadcast([P, C, SIDE]), ALU.mult).then_inc(dve_t.done("ahy"), 1)
                for k in range(8):
                    v.wait_ge(pe_t.sem, pe_t.upto(t, f"a{k}"))
                    nc.vector.tensor_copy(A[:, :, k * G8:(k + 1) * G8].rearrange("q x n -> q n x"),
                                          ring[:, k % 4].rearrange("q (n x) -> q n x", x=SIDE)).then_inc(dve_t.done(f"a{k}"), 1)


def merge_phase(nc, b, x_dram, base_dram, out_dram, wbv, bn, val):
    H = HALVES
    with ExitStack() as ctx:
        def sb(name, shape):
            return ctx.enter_context(nc.sbuf_tensor(f"me{b}_{name}", shape, F32))
        w_sb = sb("w", [P, 256])
        x_sb, base, tmp, res = (sb(n, [P, H, CHUNK]) for n in ("x", "base", "tmp", "res"))
        ps = ctx.enter_context(nc.psum_tensor(f"me{b}_ps", [P, H, 512], F32))
        ready = ctx.enter_context(nc.semaphore(f"me{b}_constants"))
        x_loads = Loads(ctx, nc, f"me{b}_x_loaded")
        base_loads = Loads(ctx, nc, f"me{b}_base_loaded")
        stores = Loads(ctx, nc, f"me{b}_stored")
        pe_t = Track(ctx, nc, f"me{b}_pe", ["conv"])
        act_t = Track(ctx, nc, f"me{b}_act", ["relu0", "relu1"])
        dve_t = Track(ctx, nc, f"me{b}_dve", ["sum", "res"])
        stored_t = Track(ctx, nc, f"me{b}_res_stored", ["stored"])
        block = ctx.enter_context(nc.Block())

        @block.sync
        def _(sp):
            sp.dma_start(w_sb[:], wbv).then_inc(ready, 16)
            with sp.Fori(0, CHUNKS) as t:
                sp.wait_ge(dve_t.sem, dve_t.last_turn(t, "sum"))
                sp.dma_start(base[:], chunk_of(base_dram, t + b * CHUNKS)).then_inc(base_loads.sem, 16)
                sp.wait_ge(dve_t.sem, dve_t.last_turn(t, "res"))
                sp.dma_start(x_sb[:], chunk_of(x_dram, t + b * CHUNKS)).then_inc(x_loads.sem, 16)

        @block.gpsimd
        def _(pool):
            stored_t.credit(pool)
            with pool.Fori(0, CHUNKS) as t:
                pool.wait_ge(dve_t.sem, dve_t.upto(t, "res"))
                pool.dma_start(chunk_of(out_dram, t + b * CHUNKS), res[:]).then_inc(stores.sem, 16)
                pool.wait_ge(stores.sem, stores.upto(t))
                pool.sem_inc(stored_t.done("stored"), 1)

        @block.tensor
        def _(pe):
            pe_t.credit(pe)
            pe.wait_ge(ready, 16)
            with pe.Fori(0, CHUNKS) as t:
                pe.wait_ge(dve_t.sem, dve_t.last_turn(t, "sum"))
                for h in range(H):
                    mm = nc.tensor.matmul(ps[:, h], w_sb[:, h * P:(h + 1) * P], val[:, bass.ds(t * CHUNK + P, CHUNK)], start=True, stop=True)
                mm.then_inc(pe_t.done("conv"), 1)

        @block.scalar
        def _(act):
            act_t.credit(act)
            with act.Fori(0, CHUNKS) as t:
                act.wait_ge(dve_t.sem, dve_t.upto(t, "sum"))
                for h in range(H):
                    nc.scalar.activation(tmp[:, h], tmp[:, h], ACT.Relu, bias=bn[:, h, 1:2], scale=bn[:, h, 0:1]).then_inc(act_t.done(f"relu{h}"), 1)

        @block.vector
        def _(v):
            dve_t.credit(v)
            with v.Fori(0, CHUNKS) as t:
                v.wait_ge(pe_t.sem, pe_t.upto(t, "conv"))
                v.wait_ge(base_loads.sem, base_loads.upto(t))
                v.wait_ge(dve_t.sem, dve_t.so_far(t))
                nc.vector.tensor_tensor(tmp[:], base[:], ps[:], ALU.add).then_inc(dve_t.done("sum"), 1)
                v.wait_ge(act_t.sem, act_t.upto(t, "relu1"))
                v.wait_ge(x_loads.sem, x_loads.upto(t))
                v.wait_ge(stored_t.sem, stored_t.last_turn(t, "stored"))
                nc.vector.tensor_tensor(res[:], tmp[:], x_sb[:], ALU.add).then_inc(dve_t.done("res"), 1)


def conv_layer(nc, x_dram, base_dram, out_dram, w):
    with ExitStack() as ctx:
        def sb(name, shape):
            return ctx.enter_context(nc.sbuf_tensor("cl_" + name, shape, F32))
        gn = sb("gn", [P, BATCH * HALVES, 2])
        bn = sb("bn", [P, HALVES, 2])
        norm_phase(nc, x_dram, w["gmean"], w["gamma"], w["beta"], w["rmean"], w["rvar"], gn, bn)
        q_rows = sb("q_rows", [64, ROWPAIRS * SIDE])
        k_table = sb("k_table", [64, SIDE, P])
        v_table = sb("v_table", [P, SIDE, P])
        where = sb("where", [P, 2, ROWPAIRS * CELLS])
        for b in range(BATCH):
            with ExitStack() as inner:
                qf = inner.enter_context(nc.sbuf_tensor(f"qf{b}", [P, TOKENS], F32))
                vf = inner.enter_context(nc.sbuf_tensor(f"vf{b}", [P, TOKENS], F32))
                with nc.sbuf_tensor(f"resized{b}", [P, HALVES, TOKENS], F32) as up:
                    upsample_phase(nc, b, w["high"], up)
                    features_phase(nc, b, x_dram, base_dram, w, gn, up, qf, vf)
                tables_phase(nc, b, w, w["coords"], qf, vf, q_rows, k_table, v_table, where)
            with nc.sbuf_tensor(f"values{b}", [P, (ROWPAIRS + 1) * P], F32) as val:
                sample_phase(nc, b, w["ramp"], w["id"], q_rows, k_table, v_table, where, val)
                merge_phase(nc, b, x_dram, base_dram, out_dram, w["wbv"], bn, val)


GROUP = 16
GROUPS = CHUNK // GROUP
TINY = 1e-12
GATE_EPS = 1e-5


def attn_phase(nc, x_dram, out_dram, wq, wk, wv, wo, qb, kb, vb, ob, gate_weight, gate_bias, kv_scale, qk_scale,
               ones_mean, identity, head_rows, head_cols, group_mask, keep, restart):
    H = HALVES
    turns = BATCH * CHUNKS
    blocks = CHUNK // P
    with ExitStack() as ctx:
        def sb(name, shape):
            return ctx.enter_context(nc.sbuf_tensor("at_" + name, shape, F32))

        def psum(name, shape):
            return ctx.enter_context(nc.psum_tensor("at_" + name, shape, F32))

        w_sb = {n: sb("w" + n, [P, H, 256]) for n in "qkvo"}
        bias = {n: sb("b" + n, [P, H]) for n in "qkvo"}
        ones_sb = sb("ones", [P, P])
        ident = sb("ident", [P, P])
        to_rows = sb("to_rows", [P, H, HEADS])
        to_cols = sb("to_cols", [HEADS, H, P])
        mask = sb("mask", [P, 2])
        keep_sb = sb("keep", [P, turns])
        restart_sb = sb("restart", [P, turns])
        s_blk = sb("s_blk", [P, H, P])
        wg_blk = sb("wg_blk", [P, H, P])
        qks = sb("qks", [HEADS, 1])
        wgb = sb("wgb", [HEADS, 1])
        x_sb = sb("x", [P, H, CHUNK])
        cent = sb("cent", [P, H, CHUNK])
        sq = sb("sq", [P, H, CHUNK])
        std = sb("std", [P, CHUNK])
        xn = sb("xn", [P, H, CHUNK])
        Q = sb("q", [P, H, CHUNK])
        K = sb("k", [P, H, CHUNK])
        V = sb("v", [P, H, CHUNK])
        qk = sb("qk", [P, H, CHUNK])
        ksq = sb("ksq", [P, H, CHUNK])
        vsq = sb("vsq", [P, H, CHUNK])
        GK = sb("gk", [P, H, CHUNK])
        gp = sb("gp", [P, H, CHUNK])
        VT = sb("vt", [P, H, blocks, P])
        GT = sb("gt", [P, 2, H, blocks, P])
        pair = sb("pair", [P, 2, GROUPS, GROUP])
        weighed = sb("weighed", [P, 2, GROUPS, GROUP])
        acc = sb("acc", [P, H, GROUPS, GROUP])
        sz = sb("sz", [P, 2, H, P])
        state_sb = sb("state_sb", [P, H * P])
        keep_id = sb("keep_id", [P, P])
        ctxt = sb("ctxt", [P, H, CHUNK])
        proj = sb("proj", [P, H, CHUNK])
        res = sb("res", [P, H, CHUNK])
        sim = sb("sim", [HEADS, CHUNK])
        norms = sb("norms", [HEADS, 2, CHUNK])
        gate = sb("gate", [HEADS, CHUNK])
        most = sb("most", [HEADS, CHUNK + 1])
        expo = sb("expo", [HEADS, 2, CHUNK])
        s_run = sb("s_run", [HEADS, CHUNK])
        g_run = sb("g_run", [HEADS, CHUNK])
        s_car = sb("s_car", [HEADS, 1])
        g_car = sb("g_car", [HEADS, 1])
        ones_row = sb("ones_row", [HEADS, CHUNK])
        wrow = sb("wrow", [HEADS, CHUNK])
        erow = sb("erow", [HEADS, CHUNK])
        crow = sb("crow", [HEADS, CHUNK])
        bank = psum("bank", [P, 3, 512])
        state = psum("state", [P, 512])
        inter = psum("inter", [P, H, 512])
        paired = psum("paired", [P, 2, 512])

        G = GROUPS
        pe_t = Track(ctx, nc, "at_pe",
                     "mean var q0 q1 k0 k1 v0 v1 sim kk vv ks0 ks1 vs0 vs1 wg0 wg1 glog gs0 gs1 seed tv0 tv1 tg0 tg1".split()
                     + [f"{s}{i}" for i in range(G) for s in ("pair", "apply", "grow")] + "c0 c1 o0 o1".split())
        act_t = Track(ctx, nc, "at_act",
                      "square sqrt q0 q1 k0 k1 v0 v1 ksq vsq knorm vnorm grelu gsq vt0 vt1 gt00 gt01 gt10 gt11 exp silu o0 o1".split())
        dve_t = Track(ctx, nc, "at_dve",
                      ("center var_eps rstd norm keep_id sim floor inv kh0 kh1 vh0 vh1 gp0 gp1 gate gk0 gk1 "
                       "most0 s_car g_car most fall rise s_run g_run s_eps s_inv w e1 e_inv sw g_eps g_inv c").split()
                      + [f"{s}{i}" for i in range(G) for s in ("sz", "weigh", "add") if s != "add" or i % GROUP] + "keep_state inter ctxt0 ctxt1 res".split())
        pool_t = Track(ctx, nc, "at_pool", ["qk"] + [f"pair{i}" for i in range(G)])
        stored_t = Track(ctx, nc, "at_res_stored", ["stored"])
        ready = ctx.enter_context(nc.semaphore("at_constants"))
        zeroed = ctx.enter_context(nc.semaphore("at_zeroed"))
        scaled = ctx.enter_context(nc.semaphore("at_gate_weight"))
        loads = Loads(ctx, nc, "at_x_loaded")
        stores = Loads(ctx, nc, "at_stored")
        consts = [(w_sb["q"], wq), (w_sb["k"], wk), (w_sb["v"], wv), (w_sb["o"], wo), (bias["q"], qb), (bias["k"], kb),
                  (bias["v"], vb), (bias["o"], ob), (ones_sb, ones_mean), (ident, identity), (to_rows, head_rows),
                  (to_cols, head_cols), (mask, group_mask), (keep_sb, keep), (restart_sb, restart), (qks, qk_scale),
                  (wgb, gate_bias)]
        n_consts = len(consts) + 2 * HEADS
        block = ctx.enter_context(nc.Block())

        @block.sync
        def _(sp):
            sp.wait_ge(zeroed, 6)
            for dst, src in consts:
                sp.dma_start(dst[:], src).then_inc(ready, 16)
            for h in range(HEADS):
                r = slice(32 * (h % 4), 32 * (h % 4) + 32)
                sp.dma_start(s_blk[r, h // 4, r], kv_scale[h]).then_inc(ready, 16)
                sp.dma_start(wg_blk[r, h // 4, r], gate_weight).then_inc(ready, 16)
            with sp.Fori(0, turns) as t:
                sp.wait_ge(dve_t.sem, dve_t.last_turn(t, "res"))
                sp.dma_start(x_sb[:], chunk_of(x_dram, t)).then_inc(loads.sem, 16)

        @block.gpsimd
        def _(pool):
            stored_t.credit(pool)
            pool_t.credit(pool)
            with pool.Fori(0, turns) as t:
                pool.wait_ge(act_t.sem, act_t.upto(t, "k1"))
                pool.wait_ge(pool_t.sem, pool_t.so_far(t))
                nc.gpsimd.tensor_tensor(qk[:], Q[:], K[:], ALU.mult).then_inc(pool_t.done("qk"), 1)
                pool.wait_ge(dve_t.sem, dve_t.upto(t, "vh1"))
                for i in range(G):
                    h, far = i // GROUP, i % GROUP
                    if i >= 2:
                        pool.wait_ge(pe_t.sem, pe_t.upto(t, f"pair{i - 2}"))
                    q_part = Q[:, h].rearrange("p (g n) -> p g n", n=GROUP)[:, :, far:]
                    v_part = V[:, h].rearrange("p (g n) -> p g n", n=GROUP)[:, :, 0:GROUP - far]
                    nc.gpsimd.tensor_tensor(pair[:, i % 2, :, 0:GROUP - far], q_part, v_part, ALU.mult).then_inc(pool_t.done(f"pair{i}"), 1)
                pool.wait_ge(dve_t.sem, dve_t.upto(t, "res"))
                pool.dma_start(chunk_of(out_dram, t), res[:]).then_inc(stores.sem, 16)
                pool.wait_ge(stores.sem, stores.upto(t))
                pool.sem_inc(stored_t.done("stored"), 1)

        @block.tensor
        def _(pe):
            pe_t.credit(pe)
            pe.wait_ge(ready, 16 * n_consts)
            pe.wait_ge(scaled, 1)

            def both(dst, lhs, rhs, step):
                for k in range(H):
                    mm = nc.tensor.matmul(dst, lhs[k], rhs[k], start=(k == 0), stop=(k == H - 1))
                mm.then_inc(pe_t.done(step), 1)

            with pe.Fori(0, turns) as t:
                pe.wait_ge(loads.sem, loads.upto(t))
                ones2 = [ones_sb[:]] * 2
                both(bank[:, 0], ones2, [x_sb[:, 0], x_sb[:, 1]], "mean")
                pe.wait_ge(act_t.sem, act_t.upto(t, "square"))
                both(bank[:, 1], ones2, [sq[:, 0], sq[:, 1]], "var")
                pe.wait_ge(dve_t.sem, dve_t.upto(t, "norm"))
                for i, (n, h) in enumerate((n, h) for n in "qkv" for h in range(H)):
                    if i >= 3:
                        pe.wait_ge(act_t.sem, act_t.upto(t, ("q0", "q1", "k0")[i - 3]))
                    both(bank[:, i % 3], [w_sb[n][:, k, h * P:(h + 1) * P] for k in range(H)], [xn[:, 0], xn[:, 1]], f"{n}{h}")
                rows = [to_rows[:, 0], to_rows[:, 1]]
                pe.wait_ge(act_t.sem, act_t.upto(t, "vsq"))
                pe.wait_ge(pool_t.sem, pool_t.upto(t, "qk"))
                both(bank[0:HEADS, 0], rows, [qk[:, 0], qk[:, 1]], "sim")
                both(bank[0:HEADS, 1], rows, [ksq[:, 0], ksq[:, 1]], "kk")
                both(bank[0:HEADS, 2], rows, [vsq[:, 0], vsq[:, 1]], "vv")
                pe.wait_ge(dve_t.sem, dve_t.upto(t, "inv"))
                nc.tensor.matmul(bank[:, 0], to_cols[:, 0], norms[:, 0], start=True, stop=True).then_inc(pe_t.done("ks0"), 1)
                nc.tensor.matmul(bank[:, 1], to_cols[:, 1], norms[:, 0], start=True, stop=True).then_inc(pe_t.done("ks1"), 1)
                nc.tensor.matmul(bank[:, 2], to_cols[:, 0], norms[:, 1], start=True, stop=True).then_inc(pe_t.done("vs0"), 1)
                pe.wait_ge(dve_t.sem, dve_t.upto(t, "kh0"))
                nc.tensor.matmul(bank[:, 0], to_cols[:, 1], norms[:, 1], start=True, stop=True).then_inc(pe_t.done("vs1"), 1)
                pe.wait_ge(dve_t.sem, dve_t.upto(t, "vh1"))
                nc.tensor.matmul(bank[:, 1], wg_blk[:, 0], V[:, 0], start=True, stop=True).then_inc(pe_t.done("wg0"), 1)
                nc.tensor.matmul(bank[:, 2], wg_blk[:, 1], V[:, 1], start=True, stop=True).then_inc(pe_t.done("wg1"), 1)
                pe.wait_ge(dve_t.sem, dve_t.upto(t, "gp1"))
                both(bank[0:HEADS, 0], rows, [gp[:, 0], gp[:, 1]], "glog")
                pe.wait_ge(dve_t.sem, dve_t.upto(t, "gate"))
                nc.tensor.matmul(bank[:, 1], to_cols[:, 0], gate[:], start=True, stop=True).then_inc(pe_t.done("gs0"), 1)
                nc.tensor.matmul(bank[:, 2], to_cols[:, 1], gate[:], start=True, stop=True).then_inc(pe_t.done("gs1"), 1)
                nc.tensor.matmul(state[:, 0:H * P], keep_id[:], state_sb[:], start=True, stop=False,
                                 skip_group_check=True).then_inc(pe_t.done("seed"), 1)
                for h in range(H):
                    if h == 1:
                        pe.wait_ge(dve_t.sem, dve_t.upto(t, "gk0"))
                    for b in range(blocks):
                        mm = nc.tensor.transpose(bank[:, h, b * P:(b + 1) * P], V[:, h, b * P:(b + 1) * P], ident[:])
                    mm.then_inc(pe_t.done(f"tv{h}"), 1)
                for h in range(H):
                    if h == 0:
                        pe.wait_ge(dve_t.sem, dve_t.upto(t, "gk1"))
                    else:
                        pe.wait_ge(act_t.sem, act_t.upto(t, "vt0"))
                    for b in range(blocks):
                        mm = nc.tensor.transpose(bank[:, 2 if h == 0 else 0, b * P:(b + 1) * P], GK[:, h, b * P:(b + 1) * P], ident[:])
                    mm.then_inc(pe_t.done(f"tg{h}"), 1)
                pe.wait_ge(act_t.sem, act_t.upto(t, "gt11"))
                for i in range(G):
                    h, far = i // GROUP, i % GROUP
                    b, r, m = i // 8, slice(32 * (i % 8 // 2), 32 * (i % 8 // 2) + 32), i % 2
                    pe.wait_ge(pool_t.sem, pool_t.upto(t, f"pair{i}"))
                    if i >= 2:
                        pe.wait_ge(dve_t.sem, dve_t.upto(t, f"weigh{i - 2}"))
                    nc.tensor.matmul(paired[:, i % 2, 0:G * (GROUP - far)], s_blk[:, h], pair[:, i % 2, :, 0:GROUP - far],
                                     start=True, stop=True).then_inc(pe_t.done(f"pair{i}"), 1)
                    pe.wait_ge(dve_t.sem, dve_t.upto(t, f"sz{i}"))
                    for k in range(H):
                        mm = nc.tensor.matmul(inter[:, k, i * GROUP:(i + 1) * GROUP], sz[:, i % 2, k],
                                              Q[:, k, i * GROUP:(i + 1) * GROUP], start=True, stop=True)
                    mm.then_inc(pe_t.done(f"apply{i}"), 1)
                    for k in range(H):
                        mm = nc.tensor.matmul(state[:, k * P:(k + 1) * P], VT[r, k, b, :], GT[r, m, k, b, :],
                                              start=False, stop=False, skip_group_check=True)
                    mm.then_inc(pe_t.done(f"grow{i}"), 1)
                nc.tensor.matmul(bank[:, 0], to_cols[:, 0], crow[:], start=True, stop=True).then_inc(pe_t.done("c0"), 1)
                nc.tensor.matmul(bank[:, 1], to_cols[:, 1], crow[:], start=True, stop=True).then_inc(pe_t.done("c1"), 1)
                pe.wait_ge(dve_t.sem, dve_t.upto(t, "ctxt1"))
                for h in range(H):
                    both(bank[:, 2 if h == 0 else 0], [w_sb["o"][:, k, h * P:(h + 1) * P] for k in range(H)], [ctxt[:, 0], ctxt[:, 1]], f"o{h}")

        @block.scalar
        def _(act):
            act_t.credit(act)
            act.wait_ge(ready, 16 * n_consts)
            with act.Fori(0, turns) as t:
                def own():
                    act.wait_ge(act_t.sem, act_t.so_far(t))
                act.wait_ge(dve_t.sem, dve_t.upto(t, "center"))
                nc.scalar.activation(sq[:], cent[:], ACT.Square).then_inc(act_t.done("square"), 1)
                act.wait_ge(dve_t.sem, dve_t.upto(t, "var_eps"))
                nc.scalar.activation(std[:], std[:], ACT.Sqrt).then_inc(act_t.done("sqrt"), 1)
                for i, (n, dst, h) in enumerate((n, dst, h) for n, dst in (("q", Q), ("k", K), ("v", V)) for h in range(H)):
                    act.wait_ge(pe_t.sem, pe_t.upto(t, f"{n}{h}"))
                    nc.scalar.activation(dst[:, h], bank[:, i % 3], ACT.Identity, bias=bias[n][:, h:h + 1]).then_inc(act_t.done(f"{n}{h}"), 1)
                own()
                nc.scalar.activation(ksq[:], K[:], ACT.Square).then_inc(act_t.done("ksq"), 1)
                nc.scalar.activation(vsq[:], V[:], ACT.Square).then_inc(act_t.done("vsq"), 1)
                act.wait_ge(pe_t.sem, pe_t.upto(t, "vv"))
                nc.scalar.activation(norms[:, 0], bank[0:HEADS, 1], ACT.Sqrt).then_inc(act_t.done("knorm"), 1)
                nc.scalar.activation(norms[:, 1], bank[0:HEADS, 2], ACT.Sqrt).then_inc(act_t.done("vnorm"), 1)
                act.wait_ge(pe_t.sem, pe_t.upto(t, "glog"))
                nc.scalar.activation(gate[:], bank[0:HEADS, 0], ACT.Relu, bias=wgb[:]).then_inc(act_t.done("grelu"), 1)
                own()
                nc.scalar.activation(gate[:], gate[:], ACT.Square).then_inc(act_t.done("gsq"), 1)
                for h in range(H):
                    act.wait_ge(pe_t.sem, pe_t.upto(t, f"tv{h}"))
                    nc.scalar.copy(VT[:, h], bank[:, h].rearrange("p (b c) -> p b c", c=P)).then_inc(act_t.done(f"vt{h}"), 1)
                for h in range(H):
                    act.wait_ge(pe_t.sem, pe_t.upto(t, f"tg{h}"))
                    for m in range(2):
                        nc.scalar.activation(GT[:, m, h], bank[:, 2 if h == 0 else 0].rearrange("p (b c) -> p b c", c=P), ACT.Copy,
                                             scale=mask[:, m:m + 1]).then_inc(act_t.done(f"gt{h}{m}"), 1)
                act.wait_ge(dve_t.sem, dve_t.upto(t, "rise"))
                nc.scalar.activation(expo[:], expo[:], ACT.Exp).then_inc(act_t.done("exp"), 1)
                act.wait_ge(dve_t.sem, dve_t.upto(t, "w"))
                nc.scalar.activation(erow[:], wrow[:], ACT.Exp, scale=-1.0).then_inc(act_t.done("silu"), 1)
                for h in range(H):
                    act.wait_ge(pe_t.sem, pe_t.upto(t, f"o{h}"))
                    nc.scalar.activation(proj[:, h], bank[:, 2 if h == 0 else 0], ACT.Identity, bias=bias["o"][:, h:h + 1]).then_inc(act_t.done(f"o{h}"), 1)

        @block.vector
        def _(v):
            dve_t.credit(v)
            for z in (s_blk, wg_blk, state_sb, most, s_run, g_run):
                nc.vector.memset(z[:], 0.0).then_inc(zeroed, 1)
            nc.vector.memset(ones_row[:], 1.0).then_inc(zeroed, 1)
            v.wait_ge(ready, 16 * n_consts)
            nc.vector.tensor_tensor(wg_blk[:], wg_blk[:], s_blk[:], ALU.mult).then_inc(scaled, 1)
            v.wait_ge(scaled, 1)
            v.wait_ge(zeroed, 7)
            with v.Fori(0, turns) as t:
                def step(name, ins):
                    ins.then_inc(dve_t.done(name), 1)

                def own():
                    v.wait_ge(dve_t.sem, dve_t.so_far(t))

                v.wait_ge(pe_t.sem, pe_t.upto(t, "mean"))
                own()
                nc.vector.tensor_tensor(cent[:], x_sb[:], bank[:, 0].unsqueeze(1).to_broadcast([P, H, CHUNK]),
                                        ALU.subtract).then_inc(dve_t.done("center"), 1)
                v.wait_ge(pe_t.sem, pe_t.upto(t, "var"))
                own()
                nc.vector.tensor_scalar_add(std[:], bank[:, 1], LN_EPS).then_inc(dve_t.done("var_eps"), 1)
                v.wait_ge(act_t.sem, act_t.upto(t, "sqrt"))
                own()
                nc.vector.reciprocal(std[:], std[:]).then_inc(dve_t.done("rstd"), 1)
                own()
                nc.vector.tensor_tensor(xn[:], cent[:], std[:].unsqueeze(1).to_broadcast([P, H, CHUNK]),
                                        ALU.mult).then_inc(dve_t.done("norm"), 1)
                nc.vector.tensor_scalar(keep_id[:], ident[:], keep_sb[:, bass.ds(t, 1)], None, ALU.mult).then_inc(dve_t.done("keep_id"), 1)
                v.wait_ge(pe_t.sem, pe_t.upto(t, "sim"))
                nc.vector.tensor_scalar(sim[:], bank[0:HEADS, 0], qks[:], None, ALU.mult).then_inc(dve_t.done("sim"), 1)
                v.wait_ge(act_t.sem, act_t.upto(t, "vnorm"))
                nc.vector.tensor_scalar_max(norms[:], norms[:], TINY).then_inc(dve_t.done("floor"), 1)
                own()
                nc.vector.reciprocal(norms[:], norms[:]).then_inc(dve_t.done("inv"), 1)
                for h in range(H):
                    v.wait_ge(pe_t.sem, pe_t.upto(t, f"ks{h}"))
                    nc.vector.tensor_tensor(K[:, h], K[:, h], bank[:, h], ALU.mult).then_inc(dve_t.done(f"kh{h}"), 1)
                for h in range(H):
                    v.wait_ge(pe_t.sem, pe_t.upto(t, f"vs{h}"))
                    nc.vector.tensor_tensor(V[:, h], V[:, h], bank[:, 2 if h == 0 else 0], ALU.mult).then_inc(dve_t.done(f"vh{h}"), 1)
                own()
                for h in range(H):
                    v.wait_ge(pe_t.sem, pe_t.upto(t, f"wg{h}"))
                    nc.vector.tensor_tensor(gp[:, h], K[:, h], bank[:, 1 + h], ALU.mult).then_inc(dve_t.done(f"gp{h}"), 1)
                v.wait_ge(act_t.sem, act_t.upto(t, "gsq"))
                nc.vector.tensor_scalar_add(gate[:], gate[:], GATE_EPS).then_inc(dve_t.done("gate"), 1)
                for h in range(H):
                    v.wait_ge(pe_t.sem, pe_t.upto(t, f"gs{h}"))
                    nc.vector.tensor_tensor(GK[:, h], K[:, h], bank[:, 1 + h], ALU.mult).then_inc(dve_t.done(f"gk{h}"), 1)
                kt, rt = keep_sb[0:HEADS, bass.ds(t, 1)], restart_sb[0:HEADS, bass.ds(t, 1)]
                nc.vector.tensor_scalar(most[:, 0:1], most[:, CHUNK:CHUNK + 1], kt, rt, ALU.mult, ALU.add).then_inc(dve_t.done("most0"), 1)
                nc.vector.tensor_scalar(s_car[:], s_run[:, CHUNK - 1:CHUNK], kt, None, ALU.mult).then_inc(dve_t.done("s_car"), 1)
                nc.vector.tensor_scalar(g_car[:], g_run[:, CHUNK - 1:CHUNK], kt, None, ALU.mult).then_inc(dve_t.done("g_car"), 1)
                own()
                nc.vector.tensor_tensor_scan(most[:, 1:], sim[:], sim[:], most[:, 0:1], ALU.max, ALU.max).then_inc(dve_t.done("most"), 1)
                own()
                nc.vector.tensor_tensor(expo[:, 0], most[:, 0:CHUNK], most[:, 1:], ALU.subtract).then_inc(dve_t.done("fall"), 1)
                nc.vector.tensor_tensor(expo[:, 1], sim[:], most[:, 1:], ALU.subtract).then_inc(dve_t.done("rise"), 1)
                v.wait_ge(act_t.sem, act_t.upto(t, "exp"))
                nc.vector.tensor_tensor_scan(s_run[:], expo[:, 0], expo[:, 1], s_car[:], ALU.mult, ALU.add).then_inc(dve_t.done("s_run"), 1)
                nc.vector.tensor_tensor_scan(g_run[:], ones_row[:], gate[:], g_car[:], ALU.mult, ALU.add).then_inc(dve_t.done("g_run"), 1)
                own()
                nc.vector.tensor_scalar_add(wrow[:], s_run[:], GATE_EPS).then_inc(dve_t.done("s_eps"), 1)
                own()
                nc.vector.reciprocal(wrow[:], wrow[:]).then_inc(dve_t.done("s_inv"), 1)
                own()
                nc.vector.tensor_tensor(wrow[:], expo[:, 1], wrow[:], ALU.mult).then_inc(dve_t.done("w"), 1)
                v.wait_ge(act_t.sem, act_t.upto(t, "silu"))
                nc.vector.tensor_scalar_add(erow[:], erow[:], 1.0).then_inc(dve_t.done("e1"), 1)
                own()
                nc.vector.reciprocal(erow[:], erow[:]).then_inc(dve_t.done("e_inv"), 1)
                own()
                nc.vector.tensor_tensor(wrow[:], wrow[:], erow[:], ALU.mult).then_inc(dve_t.done("sw"), 1)
                nc.vector.tensor_scalar_add(crow[:], g_run[:], GATE_EPS).then_inc(dve_t.done("g_eps"), 1)
                own()
                nc.vector.reciprocal(crow[:], crow[:]).then_inc(dve_t.done("g_inv"), 1)
                own()
                nc.vector.scalar_tensor_tensor(crow[:], wrow[:], 1.0, crow[:], ALU.add, ALU.mult).then_inc(dve_t.done("c"), 1)
                v.wait_ge(pe_t.sem, pe_t.upto(t, "seed"))
                for i in range(G):
                    h, far = i // GROUP, i % GROUP
                    if i:
                        v.wait_ge(pe_t.sem, pe_t.upto(t, f"grow{i - 1}"))
                    own()
                    nc.vector.tensor_tensor(sz[:, i % 2].rearrange("p h e -> p (h e)"), state[:, 0:H * P],
                                            s_blk[:].rearrange("p h e -> p (h e)"), ALU.mult).then_inc(dve_t.done(f"sz{i}"), 1)
                    v.wait_ge(pe_t.sem, pe_t.upto(t, f"pair{i}"))
                    gk_part = GK[:, h].rearrange("p (g n) -> p g n", n=GROUP)[:, :, 0:GROUP - far]
                    dst = acc[:, h] if far == 0 else weighed[:, i % 2, :, 0:GROUP - far]
                    nc.vector.tensor_tensor(dst, gk_part, paired[:, i % 2, 0:G * (GROUP - far)].rearrange("p (g n) -> p g n", g=G),
                                            ALU.mult).then_inc(dve_t.done(f"weigh{i}"), 1)
                    if far:
                        own()
                        nc.vector.tensor_tensor(acc[:, h, :, far:], acc[:, h, :, far:], dst, ALU.add).then_inc(dve_t.done(f"add{i}"), 1)
                v.wait_ge(pe_t.sem, pe_t.upto(t, f"grow{G - 1}"))
                own()
                nc.vector.tensor_copy(state_sb[:], state[:, 0:H * P]).then_inc(dve_t.done("keep_state"), 1)
                flat = acc[:].rearrange("p h g n -> p h (g n)")
                nc.vector.tensor_tensor(flat, flat, inter[:], ALU.add).then_inc(dve_t.done("inter"), 1)
                v.wait_ge(pe_t.sem, pe_t.upto(t, "c1"))
                own()
                for h in range(H):
                    nc.vector.tensor_tensor(ctxt[:, h], flat[:, h], bank[:, h], ALU.mult).then_inc(dve_t.done(f"ctxt{h}"), 1)
                v.wait_ge(act_t.sem, act_t.upto(t, "o1"))
                v.wait_ge(stored_t.sem, stored_t.last_turn(t, "stored"))
                own()
                nc.vector.tensor_tensor(res[:], proj[:], x_sb[:], ALU.add).then_inc(dve_t.done("res"), 1)
        return


def ffn_phase(nc, x_dram, out_dram, gate_w, gate_b, w1, b1, w2, b2, ones_mean, identity):
    E, M, H = EXPERTS, 4, HALVES
    blocks = CHUNK // P
    turns = BATCH * CHUNKS
    with ExitStack() as ctx:
        def sb(name, shape):
            return ctx.enter_context(nc.sbuf_tensor("ffn_" + name, shape, F32))

        def psum(name, shape):
            return ctx.enter_context(nc.psum_tensor("ffn_" + name, shape, F32))

        w1_sb = sb("w1", [P, E, H, 512])
        w2_sb = sb("w2", [P, E, M, 256])
        b1_sb = sb("b1", [P, E, M])
        b2_sb = sb("b2", [E, 256])
        gw_sb = sb("gw", [P, H, E])
        gb_sb = sb("gb", [P, E])
        ones_sb = sb("ones", [P, P])
        ident = sb("ident", [P, P])
        pick = sb("pick", [E, E, P])
        x_sb = sb("x", [P, H, CHUNK])
        cent = sb("cent", [P, H, CHUNK])
        sq = sb("sq", [P, H, CHUNK])
        std = sb("std", [P, CHUNK])
        xn = sb("xn", [P, H, CHUNK])
        logit = sb("logit", [P, blocks, E])
        top = sb("top", [P, blocks])
        total = sb("total", [P, blocks])
        probs = sb("probs", [P, blocks, 2 * E])
        sorted8 = sb("sorted8", [P, blocks, E])
        first2 = sb("first2", [P, blocks, E])
        marked = sb("marked", [P, blocks, 2 * E])
        cw = sb("cw", [P, blocks, E])
        cw_rows = sb("cw_rows", [E, CHUNK])
        act_out = sb("act_out", [P, 2, M, CHUNK])
        scaled = sb("scaled", [P, 2, M, CHUNK])
        res = sb("res", [P, H, CHUNK])
        small = psum("small", [P, 512])
        spread = psum("spread", [P, 512])
        hid = psum("hid", [P, M, 512])
        y = psum("y", [P, H, 512])

        pe_order = ["mean", "var", "router", "cw_rows", "cwb0"] + [f"h0_{m}" for m in range(M)]
        act_order = ["square", "sqrt", "exp", "cw_rows"]
        dve_order = ["center", "var_eps", "rstd", "norm", "logit", "top", "shift", "total", "inv", "prob"]
        dve_order += [f"sort{b}" for b in range(blocks)] + ["first2"] + [f"mark{b}" for b in range(blocks)]
        dve_order += ["chosen", "cw"]
        for e in range(E):
            act_order += [f"gelu{e}_{m}" for m in range(M)]
            dve_order += [f"scale{e}_{m}" for m in range(M)]
            if e + 1 < E:
                pe_order += [f"h{e + 1}_{m}" for m in range(M)]
            pe_order += [f"y{e}"]
            if e + 1 < E:
                pe_order += [f"cwb{e + 1}"]
        dve_order += ["res"]
        pe_t = Track(ctx, nc, "ffn_pe", pe_order)
        act_t = Track(ctx, nc, "ffn_act", act_order)
        dve_t = Track(ctx, nc, "ffn_dve", dve_order)
        stored_t = Track(ctx, nc, "ffn_res_stored", ["stored"])
        ready = ctx.enter_context(nc.semaphore("ffn_constants"))
        filled = ctx.enter_context(nc.semaphore("ffn_filled"))
        sentinels = ctx.enter_context(nc.semaphore("ffn_sentinels"))
        passed = ctx.enter_context(nc.semaphore("ffn_passed"))
        loads = Loads(ctx, nc, "ffn_x_loaded")
        stores = Loads(ctx, nc, "ffn_stored")
        consts = [(w1_sb, w1), (w2_sb, w2), (b1_sb, b1), (b2_sb, b2), (gw_sb, gate_w), (gb_sb, gate_b),
                  (ones_sb, ones_mean), (ident, identity)]
        block = ctx.enter_context(nc.Block())

        @block.sync
        def _(sp):
            for dst, src in consts:
                sp.dma_start(dst[:], src).then_inc(ready, 16)
            with sp.Fori(0, turns) as t:
                sp.wait_ge(dve_t.sem, dve_t.last_turn(t, "res"))
                sp.dma_start(x_sb[:], chunk_of(x_dram, t)).then_inc(loads.sem, 16)

        @block.gpsimd
        def _(pool):
            stored_t.credit(pool)
            pool.wait_ge(ready, 16 * len(consts))
            nc.gpsimd.tensor_copy(pick[:], ident[0:E, 0:E].unsqueeze(2).to_broadcast([E, E, P])).then_inc(filled, 1)
            with pool.Fori(0, turns) as t:
                pool.wait_ge(dve_t.sem, dve_t.upto(t, "res"))
                pool.dma_start(chunk_of(out_dram, t), res[:]).then_inc(stores.sem, 16)
                pool.wait_ge(stores.sem, stores.upto(t))
                pool.sem_inc(stored_t.done("stored"), 1)

        @block.tensor
        def _(pe):
            pe_t.credit(pe)
            pe.wait_ge(ready, 16 * len(consts))
            pe.wait_ge(filled, 1)

            def hidden(t, e):
                for m in range(M):
                    pe.wait_ge(act_t.sem, act_t.upto(t, f"gelu{e - 1}_{m}") if e else act_t.last_turn(t, f"gelu{E - 1}_{m}"))
                    for k in range(H):
                        mm = nc.tensor.matmul(hid[:, m], w1_sb[:, e, k, m * P:(m + 1) * P], xn[:, k],
                                              start=(k == 0), stop=(k == H - 1))
                    mm.then_inc(pe_t.done(f"h{e}_{m}"), 1)

            def spread_weight(t, e):
                pe.wait_ge(dve_t.sem, dve_t.upto(t, f"scale{e - 1}_{M - 1}") if e else dve_t.last_turn(t, f"scale{E - 1}_{M - 1}"))
                nc.tensor.matmul(spread[:], pick[:, e], cw_rows[:], start=True, stop=True).then_inc(pe_t.done(f"cwb{e}"), 1)

            with pe.Fori(0, turns) as t:
                pe.wait_ge(loads.sem, loads.upto(t))
                for k in range(H):
                    mm = nc.tensor.matmul(small[:], ones_sb[:], x_sb[:, k], start=(k == 0), stop=(k == H - 1))
                mm.then_inc(pe_t.done("mean"), 1)
                pe.wait_ge(act_t.sem, act_t.upto(t, "square"))
                for k in range(H):
                    mm = nc.tensor.matmul(small[:], ones_sb[:], sq[:, k], start=(k == 0), stop=(k == H - 1))
                mm.then_inc(pe_t.done("var"), 1)
                pe.wait_ge(dve_t.sem, dve_t.upto(t, "norm"))
                for b in range(blocks):
                    for k in range(H):
                        mm = nc.tensor.matmul(small[:, b * E:(b + 1) * E], xn[:, k, b * P:(b + 1) * P], gw_sb[:, k],
                                              start=(k == 0), stop=(k == H - 1))
                mm.then_inc(pe_t.done("router"), 1)
                pe.wait_ge(dve_t.sem, dve_t.upto(t, "cw"))
                for b in range(blocks):
                    mm = nc.tensor.transpose(small[0:E, b * P:(b + 1) * P], cw[:, b], ident[:])
                mm.then_inc(pe_t.done("cw_rows"), 1)
                pe.wait_ge(act_t.sem, act_t.upto(t, "cw_rows"))
                spread_weight(t, 0)
                hidden(t, 0)
                for e in range(E):
                    if e + 1 < E:
                        hidden(t, e + 1)
                    for m in range(M):
                        pe.wait_ge(dve_t.sem, dve_t.upto(t, f"scale{e}_{m}"))
                        for d in range(H):
                            mm = nc.tensor.matmul(y[:, d], w2_sb[:, e, m, d * P:(d + 1) * P], scaled[:, e % 2, m],
                                                  start=(e == 0 and m == 0), stop=False, skip_group_check=True)
                    if e == E - 1:
                        for d in range(H):
                            mm = nc.tensor.matmul(y[:, d], b2_sb[:, d * P:(d + 1) * P], cw_rows[:],
                                                  start=False, stop=True, skip_group_check=True)
                    mm.then_inc(pe_t.done(f"y{e}"), 1)
                    if e + 1 < E:
                        spread_weight(t, e + 1)

        @block.scalar
        def _(act):
            act_t.credit(act)
            act.wait_ge(ready, 16 * len(consts))
            with act.Fori(0, turns) as t:
                act.wait_ge(dve_t.sem, dve_t.upto(t, "center"))
                nc.scalar.activation(sq[:], cent[:], ACT.Square).then_inc(act_t.done("square"), 1)
                act.wait_ge(dve_t.sem, dve_t.upto(t, "var_eps"))
                nc.scalar.activation(std[:], std[:], ACT.Sqrt).then_inc(act_t.done("sqrt"), 1)
                act.wait_ge(dve_t.sem, dve_t.upto(t, "shift"))
                nc.scalar.activation(logit[:], logit[:], ACT.Exp).then_inc(act_t.done("exp"), 1)
                act.wait_ge(pe_t.sem, pe_t.upto(t, "cw_rows"))
                nc.scalar.copy(cw_rows[:], small[0:E]).then_inc(act_t.done("cw_rows"), 1)
                for e in range(E):
                    for m in range(M):
                        act.wait_ge(pe_t.sem, pe_t.upto(t, f"h{e}_{m}"))
                        if e >= 2:
                            act.wait_ge(dve_t.sem, dve_t.upto(t, f"scale{e - 2}_{m}"))
                        nc.scalar.activation(act_out[:, e % 2, m], hid[:, m], ACT.Gelu,
                                             bias=b1_sb[:, e, m:m + 1]).then_inc(act_t.done(f"gelu{e}_{m}"), 1)

        @block.vector
        def _(v):
            dve_t.credit(v)
            nc.vector.memset(probs[:], -1.0).then_inc(sentinels, 1)
            nc.vector.memset(first2[:], -1.0).then_inc(sentinels, 1)
            v.wait_ge(sentinels, 2)
            v.wait_ge(ready, 16 * len(consts))
            with v.Fori(0, turns) as t:
                def own():
                    v.wait_ge(dve_t.sem, dve_t.so_far(t))
                v.wait_ge(pe_t.sem, pe_t.upto(t, "mean"))
                own()
                nc.vector.tensor_tensor(cent[:], x_sb[:], small[:].unsqueeze(1).to_broadcast([P, H, CHUNK]),
                                        ALU.subtract).then_inc(dve_t.done("center"), 1)
                v.wait_ge(pe_t.sem, pe_t.upto(t, "var"))
                own()
                nc.vector.tensor_scalar_add(std[:], small[:], LN_EPS).then_inc(dve_t.done("var_eps"), 1)
                v.wait_ge(act_t.sem, act_t.upto(t, "sqrt"))
                own()
                nc.vector.reciprocal(std[:], std[:]).then_inc(dve_t.done("rstd"), 1)
                own()
                nc.vector.tensor_tensor(xn[:], cent[:], std[:].unsqueeze(1).to_broadcast([P, H, CHUNK]),
                                        ALU.mult).then_inc(dve_t.done("norm"), 1)
                v.wait_ge(pe_t.sem, pe_t.upto(t, "router"))
                own()
                nc.vector.tensor_tensor(logit[:], small[:, 0:blocks * E].rearrange("p (b e) -> p b e", e=E),
                                        gb_sb[:].unsqueeze(1).to_broadcast([P, blocks, E]), ALU.add).then_inc(dve_t.done("logit"), 1)
                own()
                nc.vector.tensor_reduce(top[:], logit[:], AX.X, ALU.max).then_inc(dve_t.done("top"), 1)
                own()
                nc.vector.tensor_tensor(logit[:], logit[:], top[:].unsqueeze(2).to_broadcast([P, blocks, E]),
                                        ALU.subtract).then_inc(dve_t.done("shift"), 1)
                v.wait_ge(act_t.sem, act_t.upto(t, "exp"))
                own()
                nc.vector.tensor_reduce(total[:], logit[:], AX.X, ALU.add).then_inc(dve_t.done("total"), 1)
                own()
                nc.vector.reciprocal(total[:], total[:]).then_inc(dve_t.done("inv"), 1)
                own()
                nc.vector.tensor_tensor(probs[:, :, 0:E], logit[:], total[:].unsqueeze(2).to_broadcast([P, blocks, E]),
                                        ALU.mult).then_inc(dve_t.done("prob"), 1)
                own()
                v.sem_inc(passed, 1)
                for b in range(blocks):
                    nc.vector.max(sorted8[:, b], probs[:, b, 0:E]).then_inc(dve_t.done(f"sort{b}"), 1)
                own()
                nc.vector.tensor_copy(first2[:, :, 0:2], sorted8[:, :, 0:2]).then_inc(dve_t.done("first2"), 1)
                own()
                v.sem_inc(passed, 1)
                for b in range(blocks):
                    nc.vector.match_replace(marked[:, b], first2[:, b], probs[:, b], -2.0).then_inc(dve_t.done(f"mark{b}"), 1)
                own()
                nc.vector.tensor_tensor(marked[:, :, 0:E], marked[:, :, 0:E], probs[:, :, 0:E],
                                        ALU.not_equal).then_inc(dve_t.done("chosen"), 1)
                own()
                nc.vector.tensor_tensor(cw[:], marked[:, :, 0:E], probs[:, :, 0:E], ALU.mult).then_inc(dve_t.done("cw"), 1)
                for e in range(E):
                    v.wait_ge(pe_t.sem, pe_t.upto(t, f"cwb{e}"))
                    for m in range(M):
                        v.wait_ge(act_t.sem, act_t.upto(t, f"gelu{e}_{m}"))
                        if e >= 2 and m == 0:
                            v.wait_ge(pe_t.sem, pe_t.upto(t, f"y{e - 2}"))
                        nc.vector.tensor_tensor(scaled[:, e % 2, m], act_out[:, e % 2, m], spread[:],
                                                ALU.mult).then_inc(dve_t.done(f"scale{e}_{m}"), 1)
                v.wait_ge(pe_t.sem, pe_t.upto(t, f"y{E - 1}"))
                v.wait_ge(stored_t.sem, stored_t.last_turn(t, "stored"))
                own()
                nc.vector.tensor_tensor(res[:], y[:], x_sb[:], ALU.add).then_inc(dve_t.done("res"), 1)
        return


def conv_arrays(i, pre=""):
    g = lambda n: i[pre + n]
    blocks = lambda m, k: m.T.reshape(k, P, m.shape[0]).transpose(1, 0, 2)
    halves = lambda v: v.reshape(HALVES, P).T
    lane, t, a = np.meshgrid(np.arange(P) // POINTS, np.arange(ROWPAIRS), np.arange(CELLS), indexing="ij")
    coords = np.stack([lane // 2 * CELLS + a, 2 * t + lane % 2], 1).reshape(P, 2, -1).astype(np.float32)
    return {
        "high": g("high_feature").reshape(BATCH, HALVES, P, 1024).transpose(0, 2, 1, 3),
        "w1": blocks(g("W1"), 4), "w2": blocks(g("W2"), 2), "b1": g("b1").reshape(P, 1), "b2": g("b2").reshape(P, 1),
        "wq": g("Wq").T, "wk": g("Wk").T, "wv": g("Wv").T, "bq": g("bq").reshape(QC, 1), "bk": g("bk").reshape(QC, 1),
        "bv": np.broadcast_to(g("bv"), (P, P)),
        "woff": g("Woff").reshape(POINTS, 2, P).transpose(2, 1, 0),
        "boff": np.tile(g("boff").reshape(POINTS, 2), (LANES, 1)),
        "wbv": g("Wb")[:, :P].T, "wbh": blocks(g("Wb")[:, P:], 2),
        "gamma": halves(g("gamma")), "beta": halves(g("beta")), "rmean": halves(g("rmean")), "rvar": halves(g("rvar")),
        "gmean": np.kron(np.eye(P // 8), np.full((8, 8), 1 / 8)).astype(np.float32),
        "coords": coords, "ramp": np.broadcast_to(np.arange(SIDE, dtype=np.float32), (P, SIDE)),
        "id": np.eye(P, dtype=np.float32),
    }


def attn_arrays(i, pre=""):
    g = lambda n: i[pre + n]
    head_rows = np.zeros((P, HALVES, HEADS), np.float32)
    for p in range(P):
        for h in range(HALVES):
            head_rows[p, h, h * 4 + p // 32] = 1.0
    keep = np.ones((P, BATCH * CHUNKS), np.float32)
    keep[:, ::CHUNKS] = 0.0
    restart = np.zeros((P, BATCH * CHUNKS), np.float32)
    restart[:, ::CHUNKS] = -3e38
    tok = np.arange(P)
    a = {}
    for n in "qkvo":
        a["a_w" + n] = g(f"w{n}_w").T.reshape(HALVES, P, 256).transpose(1, 0, 2)
        a["a_b" + n] = g(f"w{n}_b").reshape(HALVES, P).T
    a["a_wg"] = g("wg_w").reshape(32, 32)
    a["a_wgb"] = np.broadcast_to(g("wg_b").reshape(1, 1), (HEADS, 1))
    a["a_kvs"] = g("kv_norm_scale").reshape(HEADS, 32, 32)
    a["a_qks"] = g("qk_norm_scale").reshape(HEADS, 1)
    a["c_ones"] = np.full((P, P), 1 / 256, np.float32)
    a["c_id"] = np.eye(P, dtype=np.float32)
    a["c_hr"] = head_rows
    a["c_hc"] = head_rows.transpose(2, 1, 0)
    a["c_mask"] = np.stack([(tok % 32 // GROUP == m) for m in range(2)], 1).astype(np.float32)
    a["c_keep"] = keep
    a["c_restart"] = restart
    return a


def chunked(x):
    return x.reshape(BATCH, HALVES, P, CHUNKS, CHUNK).transpose(0, 3, 2, 1, 4).reshape(-1, P, HALVES, CHUNK)


def unchunked(x):
    return np.ascontiguousarray(x.reshape(BATCH, CHUNKS, P, HALVES, CHUNK).transpose(0, 3, 2, 1, 4).reshape(BATCH, 256, 64, 64))


ATTN_ARGS = ["a_wq", "a_wk", "a_wv", "a_wo", "a_bq", "a_bk", "a_bv", "a_bo", "a_wg", "a_wgb", "a_kvs", "a_qks",
             "c_ones", "c_id", "c_hr", "c_hc", "c_mask", "c_keep", "c_restart"]


def ffn_arrays(i, pre=""):
    g = lambda n: i[pre + n]
    return {
        "f_gw": g("gate_w").reshape(HALVES, P, EXPERTS).transpose(1, 0, 2),
        "f_gb": np.broadcast_to(g("gate_b"), (P, EXPERTS)),
        "f_w1": g("W1").reshape(EXPERTS, HALVES, P, 512).transpose(2, 0, 1, 3),
        "f_b1": g("b1").reshape(EXPERTS, 4, P).transpose(2, 0, 1),
        "f_w2": g("W2").reshape(EXPERTS, 4, P, 256).transpose(2, 0, 1, 3),
        "f_b2": g("b2"),
    }


FFN_ARGS = ["f_gw", "f_gb", "f_w1", "f_b1", "f_w2", "f_b2", "c_ones", "c_id"]


def build(nc, arrays):
    d = {k: nc.dram_tensor(f"in_{k}", a.shape, F32, kind="ExternalInput").ap() for k, a in arrays.items()}
    shape = (BATCH * CHUNKS, P, HALVES, CHUNK)
    base, x1, x2 = (nc.dram_tensor(n, shape, F32, kind="Internal").ap() for n in ("base", "after_conv", "after_attention"))
    out = nc.dram_tensor("out", shape, F32, kind="ExternalOutput").ap()
    conv_layer(nc, d["x_in"], base, x1, d)
    attn_phase(nc, x1, x2, *[d[n] for n in ATTN_ARGS])
    ffn_phase(nc, x2, out, *[d[n] for n in FFN_ARGS])


def kernel(**inputs):
    import concourse.bacc as bacc
    from concourse.bass_utils import run_bass_kernel_spmd as run

    i = {k: np.asarray(v) for k, v in inputs.items()}
    arrays = {"x_in": chunked(i["x"])}
    arrays.update(conv_arrays(i, "L0_conv_"))
    arrays.update(attn_arrays(i, "L1_attn_"))
    arrays.update(ffn_arrays(i, "L1_ffn_"))
    arrays = {k: np.ascontiguousarray(a) for k, a in arrays.items()}
    nc = bacc.Bacc("TRN2", target_bir_lowering=False, num_devices=1)
    build(nc, arrays)
    r = run(nc, [{f"in_{k}": a for k, a in arrays.items()}], core_ids=[0])
    return unchunked(r.results[0]["out"])
```

```python
from contextlib import ExitStack

import numpy as np
import concourse.bass as bass
from concourse import mybir

ALU = mybir.AluOpType
ACT = mybir.ActivationFunctionType
AX = mybir.AxisListType
F32 = mybir.dt.float32
BF16 = mybir.dt.bfloat16

P = 128
BATCH = 2
HALVES = 2
CHUNK = 512
CHUNKS = 8
TOKENS = CHUNK * CHUNKS
HEADS = 8
EXPERTS = 8
LN_EPS = 1e-5


class Track:

    def __init__(self, ctx, nc, name, steps):
        self.sem = ctx.enter_context(nc.semaphore(name))
        self.steps = steps
        self.place = {s: i + 1 for i, s in enumerate(steps)}
        assert len(self.place) == len(steps), name
        self.per = len(steps)
        self.emitted = 0

    def credit(self, eng):
        eng.sem_inc(self.sem, self.per)

    def done(self, step):
        assert self.steps[self.emitted % self.per] == step, (step, self.steps[self.emitted % self.per])
        self.emitted += 1
        return self.sem

    def upto(self, t, step):
        return t * self.per + (self.per + self.place[step])

    def last_turn(self, t, step):
        return t * self.per + self.place[step]

    def so_far(self, t):
        return t * self.per + (self.per + self.emitted % self.per)


class Loads:

    def __init__(self, ctx, nc, name, per=1):
        self.sem = ctx.enter_context(nc.semaphore(name))
        self.per = per

    def upto(self, t):
        return t * (16 * self.per) + 16 * self.per


def chunk_of(dram, index):
    return dram[bass.ds(index, 1)].rearrange("o p k n -> (o p) k n")


SIDE = 64
POINTS = 32
ROWPAIRS = SIDE // 2
LANES = 4
CELLS = SIDE // 2
QC = 16


def norm_phase(nc, x_dram, group_mean, gamma, beta, rmean, rvar, gn, bn):
    n = BATCH * HALVES
    with ExitStack() as ctx:
        def sb(name, shape):
            return ctx.enter_context(nc.sbuf_tensor("gn_" + name, shape, F32))
        x_sb = sb("x", [P, BATCH * CHUNKS, HALVES, CHUNK])
        avg = sb("avg", [P, P])
        stats = sb("stats", [P, n, CHUNKS, 6])
        mv = sb("mv", [P, n, 2])
        off = sb("off", [P, n])
        spread = sb("spread", [P, n])
        par = sb("par", [P, 4, HALVES])
        means = ctx.enter_context(nc.psum_tensor("gn_means", [P, n], F32))
        variances = ctx.enter_context(nc.psum_tensor("gn_vars", [P, n], F32))
        ready = ctx.enter_context(nc.semaphore("gn_constants"))
        parts = [Loads(ctx, nc, f"gn_x_loaded{i}") for i in range(4)]
        dve_t = Track(ctx, nc, "gn_dve", [f"stats{i}" for i in range(n * CHUNKS)] + [f"mv{i}" for i in range(n)]
                      + "off offsq spread eps inv shift rv_eps rv_inv scale bias0 bias".split())
        pe_t = Track(ctx, nc, "gn_pe", ["mean", "var"])
        act_t = Track(ctx, nc, "gn_act", ["std", "rv_std"])
        block = ctx.enter_context(nc.Block())

        @block.sync
        def _(sp):
            for i in range(4):
                sp.dma_start(x_sb[:, 4 * i:4 * i + 4], x_dram[4 * i:4 * i + 4].rearrange("c p k n -> p c k n")).then_inc(parts[i].sem, 16)
            sp.dma_start(avg[:], group_mean).then_inc(ready, 16)
            for i, src in enumerate((gamma, beta, rmean, rvar)):
                sp.dma_start(par[:, i], src).then_inc(ready, 16)

        @block.tensor
        def _(pe):
            pe_t.credit(pe)
            pe.wait_ge(ready, 80)
            pe.wait_ge(dve_t.sem, dve_t.upto(0, f"mv{n - 1}"))
            nc.tensor.matmul(means[:], avg[:], mv[:, :, 0], start=True, stop=True).then_inc(pe_t.done("mean"), 1)
            pe.wait_ge(dve_t.sem, dve_t.upto(0, "spread"))
            nc.tensor.matmul(variances[:], avg[:], spread[:], start=True, stop=True).then_inc(pe_t.done("var"), 1)

        @block.scalar
        def _(act):
            act_t.credit(act)
            act.wait_ge(dve_t.sem, dve_t.upto(0, "eps"))
            nc.scalar.activation(gn[:, :, 0], gn[:, :, 0], ACT.Sqrt).then_inc(act_t.done("std"), 1)
            act.wait_ge(dve_t.sem, dve_t.upto(0, "rv_eps"))
            nc.scalar.activation(bn[:, :, 0], bn[:, :, 0], ACT.Sqrt).then_inc(act_t.done("rv_std"), 1)

        @block.vector
        def _(v):
            dve_t.credit(v)

            def own():
                v.wait_ge(dve_t.sem, dve_t.so_far(0))
            i = 0
            for c in range(BATCH * CHUNKS):
                if c % 4 == 0:
                    v.wait_ge(parts[c // 4].sem, 16)
                for h in range(HALVES):
                    nc.vector.bn_stats(stats[:, c // CHUNKS * HALVES + h, c % CHUNKS], x_sb[:, c, h]).then_inc(dve_t.done(f"stats{i}"), 1)
                    i += 1
            own()
            for i in range(n):
                nc.vector.bn_aggr(mv[:, i], stats[:, i].rearrange("p c s -> p (c s)")).then_inc(dve_t.done(f"mv{i}"), 1)
            v.wait_ge(pe_t.sem, pe_t.upto(0, "mean"))
            own()
            nc.vector.tensor_tensor(off[:], mv[:, :, 0], means[:], ALU.subtract).then_inc(dve_t.done("off"), 1)
            own()
            nc.vector.tensor_tensor(off[:], off[:], off[:], ALU.mult).then_inc(dve_t.done("offsq"), 1)
            own()
            nc.vector.tensor_tensor(spread[:], off[:], mv[:, :, 1], ALU.add).then_inc(dve_t.done("spread"), 1)
            v.wait_ge(pe_t.sem, pe_t.upto(0, "var"))
            nc.vector.tensor_scalar_add(gn[:, :, 0], variances[:], LN_EPS).then_inc(dve_t.done("eps"), 1)
            v.wait_ge(act_t.sem, act_t.upto(0, "std"))
            nc.vector.reciprocal(gn[:, :, 0], gn[:, :, 0]).then_inc(dve_t.done("inv"), 1)
            own()
            nc.vector.scalar_tensor_tensor(gn[:, :, 1], means[:], -1.0, gn[:, :, 0], ALU.mult, ALU.mult).then_inc(dve_t.done("shift"), 1)
            v.wait_ge(ready, 80)
            nc.vector.tensor_scalar_add(bn[:, :, 0], par[:, 3], LN_EPS).then_inc(dve_t.done("rv_eps"), 1)
            v.wait_ge(act_t.sem, act_t.upto(0, "rv_std"))
            nc.vector.reciprocal(bn[:, :, 0], bn[:, :, 0]).then_inc(dve_t.done("rv_inv"), 1)
            own()
            nc.vector.tensor_tensor(bn[:, :, 0], bn[:, :, 0], par[:, 0], ALU.mult).then_inc(dve_t.done("scale"), 1)
            own()
            nc.vector.tensor_tensor(bn[:, :, 1], par[:, 2], bn[:, :, 0], ALU.mult).then_inc(dve_t.done("bias0"), 1)
            own()
            nc.vector.tensor_tensor(bn[:, :, 1], par[:, 1], bn[:, :, 1], ALU.subtract).then_inc(dve_t.done("bias"), 1)


def upsample_phase(nc, b, high, up):
    S = SIDE // 2
    with ExitStack() as ctx:
        bufs = []
        for h in range(HALVES):
            def sb(name, shape):
                return ctx.enter_context(nc.sbuf_tensor(f"up{b}{h}_{name}", shape, F32))
            bufs.append((sb("in", [P, S, S]), sb("q", [P, S, S + 2]), sb("t", [P, S, S]), sb("wide", [P, S, S, 2])))
        tall_q = ctx.enter_context(nc.sbuf_tensor(f"up{b}_tq", [P, S + 2, SIDE], F32))
        tall_t = ctx.enter_context(nc.sbuf_tensor(f"up{b}_tt", [P, S, SIDE], F32))
        loaded = [ctx.enter_context(nc.semaphore(f"up{b}_loaded{h}")) for h in range(HALVES)]
        wide_steps = "q q_left q_right t even odd".split()
        tall_steps = "tq tq_top tq_bottom tt rows_even rows_odd".split()
        wide_t = [Track(ctx, nc, f"up{b}_wide{h}", wide_steps) for h in range(HALVES)]
        tall_t_ = Track(ctx, nc, f"up{b}_tall", [f"{s}{h}" for h in range(HALVES) for s in tall_steps])
        block = ctx.enter_context(nc.Block())

        def widen(eng, ops, h):
            tr = wide_t[h]
            tr.credit(eng)
            src, q, t, wide = bufs[h]
            eng.wait_ge(loaded[h], 16)
            ops.tensor_scalar(q[:, :, 1:S + 1], src[:], 0.25, None, ALU.mult).then_inc(tr.done("q"), 1)
            ops.tensor_scalar(q[:, :, 0:1], src[:, :, 0:1], 0.25, None, ALU.mult).then_inc(tr.done("q_left"), 1)
            ops.tensor_scalar(q[:, :, S + 1:], src[:, :, S - 1:], 0.25, None, ALU.mult).then_inc(tr.done("q_right"), 1)
            ops.tensor_scalar(t[:], src[:], 0.75, None, ALU.mult).then_inc(tr.done("t"), 1)
            eng.wait_ge(tr.sem, tr.upto(0, "t"))
            ops.tensor_tensor(wide[:, :, :, 0], q[:, :, 0:S], t[:], ALU.add).then_inc(tr.done("even"), 1)
            ops.tensor_tensor(wide[:, :, :, 1], q[:, :, 2:], t[:], ALU.add).then_inc(tr.done("odd"), 1)

        @block.sync
        def _(sp):
            for h in range(HALVES):
                sp.dma_start(bufs[h][0][:], high[b, :, h].rearrange("p (y x) -> p y x", x=S)).then_inc(loaded[h], 16)

        @block.gpsimd
        def _(pool):
            widen(pool, nc.gpsimd, 1)

        @block.vector
        def _(v):
            widen(v, nc.vector, 0)
            tr = tall_t_
            tr.credit(v)
            for h in range(HALVES):
                wide = bufs[h][3][:].rearrange("p y x e -> p y (x e)")
                rows = up[:, h].rearrange("p (y e x) -> p y e x", e=2, x=SIDE)
                v.wait_ge(wide_t[h].sem, wide_t[h].upto(0, "odd"))
                v.wait_ge(tr.sem, tr.so_far(0))
                nc.vector.tensor_scalar(tall_q[:, 1:S + 1], wide, 0.25, None, ALU.mult).then_inc(tr.done(f"tq{h}"), 1)
                nc.vector.tensor_scalar(tall_q[:, 0:1], wide[:, 0:1], 0.25, None, ALU.mult).then_inc(tr.done(f"tq_top{h}"), 1)
                nc.vector.tensor_scalar(tall_q[:, S + 1:], wide[:, S - 1:], 0.25, None, ALU.mult).then_inc(tr.done(f"tq_bottom{h}"), 1)
                nc.vector.tensor_scalar(tall_t[:], wide, 0.75, None, ALU.mult).then_inc(tr.done(f"tt{h}"), 1)
                v.wait_ge(tr.sem, tr.so_far(0))
                nc.vector.tensor_tensor(rows[:, :, 0], tall_q[:, 0:S], tall_t[:], ALU.add).then_inc(tr.done(f"rows_even{h}"), 1)
                nc.vector.tensor_tensor(rows[:, :, 1], tall_q[:, 2:], tall_t[:], ALU.add).then_inc(tr.done(f"rows_odd{h}"), 1)


def features_phase(nc, b, x_dram, base_dram, w, gn, up, qf, vf):
    with ExitStack() as ctx:
        def sb(name, shape):
            return ctx.enter_context(nc.sbuf_tensor(f"fe{b}_{name}", shape, F32))
        w1 = sb("w1", [P, 4, P])
        w2 = sb("w2", [P, HALVES, P])
        wb = sb("wb", [P, HALVES, 256])
        b1 = sb("b1", [P, 1])
        b2 = sb("b2", [P, 1])
        x_sb = sb("x", [P, HALVES, CHUNK])
        xg = sb("xg", [P, HALVES, CHUNK])
        base = sb("base", [P, HALVES, CHUNK])
        ps = ctx.enter_context(nc.psum_tensor(f"fe{b}_ps", [P, 2, 512], F32))
        ps_base = ctx.enter_context(nc.psum_tensor(f"fe{b}_psb", [P, HALVES, 512], F32))
        ready = ctx.enter_context(nc.semaphore(f"fe{b}_constants"))
        loads = Loads(ctx, nc, f"fe{b}_x_loaded")
        stores = Loads(ctx, nc, f"fe{b}_stored")
        pe_t = Track(ctx, nc, f"fe{b}_pe", ["vf", "base", "qf"])
        act_t = Track(ctx, nc, f"fe{b}_act", ["gn0", "gn1", "qf"])
        dve_t = Track(ctx, nc, f"fe{b}_dve", ["vf", "base"])
        stored_t = Track(ctx, nc, f"fe{b}_base_stored", ["stored"])
        consts = [(w1, w["w1"]), (w2, w["w2"]), (wb, w["wbh"]), (b1, w["b1"]), (b2, w["b2"])]
        block = ctx.enter_context(nc.Block())

        @block.sync
        def _(sp):
            for dst, src in consts:
                sp.dma_start(dst[:], src).then_inc(ready, 16)
            with sp.Fori(0, CHUNKS) as t:
                sp.wait_ge(act_t.sem, act_t.last_turn(t, "gn1"))
                sp.dma_start(x_sb[:], chunk_of(x_dram, t + b * CHUNKS)).then_inc(loads.sem, 16)

        @block.gpsimd
        def _(pool):
            stored_t.credit(pool)
            with pool.Fori(0, CHUNKS) as t:
                pool.wait_ge(dve_t.sem, dve_t.upto(t, "base"))
                pool.dma_start(chunk_of(base_dram, t + b * CHUNKS), base[:]).then_inc(stores.sem, 16)
                pool.wait_ge(stores.sem, stores.upto(t))
                pool.sem_inc(stored_t.done("stored"), 1)

        @block.tensor
        def _(pe):
            pe_t.credit(pe)
            pe.wait_ge(ready, 16 * len(consts))
            with pe.Fori(0, CHUNKS) as t:
                u = [up[:, k, bass.ds(t * CHUNK, CHUNK)] for k in range(HALVES)]
                pe.wait_ge(dve_t.sem, dve_t.last_turn(t, "vf"))
                for k in range(HALVES):
                    mm = nc.tensor.matmul(ps[:, 1], w2[:, k], u[k], start=(k == 0), stop=(k == 1))
                mm.then_inc(pe_t.done("vf"), 1)
                pe.wait_ge(dve_t.sem, dve_t.last_turn(t, "base"))
                for h in range(HALVES):
                    for k in range(HALVES):
                        mm = nc.tensor.matmul(ps_base[:, h], wb[:, k, h * P:(h + 1) * P], u[k], start=(k == 0), stop=(k == 1))
                mm.then_inc(pe_t.done("base"), 1)
                pe.wait_ge(act_t.sem, act_t.upto(t, "gn1"))
                for k in range(4):
                    mm = nc.tensor.matmul(ps[:, 0], w1[:, k], u[k] if k < 2 else xg[:, k - 2], start=(k == 0), stop=(k == 3))
                mm.then_inc(pe_t.done("qf"), 1)

        @block.scalar
        def _(act):
            act_t.credit(act)
            act.wait_ge(ready, 16 * len(consts))
            with act.Fori(0, CHUNKS) as t:
                act.wait_ge(loads.sem, loads.upto(t))
                act.wait_ge(pe_t.sem, pe_t.last_turn(t, "qf"))
                for h in range(HALVES):
                    g = b * HALVES + h
                    nc.scalar.activation(xg[:, h], x_sb[:, h], ACT.Identity, bias=gn[:, g, 1:2], scale=gn[:, g, 0:1]).then_inc(act_t.done(f"gn{h}"), 1)
                act.wait_ge(pe_t.sem, pe_t.upto(t, "qf"))
                nc.scalar.activation(qf[:, bass.ds(t * CHUNK, CHUNK)], ps[:, 0], ACT.Identity, bias=b1[:]).then_inc(act_t.done("qf"), 1)

        @block.vector
        def _(v):
            dve_t.credit(v)
            v.wait_ge(ready, 16 * len(consts))
            with v.Fori(0, CHUNKS) as t:
                v.wait_ge(pe_t.sem, pe_t.upto(t, "vf"))
                nc.vector.tensor_scalar(vf[:, bass.ds(t * CHUNK, CHUNK)], ps[:, 1], b2[:], None, ALU.add).then_inc(dve_t.done("vf"), 1)
                v.wait_ge(pe_t.sem, pe_t.upto(t, "base"))
                v.wait_ge(stored_t.sem, stored_t.last_turn(t, "stored"))
                nc.vector.tensor_copy(base[:], ps_base[:]).then_inc(dve_t.done("base"), 1)


def tables_phase(nc, b, w, coords, qf, vf, q_parts, k_parts, v_table, where):
    with ExitStack() as ctx:
        def sb(name, shape, dt=F32):
            return ctx.enter_context(nc.sbuf_tensor(f"ta{b}_{name}", shape, dt))
        wq, wk, wv, woff = sb("wq", [P, P]), sb("wk", [P, P]), sb("wv", [P, P]), sb("woff", [P, 2, POINTS])
        bq, bk, bv, boff = sb("bq", [P, 1]), sb("bk", [P, 1]), sb("bv", [P, P]), sb("boff", [P, 2])
        minus = sb("minus", [P, 2, 2])
        xy = sb("xy", [P, 2, ROWPAIRS * CELLS])
        whole = sb("whole", [P, 2, CHUNK])
        part = sb("part", [P, 2, CHUNK], BF16)
        ring = ctx.enter_context(nc.psum_tensor(f"ta{b}_ring", [P, 4, 512], F32))
        ready = ctx.enter_context(nc.semaphore(f"ta{b}_constants"))
        splits = [f"{n}{c}" for c in range(8) for n in "qk"]
        groups = splits + [f"v{g}" for g in range(8)] + [f"off{i}" for i in range(4)]
        pe_t = Track(ctx, nc, f"ta{b}_pe", groups)
        act_order, dve_order = [], []
        for i in range(len(splits) + 1):
            if i < len(splits):
                act_order += [f"whole_{splits[i]}", f"first_{splits[i]}"]
                dve_order += [f"rest_{splits[i]}"]
            if i:
                act_order += [f"second_{splits[i - 1]}", f"third_{splits[i - 1]}"]
                dve_order += [f"last_{splits[i - 1]}"]
        act_t = Track(ctx, nc, f"ta{b}_act", act_order)
        dve_t = Track(ctx, nc, f"ta{b}_dve", dve_order + [f"v{g}" for g in range(8)]
                      + [f"{s}{i}" for i in range(4) for s in ("off", "clamp")])
        consts = [(wq, w["wq"]), (wk, w["wk"]), (wv, w["wv"]), (woff, w["woff"]), (bq, w["bq"]), (bk, w["bk"]),
                  (bv, w["bv"]), (boff, w["boff"]), (xy, coords), (minus, w["minus"])]
        block = ctx.enter_context(nc.Block())

        @block.sync
        def _(sp):
            for dst, src in consts:
                sp.dma_start(dst[:], src).then_inc(ready, 16)

        @block.tensor
        def _(pe):
            pe_t.credit(pe)
            pe.wait_ge(ready, 16 * len(consts))
            for i, name in enumerate(groups):
                kind, n = name.rstrip("0123456789"), int(name.lstrip("qkvof"))
                dst = ring[:, i % 4]
                if i >= 4:
                    last = groups[i - 4]
                    if last[0] in "qk":
                        pe.wait_ge(act_t.sem, act_t.upto(0, f"whole_{last}"))
                    else:
                        pe.wait_ge(dve_t.sem, dve_t.upto(0, last))
                if kind in "qk":
                    src = qf if kind == "q" else vf
                    mm = nc.tensor.matmul(dst, (wq if kind == "q" else wk)[:], src[:, n * CHUNK:(n + 1) * CHUNK], start=True, stop=True)
                elif kind == "v":
                    cols = vf[:].rearrange("p (y x) -> p x y", x=SIDE)
                    for j in range(4):
                        for h in range(2):
                            mm = nc.tensor.matmul(dst[64 * h:64 * h + 64, j * P:(j + 1) * P], cols[:, 32 * h + 4 * n + j], wv[:],
                                                  start=True, stop=True)
                else:
                    cells = qf[:].rearrange("p (t r h a) -> p t r h a", r=2, h=2, a=CELLS)
                    half = slice(n % 2 * 16, n % 2 * 16 + 16)
                    for lane in range(LANES):
                        mm = nc.tensor.matmul(dst[32 * lane:32 * lane + 32], woff[:, n // 2], cells[:, half, lane % 2, lane // 2],
                                              start=True, stop=True)
                mm.then_inc(pe_t.done(name), 1)

        @block.scalar
        def _(act):
            act_t.credit(act)
            act.wait_ge(ready, 16 * len(consts))
            for i in range(len(splits) + 1):
                if i < len(splits):
                    name = splits[i]
                    act.wait_ge(pe_t.sem, pe_t.upto(0, name))
                    if i >= 2:
                        act.wait_ge(act_t.sem, act_t.upto(0, f"third_{splits[i - 2]}"))
                    nc.scalar.activation(whole[:, i % 2], ring[:, i % 4], ACT.Identity, bias=(bq if name[0] == "q" else bk)[:]
                                         ).then_inc(act_t.done(f"whole_{name}"), 1)
                    act.wait_ge(act_t.sem, act_t.so_far(0))
                    if i >= 2:
                        act.wait_ge(dve_t.sem, dve_t.upto(0, f"last_{splits[i - 2]}"))
                    nc.scalar.copy(part[:, i % 2], whole[:, i % 2]).then_inc(act_t.done(f"first_{name}"), 1)
                if i:
                    name, j = splits[i - 1], (i - 1) % 2
                    c = int(name[1:])
                    act.wait_ge(dve_t.sem, dve_t.upto(0, f"rest_{name}"))
                    nc.scalar.copy(part[:, j], whole[:, j]).then_inc(act_t.done(f"second_{name}"), 1)
                    act.wait_ge(dve_t.sem, dve_t.upto(0, f"last_{name}"))
                    if name[0] == "q":
                        dst, src = q_parts[:, c * CHUNK:(c + 1) * CHUNK], whole[:, j]
                    else:
                        dst, src = k_parts[:, :, 8 * c:8 * c + 8], whole[:, j].rearrange("p (y x) -> p x y", x=SIDE)
                    nc.scalar.copy(dst, src).then_inc(act_t.done(f"third_{name}"), 1)

        @block.vector
        def _(v):
            dve_t.credit(v)
            v.wait_ge(ready, 16 * len(consts))

            def take_off(step, after, name, j, which):
                v.wait_ge(act_t.sem, act_t.upto(0, f"{after}_{name}"))
                which = minus[:, "qk".index(name[0]), which:which + 1]
                nc.vector.scalar_tensor_tensor(whole[:, j], part[:, j], which, whole[:, j], ALU.mult, ALU.add
                                               ).then_inc(dve_t.done(f"{step}_{name}"), 1)

            for i in range(len(splits) + 1):
                if i < len(splits):
                    take_off("rest", "first", splits[i], i % 2, 0)
                if i:
                    take_off("last", "second", splits[i - 1], (i - 1) % 2, 1)
            for g in range(8):
                v.wait_ge(pe_t.sem, pe_t.upto(0, f"v{g}"))
                nc.vector.tensor_tensor(v_table[:, 4 * g:4 * g + 4], ring[:, (16 + g) % 4].rearrange("p (x c) -> p x c", c=P),
                                        bv[:].unsqueeze(1).to_broadcast([P, 4, P]), ALU.add).then_inc(dve_t.done(f"v{g}"), 1)
            for i in range(4):
                v.wait_ge(pe_t.sem, pe_t.upto(0, f"off{i}"))
                piece = where[:, i // 2, i % 2 * 512:i % 2 * 512 + 512]
                nc.vector.scalar_tensor_tensor(piece, ring[:, i % 4], boff[:, i // 2:i // 2 + 1], xy[:, i // 2, i % 2 * 512:i % 2 * 512 + 512],
                                               ALU.add, ALU.add).then_inc(dve_t.done(f"off{i}"), 1)
                v.wait_ge(dve_t.sem, dve_t.upto(0, f"off{i}"))
                nc.vector.tensor_scalar(piece, piece, 0.0, float(SIDE - 1), ALU.max, ALU.min).then_inc(dve_t.done(f"clamp{i}"), 1)


def sample_phase(nc, b, ramp, identity, q_parts, k_parts, v_table, where, val):
    C, G8, HS = CELLS, 8, SIDE // 2
    with ExitStack() as ctx:
        def sb(name, shape, dt=F32):
            return ctx.enter_context(nc.sbuf_tensor(f"sa{b}_{name}", shape, dt))
        ramp_sb = sb("ramp", [P, SIDE])
        ident = sb("ident", [P, P])
        qt = sb("qt", [P, P], BF16)
        scores = sb("scores", [P, SIDE, SIDE])
        hx = sb("hx", [P, C, SIDE])
        hx_own = sb("hx_own", [P, C, 2, LANES, HS])
        hy = sb("hy", [P, C, SIDE])
        ahy = sb("ahy", [P, C, SIDE])
        hy_t = sb("hy_t", [P, C, P])
        prod = sb("prod", [P, C, SIDE])
        A = sb("A", [P, HS, P])
        logit, logit_t, probs, attn_t, attn = (sb(n, [P, 32]) for n in ("logit", "logit_t", "probs", "attn_t", "attn"))
        most, total = sb("most", [P, 1]), sb("total", [P, 1])
        ring = ctx.enter_context(nc.psum_tensor(f"sa{b}_ring", [P, 3, 1024], F32))
        out_ps = ctx.enter_context(nc.psum_tensor(f"sa{b}_out", [P, 512], F32))
        ready = ctx.enter_context(nc.semaphore(f"sa{b}_constants"))
        zeroed = ctx.enter_context(nc.semaphore(f"sa{b}_zeroed"))
        passed = ctx.enter_context(nc.semaphore(f"sa{b}_passed"))
        passed_pool = ctx.enter_context(nc.semaphore(f"sa{b}_passed_pool"))
        fills = [f"tr{g}" for g in range(4)] + [f"s{k}" for k in range(8)] + [f"l{k}" for k in range(4)] + [f"a{k}" for k in range(4)]
        place = {name: i % 3 for i, name in enumerate(fills)}
        first_a = fills.index("a0")
        pe_t = Track(ctx, nc, f"sa{b}_pe", fills[:first_a] + ["out"] + fills[first_a:])
        act_t = Track(ctx, nc, f"sa{b}_act", ["abs_y", "hat_y", "abs_x", "hat_x"] + [f"tr{g}{r}" for g in range(4) for r in "ab"] + ["qt"]
                      + [f"s{k}{r}" for k in range(0, 8, 2) for r in "ab"] + "exp out".split())
        dve_t = Track(ctx, nc, f"sa{b}_dve", ["own2", "own3"] + [f"s{k}{r}" for k in range(1, 8, 2) for r in "ab"] + [f"l{k}{h}" for k in range(4) for h in "ab"]
                      + "logit logit_t most neg inv attn_t attn ahy".split() + [f"a{k}" for k in range(4)])
        pool_t = Track(ctx, nc, f"sa{b}_pool", ["dist_y", "dist_x", "own0", "own1"])
        tail_pe = Track(ctx, nc, f"sa{b}_tail_pe", ["out"])
        tail_act = Track(ctx, nc, f"sa{b}_tail_act", ["out"])
        block = ctx.enter_context(nc.Block())

        def own_lane(lane):
            s = slice(POINTS * lane, POINTS * lane + POINTS)
            return hx_own[s].rearrange("q a h l x -> q (a h) l x")[:, :, lane], hx[s].rearrange("q a (h x) -> q (a h) x", h=2)

        @block.sync
        def _(sp):
            sp.dma_start(ramp_sb[:], ramp).then_inc(ready, 16)
            sp.dma_start(ident[:], identity).then_inc(ready, 16)

        @block.gpsimd
        def _(pool):
            pool_t.credit(pool)
            nc.gpsimd.memset(hy_t[:], 0.0).then_inc(zeroed, 1)
            nc.gpsimd.memset(hx_own[:], 0.0).then_inc(zeroed, 1)
            nc.gpsimd.memset(A[:], 0.0).then_inc(zeroed, 1)
            pool.wait_ge(ready, 32)
            pool.wait_ge(zeroed, 3)
            grid = ramp_sb[:].unsqueeze(1).to_broadcast([P, C, SIDE])
            with pool.Fori(0, ROWPAIRS) as t:
                places = where[:, :, bass.ds(t * C, C)]
                pool.wait_ge(dve_t.sem, dve_t.last_turn(t, "ahy"))
                pool.wait_ge(pool_t.sem, pool_t.so_far(t))
                nc.gpsimd.tensor_tensor(hy[:], grid, places[:, 1].unsqueeze(2).to_broadcast([P, C, SIDE]),
                                        ALU.subtract).then_inc(pool_t.done("dist_y"), 1)
                nc.gpsimd.tensor_tensor(hx[:], grid, places[:, 0].unsqueeze(2).to_broadcast([P, C, SIDE]),
                                        ALU.subtract).then_inc(pool_t.done("dist_x"), 1)
                pool.wait_ge(act_t.sem, act_t.upto(t, "hat_x"))
                pool.wait_ge(pe_t.sem, pe_t.last_turn(t, "a3"))
                pool.sem_inc(passed_pool, 1)
                for lane in range(2):
                    nc.gpsimd.tensor_copy(*own_lane(lane)).then_inc(pool_t.done(f"own{lane}"), 1)

        @block.tensor
        def _(pe):
            pe_t.credit(pe)
            pe.wait_ge(ready, 32)
            pe.wait_ge(zeroed, 3)

            def free(t, i):
                last = i >= 3
                name = fills[i - 3 if last else i + 3 * ((len(fills) - 1 - i) // 3)]
                if name[0] == "t" or name in ("s0", "s2", "s4", "s6"):
                    tr, step = act_t, name + "b"
                else:
                    tr, step = dve_t, name if name[0] == "a" else name + "b"
                pe.wait_ge(tr.sem, tr.upto(t, step) if last else tr.last_turn(t, step))

            def weighted_values(tr):
                for x in range(HS):
                    mm = nc.tensor.matmul(out_ps[:, 0:P], v_table[:, x], A[:, x], start=(x == 0), stop=(x == HS - 1))
                mm.then_inc(tr.done("out"), 1)

            with pe.Fori(0, ROWPAIRS) as t:
                pe.wait_ge(act_t.sem, act_t.upto(t, "hat_y"))
                for i, name in enumerate(fills):
                    pair = ring[:, place[name]]
                    n = int(name.lstrip("trsla"))
                    if name == "s0":
                        pe.wait_ge(act_t.sem, act_t.upto(t, "qt"))
                    if name == "l0":
                        pe.wait_ge(act_t.sem, act_t.upto(t, "s6b"))
                        pe.wait_ge(dve_t.sem, dve_t.upto(t, "s7b"))
                    if name == "a0":
                        pe.wait_ge(dve_t.sem, dve_t.last_turn(t, "a3"))
                        pe.wait_ge(act_t.sem, act_t.last_turn(t, "out"))
                        weighted_values(pe_t)
                        pe.wait_ge(pool_t.sem, pool_t.upto(t, "own1"))
                        pe.wait_ge(dve_t.sem, dve_t.upto(t, "ahy"))
                    free(t, i)
                    if name[0] == "t":
                        pe.sem_inc(passed, 1)
                        for j in range(G8):
                            mm = nc.tensor.transpose(pair[0:64, j * P:(j + 1) * P], hy[:, G8 * n + j], ident[:])
                    elif name[0] == "s":
                        for j in range(G8):
                            mm = nc.tensor.matmul(pair[0:64, j * P:(j + 1) * P], k_parts[:, n * G8 + j], qt[:], start=True, stop=True)
                    elif name[0] == "l":
                        own_rows = scores[:].rearrange("q (h a) x -> q a h x", h=2)
                        for j in range(G8):
                            mm = nc.tensor.matmul(pair[:, j * P:(j + 1) * P], hy_t[:, n * G8 + j], own_rows[:, n * G8 + j],
                                                  start=True, stop=True)
                    else:
                        for j in range(G8):
                            for h in range(2):
                                a = n * G8 + j
                                mm = nc.tensor.matmul(pair[64 * h:64 * h + 64, j * P:(j + 1) * P], ahy[:, a],
                                                      hx_own[:, a, h].rearrange("q l x -> q (l x)"), start=True, stop=True)
                    mm.then_inc(pe_t.done(name), 1)
            tail_pe.credit(pe)
            pe.wait_ge(dve_t.sem, dve_t.last_turn(ROWPAIRS, "a3"))
            pe.wait_ge(act_t.sem, act_t.last_turn(ROWPAIRS, "out"))
            weighted_values(tail_pe)

        def half_scores(copy, k, r):
            src = ring[0:64, place[f"s{k}"]].rearrange("q (x r n) -> q r x n", r=2, n=SIDE)[:, r]
            return copy(scores[64 * r:64 * r + 64, :, k * G8:(k + 1) * G8].rearrange("q n x -> q x n"), src)

        @block.scalar
        def _(act):
            act_t.credit(act)
            act.wait_ge(zeroed, 3)

            def keep_values(slot, tr):
                nc.scalar.copy(slot.rearrange("p (r h a) -> p r h a", r=2, h=2),
                               out_ps[:, 0:P].rearrange("p (a h r) -> p r h a", h=2, r=2)).then_inc(tr.done("out"), 1)

            with act.Fori(0, ROWPAIRS) as t:
                for buf, c in ((hy, "y"), (hx, "x")):
                    act.wait_ge(pool_t.sem, pool_t.upto(t, f"dist_{c}"))
                    nc.scalar.activation(buf[:], buf[:], ACT.Abs).then_inc(act_t.done(f"abs_{c}"), 1)
                    act.wait_ge(act_t.sem, act_t.so_far(t))
                    nc.scalar.activation(buf[:], buf[:], ACT.Relu, bias=1.0, scale=-1.0).then_inc(act_t.done(f"hat_{c}"), 1)
                act.wait_ge(pe_t.sem, pe_t.last_turn(t, "l3"))
                for g in range(4):
                    act.wait_ge(pe_t.sem, pe_t.upto(t, f"tr{g}"))
                    src = ring[0:64, place[f"tr{g}"]].rearrange("q (i r p) -> q i r p", r=2, p=POINTS)
                    for r in range(2):
                        dst = hy_t[64 * r:64 * r + 64, G8 * g:G8 * g + G8].rearrange("q a (h r p) -> q (a h) r p", h=2, r=2)
                        nc.scalar.copy(dst[:, :, r], src[:, :, r]).then_inc(act_t.done(f"tr{g}{'ab'[r]}"), 1)
                nc.scalar.copy(qt[:], q_parts[:, bass.ds(t * P, P)]).then_inc(act_t.done("qt"), 1)
                for k in range(0, 8, 2):
                    act.wait_ge(pe_t.sem, pe_t.upto(t, f"s{k}"))
                    for r in range(2):
                        half_scores(nc.scalar.copy, k, r).then_inc(act_t.done(f"s{k}{'ab'[r]}"), 1)
                act.wait_ge(dve_t.sem, dve_t.upto(t, "neg"))
                nc.scalar.activation(probs[:], logit_t[:], ACT.Exp, bias=most[:], scale=0.25, accum_out=total[:]).then_inc(act_t.done("exp"), 1)
                act.wait_ge(pe_t.sem, pe_t.upto(t, "out"))
                keep_values(val[:, bass.ds(t * P, P)], act_t)
            tail_act.credit(act)
            act.wait_ge(tail_pe.sem, tail_pe.upto(0, "out"))
            keep_values(val[:, ROWPAIRS * P:], tail_act)

        @block.vector
        def _(v):
            dve_t.credit(v)
            v.wait_ge(zeroed, 3)
            with v.Fori(0, ROWPAIRS) as t:
                def own():
                    v.wait_ge(dve_t.sem, dve_t.so_far(t))
                v.wait_ge(act_t.sem, act_t.upto(t, "hat_x"))
                v.wait_ge(pe_t.sem, pe_t.last_turn(t, "a3"))
                own()
                for lane in range(2, 4):
                    nc.vector.tensor_copy(*own_lane(lane)).then_inc(dve_t.done(f"own{lane}"), 1)
                for k in range(1, 8, 2):
                    v.wait_ge(pe_t.sem, pe_t.upto(t, f"s{k}"))
                    for r in range(2):
                        half_scores(nc.vector.tensor_copy, k, r).then_inc(dve_t.done(f"s{k}{'ab'[r]}"), 1)
                for k in range(4):
                    v.wait_ge(pe_t.sem, pe_t.upto(t, f"l{k}"))
                    for h in range(2):
                        s, cells = slice(64 * h, 64 * h + 64), slice(k * G8, (k + 1) * G8)
                        src = ring[s, place[f"l{k}"]].rearrange("p (a h x) -> p h a x", h=2, x=SIDE)[:, h]
                        nc.vector.tensor_tensor(prod[s, cells], hx[s, cells], src, ALU.mult).then_inc(dve_t.done(f"l{k}{'ab'[h]}"), 1)
                own()
                nc.vector.tensor_reduce(logit[:], prod[:], AX.X, ALU.add).then_inc(dve_t.done("logit"), 1)
                own()
                nc.vector.transpose(logit_t[:], logit[:]).then_inc(dve_t.done("logit_t"), 1)
                own()
                nc.vector.tensor_reduce(most[:], logit_t[:], AX.X, ALU.max).then_inc(dve_t.done("most"), 1)
                own()
                nc.vector.tensor_scalar(most[:], most[:], -0.25, None, ALU.mult).then_inc(dve_t.done("neg"), 1)
                v.wait_ge(act_t.sem, act_t.upto(t, "exp"))
                nc.vector.reciprocal(total[:], total[:]).then_inc(dve_t.done("inv"), 1)
                own()
                nc.vector.tensor_scalar(attn_t[:], probs[:], total[:], None, ALU.mult).then_inc(dve_t.done("attn_t"), 1)
                own()
                nc.vector.transpose(attn[:], attn_t[:]).then_inc(dve_t.done("attn"), 1)
                own()
                nc.vector.tensor_tensor(ahy[:], hy[:], attn[:].unsqueeze(2).to_broadcast([P, C, SIDE]), ALU.mult).then_inc(dve_t.done("ahy"), 1)
                v.wait_ge(pe_t.sem, pe_t.upto(t, "out"))
                for k in range(4):
                    v.wait_ge(pe_t.sem, pe_t.upto(t, f"a{k}"))
                    nc.vector.tensor_copy(A[:, :, k * 32:(k + 1) * 32].rearrange("q x n -> q n x"),
                                          ring[:, place[f"a{k}"]].rearrange("q (n x) -> q n x", x=HS)).then_inc(dve_t.done(f"a{k}"), 1)


def merge_phase(nc, b, x_dram, base_dram, out_dram, wbv, bn, val):
    H = HALVES
    with ExitStack() as ctx:
        def sb(name, shape):
            return ctx.enter_context(nc.sbuf_tensor(f"me{b}_{name}", shape, F32))
        w_sb = sb("w", [P, 256])
        x_sb, base, tmp, res = (sb(n, [P, H, CHUNK]) for n in ("x", "base", "tmp", "res"))
        ps = ctx.enter_context(nc.psum_tensor(f"me{b}_ps", [P, H, 512], F32))
        ready = ctx.enter_context(nc.semaphore(f"me{b}_constants"))
        x_loads = Loads(ctx, nc, f"me{b}_x_loaded")
        base_loads = Loads(ctx, nc, f"me{b}_base_loaded")
        stores = Loads(ctx, nc, f"me{b}_stored")
        pe_t = Track(ctx, nc, f"me{b}_pe", ["conv"])
        act_t = Track(ctx, nc, f"me{b}_act", ["relu0", "relu1"])
        dve_t = Track(ctx, nc, f"me{b}_dve", ["sum", "res"])
        stored_t = Track(ctx, nc, f"me{b}_res_stored", ["stored"])
        block = ctx.enter_context(nc.Block())

        @block.sync
        def _(sp):
            sp.dma_start(w_sb[:], wbv).then_inc(ready, 16)
            with sp.Fori(0, CHUNKS) as t:
                sp.wait_ge(dve_t.sem, dve_t.last_turn(t, "sum"))
                sp.dma_start(base[:], chunk_of(base_dram, t + b * CHUNKS)).then_inc(base_loads.sem, 16)
                sp.wait_ge(dve_t.sem, dve_t.last_turn(t, "res"))
                sp.dma_start(x_sb[:], chunk_of(x_dram, t + b * CHUNKS)).then_inc(x_loads.sem, 16)

        @block.gpsimd
        def _(pool):
            stored_t.credit(pool)
            with pool.Fori(0, CHUNKS) as t:
                pool.wait_ge(dve_t.sem, dve_t.upto(t, "res"))
                pool.dma_start(chunk_of(out_dram, t + b * CHUNKS), res[:]).then_inc(stores.sem, 16)
                pool.wait_ge(stores.sem, stores.upto(t))
                pool.sem_inc(stored_t.done("stored"), 1)

        @block.tensor
        def _(pe):
            pe_t.credit(pe)
            pe.wait_ge(ready, 16)
            with pe.Fori(0, CHUNKS) as t:
                pe.wait_ge(dve_t.sem, dve_t.last_turn(t, "sum"))
                for h in range(H):
                    mm = nc.tensor.matmul(ps[:, h], w_sb[:, h * P:(h + 1) * P], val[:, bass.ds(t * CHUNK + P, CHUNK)], start=True, stop=True)
                mm.then_inc(pe_t.done("conv"), 1)

        @block.scalar
        def _(act):
            act_t.credit(act)
            with act.Fori(0, CHUNKS) as t:
                act.wait_ge(dve_t.sem, dve_t.upto(t, "sum"))
                for h in range(H):
                    nc.scalar.activation(tmp[:, h], tmp[:, h], ACT.Relu, bias=bn[:, h, 1:2], scale=bn[:, h, 0:1]).then_inc(act_t.done(f"relu{h}"), 1)

        @block.vector
        def _(v):
            dve_t.credit(v)
            with v.Fori(0, CHUNKS) as t:
                v.wait_ge(pe_t.sem, pe_t.upto(t, "conv"))
                v.wait_ge(base_loads.sem, base_loads.upto(t))
                v.wait_ge(dve_t.sem, dve_t.so_far(t))
                nc.vector.tensor_tensor(tmp[:], base[:], ps[:], ALU.add).then_inc(dve_t.done("sum"), 1)
                v.wait_ge(act_t.sem, act_t.upto(t, "relu1"))
                v.wait_ge(x_loads.sem, x_loads.upto(t))
                v.wait_ge(stored_t.sem, stored_t.last_turn(t, "stored"))
                nc.vector.tensor_tensor(res[:], tmp[:], x_sb[:], ALU.add).then_inc(dve_t.done("res"), 1)


def conv_layer(nc, x_dram, base_dram, out_dram, w):
    with ExitStack() as ctx:
        def sb(name, shape, dt=F32):
            return ctx.enter_context(nc.sbuf_tensor("cl_" + name, shape, dt))
        gn = sb("gn", [P, BATCH * HALVES, 2])
        bn = sb("bn", [P, HALVES, 2])
        norm_phase(nc, x_dram, w["gmean"], w["gamma"], w["beta"], w["rmean"], w["rvar"], gn, bn)
        q_parts = sb("q_parts", [P, TOKENS], BF16)
        k_parts = sb("k_parts", [P, SIDE, SIDE], BF16)
        v_table = sb("v_table", [P, SIDE // 2, P])
        where = sb("where", [P, 2, ROWPAIRS * CELLS])
        for b in range(BATCH):
            with ExitStack() as inner:
                qf = inner.enter_context(nc.sbuf_tensor(f"qf{b}", [P, TOKENS], F32))
                vf = inner.enter_context(nc.sbuf_tensor(f"vf{b}", [P, TOKENS], F32))
                with nc.sbuf_tensor(f"resized{b}", [P, HALVES, TOKENS], F32) as up:
                    upsample_phase(nc, b, w["high"], up)
                    features_phase(nc, b, x_dram, base_dram, w, gn, up, qf, vf)
                tables_phase(nc, b, w, w["coords"], qf, vf, q_parts, k_parts, v_table, where)
            with nc.sbuf_tensor(f"values{b}", [P, (ROWPAIRS + 1) * P], F32) as val:
                sample_phase(nc, b, w["ramp"], w["id"], q_parts, k_parts, v_table, where, val)
                merge_phase(nc, b, x_dram, base_dram, out_dram, w["wbv"], bn, val)


GROUP = 16
GROUPS = CHUNK // GROUP
TINY = 1e-12
GATE_EPS = 1e-5


def attn_phase(nc, x_dram, out_dram, wq, wk, wv, wo, qb, kb, vb, ob, gate_weight, gate_bias, kv_scale, qk_scale,
               ones_mean, identity, head_rows, head_cols, group_mask, keep, restart):
    H = HALVES
    turns = BATCH * CHUNKS
    blocks = CHUNK // P
    with ExitStack() as ctx:
        def sb(name, shape):
            return ctx.enter_context(nc.sbuf_tensor("at_" + name, shape, F32))

        def psum(name, shape):
            return ctx.enter_context(nc.psum_tensor("at_" + name, shape, F32))

        w_sb = {n: sb("w" + n, [P, H, 256]) for n in "qkvo"}
        bias = {n: sb("b" + n, [P, H]) for n in "qkvo"}
        ones_sb = sb("ones", [P, P])
        ident = sb("ident", [P, P])
        to_rows = sb("to_rows", [P, H, HEADS])
        to_cols = sb("to_cols", [HEADS, H, P])
        mask = sb("mask", [P, 2])
        keep_sb = sb("keep", [P, turns])
        restart_sb = sb("restart", [P, turns])
        s_blk = sb("s_blk", [P, H, P])
        wg_blk = sb("wg_blk", [P, H, P])
        qks = sb("qks", [HEADS, 1])
        wgb = sb("wgb", [HEADS, 1])
        x_sb = sb("x", [P, H, CHUNK])
        cent = sb("cent", [P, H, CHUNK])
        sq = sb("sq", [P, H, CHUNK])
        std = sb("std", [P, CHUNK])
        xn = sb("xn", [P, H, CHUNK])
        Q = sb("q", [P, H, CHUNK])
        K = sb("k", [P, H, CHUNK])
        V = sb("v", [P, H, CHUNK])
        qk = sb("qk", [P, H, CHUNK])
        ksq = sb("ksq", [P, H, CHUNK])
        vsq = sb("vsq", [P, H, CHUNK])
        GK = sb("gk", [P, H, CHUNK])
        gp = sb("gp", [P, H, CHUNK])
        VT = sb("vt", [P, H, blocks, P])
        GT = sb("gt", [P, 2, H, blocks, P])
        pair = sb("pair", [P, 2, GROUPS, GROUP])
        weighed = sb("weighed", [P, 2, GROUPS, GROUP])
        acc = sb("acc", [P, H, GROUPS, GROUP])
        sz = sb("sz", [P, 2, H, P])
        state_sb = sb("state_sb", [P, H * P])
        keep_id = sb("keep_id", [P, P])
        ctxt = sb("ctxt", [P, H, CHUNK])
        proj = sb("proj", [P, H, CHUNK])
        res = sb("res", [P, H, CHUNK])
        sim = sb("sim", [HEADS, CHUNK])
        norms = sb("norms", [HEADS, 2, CHUNK])
        gate = sb("gate", [HEADS, CHUNK])
        most = sb("most", [HEADS, CHUNK + 1])
        expo = sb("expo", [HEADS, 2, CHUNK])
        s_run = sb("s_run", [HEADS, CHUNK])
        g_run = sb("g_run", [HEADS, CHUNK])
        s_car = sb("s_car", [HEADS, 1])
        g_car = sb("g_car", [HEADS, 1])
        ones_row = sb("ones_row", [HEADS, CHUNK])
        wrow = sb("wrow", [HEADS, CHUNK])
        erow = sb("erow", [HEADS, CHUNK])
        crow = sb("crow", [HEADS, CHUNK])
        bank = psum("bank", [P, 3, 512])
        state = psum("state", [P, 512])
        inter = psum("inter", [P, H, 512])
        paired = psum("paired", [P, 2, 512])

        G = GROUPS
        pe_t = Track(ctx, nc, "at_pe",
                     "mean var q0 q1 k0 k1 v0 v1 sim kk vv ks0 ks1 vs0 vs1 wg0 wg1 glog gs0 gs1 seed tv0 tv1 tg0 tg1".split()
                     + [f"{s}{i}" for i in range(G) for s in ("pair", "apply", "grow")] + "c0 c1 o0 o1".split())
        act_t = Track(ctx, nc, "at_act",
                      "square sqrt q0 q1 k0 k1 v0 v1 ksq vsq knorm vnorm grelu gsq vt0 vt1 gt00 gt01 gt10 gt11 exp silu o0 o1".split())
        dve_t = Track(ctx, nc, "at_dve",
                      ("center var_eps rstd norm keep_id sim floor inv kh0 kh1 vh0 vh1 gp0 gp1 gate gk0 gk1 "
                       "most0 s_car g_car most fall rise s_run g_run s_eps s_inv w e1 e_inv sw g_eps g_inv c").split()
                      + [f"{s}{i}" for i in range(G) for s in ("sz", "weigh", "add") if s != "add" or i % GROUP] + "keep_state inter ctxt0 ctxt1 res".split())
        pool_t = Track(ctx, nc, "at_pool", ["qk"] + [f"pair{i}" for i in range(G)])
        stored_t = Track(ctx, nc, "at_res_stored", ["stored"])
        ready = ctx.enter_context(nc.semaphore("at_constants"))
        zeroed = ctx.enter_context(nc.semaphore("at_zeroed"))
        scaled = ctx.enter_context(nc.semaphore("at_gate_weight"))
        loads = Loads(ctx, nc, "at_x_loaded")
        stores = Loads(ctx, nc, "at_stored")
        consts = [(w_sb["q"], wq), (w_sb["k"], wk), (w_sb["v"], wv), (w_sb["o"], wo), (bias["q"], qb), (bias["k"], kb),
                  (bias["v"], vb), (bias["o"], ob), (ones_sb, ones_mean), (ident, identity), (to_rows, head_rows),
                  (to_cols, head_cols), (mask, group_mask), (keep_sb, keep), (restart_sb, restart), (qks, qk_scale),
                  (wgb, gate_bias)]
        n_consts = len(consts) + 2 * HEADS
        block = ctx.enter_context(nc.Block())

        @block.sync
        def _(sp):
            sp.wait_ge(zeroed, 6)
            for dst, src in consts:
                sp.dma_start(dst[:], src).then_inc(ready, 16)
            for h in range(HEADS):
                r = slice(32 * (h % 4), 32 * (h % 4) + 32)
                sp.dma_start(s_blk[r, h // 4, r], kv_scale[h]).then_inc(ready, 16)
                sp.dma_start(wg_blk[r, h // 4, r], gate_weight).then_inc(ready, 16)
            with sp.Fori(0, turns) as t:
                sp.wait_ge(dve_t.sem, dve_t.last_turn(t, "res"))
                sp.dma_start(x_sb[:], chunk_of(x_dram, t)).then_inc(loads.sem, 16)

        @block.gpsimd
        def _(pool):
            stored_t.credit(pool)
            pool_t.credit(pool)
            with pool.Fori(0, turns) as t:
                pool.wait_ge(act_t.sem, act_t.upto(t, "k1"))
                pool.wait_ge(pool_t.sem, pool_t.so_far(t))
                nc.gpsimd.tensor_tensor(qk[:], Q[:], K[:], ALU.mult).then_inc(pool_t.done("qk"), 1)
                pool.wait_ge(dve_t.sem, dve_t.upto(t, "vh1"))
                for i in range(G):
                    h, far = i // GROUP, i % GROUP
                    if i >= 2:
                        pool.wait_ge(pe_t.sem, pe_t.upto(t, f"pair{i - 2}"))
                    q_part = Q[:, h].rearrange("p (g n) -> p g n", n=GROUP)[:, :, far:]
                    v_part = V[:, h].rearrange("p (g n) -> p g n", n=GROUP)[:, :, 0:GROUP - far]
                    nc.gpsimd.tensor_tensor(pair[:, i % 2, :, 0:GROUP - far], q_part, v_part, ALU.mult).then_inc(pool_t.done(f"pair{i}"), 1)
                pool.wait_ge(dve_t.sem, dve_t.upto(t, "res"))
                pool.dma_start(chunk_of(out_dram, t), res[:]).then_inc(stores.sem, 16)
                pool.wait_ge(stores.sem, stores.upto(t))
                pool.sem_inc(stored_t.done("stored"), 1)

        @block.tensor
        def _(pe):
            pe_t.credit(pe)
            pe.wait_ge(ready, 16 * n_consts)
            pe.wait_ge(scaled, 1)

            def both(dst, lhs, rhs, step):
                for k in range(H):
                    mm = nc.tensor.matmul(dst, lhs[k], rhs[k], start=(k == 0), stop=(k == H - 1))
                mm.then_inc(pe_t.done(step), 1)

            with pe.Fori(0, turns) as t:
                pe.wait_ge(loads.sem, loads.upto(t))
                ones2 = [ones_sb[:]] * 2
                both(bank[:, 0], ones2, [x_sb[:, 0], x_sb[:, 1]], "mean")
                pe.wait_ge(act_t.sem, act_t.upto(t, "square"))
                both(bank[:, 1], ones2, [sq[:, 0], sq[:, 1]], "var")
                pe.wait_ge(dve_t.sem, dve_t.upto(t, "norm"))
                for i, (n, h) in enumerate((n, h) for n in "qkv" for h in range(H)):
                    if i >= 3:
                        pe.wait_ge(act_t.sem, act_t.upto(t, ("q0", "q1", "k0")[i - 3]))
                    both(bank[:, i % 3], [w_sb[n][:, k, h * P:(h + 1) * P] for k in range(H)], [xn[:, 0], xn[:, 1]], f"{n}{h}")
                rows = [to_rows[:, 0], to_rows[:, 1]]
                pe.wait_ge(act_t.sem, act_t.upto(t, "vsq"))
                pe.wait_ge(pool_t.sem, pool_t.upto(t, "qk"))
                both(bank[0:HEADS, 0], rows, [qk[:, 0], qk[:, 1]], "sim")
                both(bank[0:HEADS, 1], rows, [ksq[:, 0], ksq[:, 1]], "kk")
                both(bank[0:HEADS, 2], rows, [vsq[:, 0], vsq[:, 1]], "vv")
                pe.wait_ge(dve_t.sem, dve_t.upto(t, "inv"))
                nc.tensor.matmul(bank[:, 0], to_cols[:, 0], norms[:, 0], start=True, stop=True).then_inc(pe_t.done("ks0"), 1)
                nc.tensor.matmul(bank[:, 1], to_cols[:, 1], norms[:, 0], start=True, stop=True).then_inc(pe_t.done("ks1"), 1)
                nc.tensor.matmul(bank[:, 2], to_cols[:, 0], norms[:, 1], start=True, stop=True).then_inc(pe_t.done("vs0"), 1)
                pe.wait_ge(dve_t.sem, dve_t.upto(t, "kh0"))
                nc.tensor.matmul(bank[:, 0], to_cols[:, 1], norms[:, 1], start=True, stop=True).then_inc(pe_t.done("vs1"), 1)
                pe.wait_ge(dve_t.sem, dve_t.upto(t, "vh1"))
                nc.tensor.matmul(bank[:, 1], wg_blk[:, 0], V[:, 0], start=True, stop=True).then_inc(pe_t.done("wg0"), 1)
                nc.tensor.matmul(bank[:, 2], wg_blk[:, 1], V[:, 1], start=True, stop=True).then_inc(pe_t.done("wg1"), 1)
                pe.wait_ge(dve_t.sem, dve_t.upto(t, "gp1"))
                both(bank[0:HEADS, 0], rows, [gp[:, 0], gp[:, 1]], "glog")
                pe.wait_ge(dve_t.sem, dve_t.upto(t, "gate"))
                nc.tensor.matmul(bank[:, 1], to_cols[:, 0], gate[:], start=True, stop=True).then_inc(pe_t.done("gs0"), 1)
                nc.tensor.matmul(bank[:, 2], to_cols[:, 1], gate[:], start=True, stop=True).then_inc(pe_t.done("gs1"), 1)
                nc.tensor.matmul(state[:, 0:H * P], keep_id[:], state_sb[:], start=True, stop=False,
                                 skip_group_check=True).then_inc(pe_t.done("seed"), 1)
                for h in range(H):
                    if h == 1:
                        pe.wait_ge(dve_t.sem, dve_t.upto(t, "gk0"))
                    for b in range(blocks):
                        mm = nc.tensor.transpose(bank[:, h, b * P:(b + 1) * P], V[:, h, b * P:(b + 1) * P], ident[:])
                    mm.then_inc(pe_t.done(f"tv{h}"), 1)
                for h in range(H):
                    if h == 0:
                        pe.wait_ge(dve_t.sem, dve_t.upto(t, "gk1"))
                    else:
                        pe.wait_ge(act_t.sem, act_t.upto(t, "vt0"))
                    for b in range(blocks):
                        mm = nc.tensor.transpose(bank[:, 2 if h == 0 else 0, b * P:(b + 1) * P], GK[:, h, b * P:(b + 1) * P], ident[:])
                    mm.then_inc(pe_t.done(f"tg{h}"), 1)
                pe.wait_ge(act_t.sem, act_t.upto(t, "gt11"))
                for i in range(G):
                    h, far = i // GROUP, i % GROUP
                    b, r, m = i // 8, slice(32 * (i % 8 // 2), 32 * (i % 8 // 2) + 32), i % 2
                    pe.wait_ge(pool_t.sem, pool_t.upto(t, f"pair{i}"))
                    if i >= 2:
                        pe.wait_ge(dve_t.sem, dve_t.upto(t, f"weigh{i - 2}"))
                    nc.tensor.matmul(paired[:, i % 2, 0:G * (GROUP - far)], s_blk[:, h], pair[:, i % 2, :, 0:GROUP - far],
                                     start=True, stop=True).then_inc(pe_t.done(f"pair{i}"), 1)
                    pe.wait_ge(dve_t.sem, dve_t.upto(t, f"sz{i}"))
                    for k in range(H):
                        mm = nc.tensor.matmul(inter[:, k, i * GROUP:(i + 1) * GROUP], sz[:, i % 2, k],
                                              Q[:, k, i * GROUP:(i + 1) * GROUP], start=True, stop=True)
                    mm.then_inc(pe_t.done(f"apply{i}"), 1)
                    for k in range(H):
                        mm = nc.tensor.matmul(state[:, k * P:(k + 1) * P], VT[r, k, b, :], GT[r, m, k, b, :],
                                              start=False, stop=False, skip_group_check=True)
                    mm.then_inc(pe_t.done(f"grow{i}"), 1)
                nc.tensor.matmul(bank[:, 0], to_cols[:, 0], crow[:], start=True, stop=True).then_inc(pe_t.done("c0"), 1)
                nc.tensor.matmul(bank[:, 1], to_cols[:, 1], crow[:], start=True, stop=True).then_inc(pe_t.done("c1"), 1)
                pe.wait_ge(dve_t.sem, dve_t.upto(t, "ctxt1"))
                for h in range(H):
                    both(bank[:, 2 if h == 0 else 0], [w_sb["o"][:, k, h * P:(h + 1) * P] for k in range(H)], [ctxt[:, 0], ctxt[:, 1]], f"o{h}")

        @block.scalar
        def _(act):
            act_t.credit(act)
            act.wait_ge(ready, 16 * n_consts)
            with act.Fori(0, turns) as t:
                def own():
                    act.wait_ge(act_t.sem, act_t.so_far(t))
                act.wait_ge(dve_t.sem, dve_t.upto(t, "center"))
                nc.scalar.activation(sq[:], cent[:], ACT.Square).then_inc(act_t.done("square"), 1)
                act.wait_ge(dve_t.sem, dve_t.upto(t, "var_eps"))
                nc.scalar.activation(std[:], std[:], ACT.Sqrt).then_inc(act_t.done("sqrt"), 1)
                for i, (n, dst, h) in enumerate((n, dst, h) for n, dst in (("q", Q), ("k", K), ("v", V)) for h in range(H)):
                    act.wait_ge(pe_t.sem, pe_t.upto(t, f"{n}{h}"))
                    nc.scalar.activation(dst[:, h], bank[:, i % 3], ACT.Identity, bias=bias[n][:, h:h + 1]).then_inc(act_t.done(f"{n}{h}"), 1)
                own()
                nc.scalar.activation(ksq[:], K[:], ACT.Square).then_inc(act_t.done("ksq"), 1)
                nc.scalar.activation(vsq[:], V[:], ACT.Square).then_inc(act_t.done("vsq"), 1)
                act.wait_ge(pe_t.sem, pe_t.upto(t, "vv"))
                nc.scalar.activation(norms[:, 0], bank[0:HEADS, 1], ACT.Sqrt).then_inc(act_t.done("knorm"), 1)
                nc.scalar.activation(norms[:, 1], bank[0:HEADS, 2], ACT.Sqrt).then_inc(act_t.done("vnorm"), 1)
                act.wait_ge(pe_t.sem, pe_t.upto(t, "glog"))
                nc.scalar.activation(gate[:], bank[0:HEADS, 0], ACT.Relu, bias=wgb[:]).then_inc(act_t.done("grelu"), 1)
                own()
                nc.scalar.activation(gate[:], gate[:], ACT.Square).then_inc(act_t.done("gsq"), 1)
                for h in range(H):
                    act.wait_ge(pe_t.sem, pe_t.upto(t, f"tv{h}"))
                    nc.scalar.copy(VT[:, h], bank[:, h].rearrange("p (b c) -> p b c", c=P)).then_inc(act_t.done(f"vt{h}"), 1)
                for h in range(H):
                    act.wait_ge(pe_t.sem, pe_t.upto(t, f"tg{h}"))
                    for m in range(2):
                        nc.scalar.activation(GT[:, m, h], bank[:, 2 if h == 0 else 0].rearrange("p (b c) -> p b c", c=P), ACT.Copy,
                                             scale=mask[:, m:m + 1]).then_inc(act_t.done(f"gt{h}{m}"), 1)
                act.wait_ge(dve_t.sem, dve_t.upto(t, "rise"))
                nc.scalar.activation(expo[:], expo[:], ACT.Exp).then_inc(act_t.done("exp"), 1)
                act.wait_ge(dve_t.sem, dve_t.upto(t, "w"))
                nc.scalar.activation(erow[:], wrow[:], ACT.Exp, scale=-1.0).then_inc(act_t.done("silu"), 1)
                for h in range(H):
                    act.wait_ge(pe_t.sem, pe_t.upto(t, f"o{h}"))
                    nc.scalar.activation(proj[:, h], bank[:, 2 if h == 0 else 0], ACT.Identity, bias=bias["o"][:, h:h + 1]).then_inc(act_t.done(f"o{h}"), 1)

        @block.vector
        def _(v):
            dve_t.credit(v)
            for z in (s_blk, wg_blk, state_sb, most, s_run, g_run):
                nc.vector.memset(z[:], 0.0).then_inc(zeroed, 1)
            nc.vector.memset(ones_row[:], 1.0).then_inc(zeroed, 1)
            v.wait_ge(ready, 16 * n_consts)
            nc.vector.tensor_tensor(wg_blk[:], wg_blk[:], s_blk[:], ALU.mult).then_inc(scaled, 1)
            v.wait_ge(scaled, 1)
            v.wait_ge(zeroed, 7)
            with v.Fori(0, turns) as t:
                def step(name, ins):
                    ins.then_inc(dve_t.done(name), 1)

                def own():
                    v.wait_ge(dve_t.sem, dve_t.so_far(t))

                v.wait_ge(pe_t.sem, pe_t.upto(t, "mean"))
                own()
                nc.vector.tensor_tensor(cent[:], x_sb[:], bank[:, 0].unsqueeze(1).to_broadcast([P, H, CHUNK]),
                                        ALU.subtract).then_inc(dve_t.done("center"), 1)
                v.wait_ge(pe_t.sem, pe_t.upto(t, "var"))
                own()
                nc.vector.tensor_scalar_add(std[:], bank[:, 1], LN_EPS).then_inc(dve_t.done("var_eps"), 1)
                v.wait_ge(act_t.sem, act_t.upto(t, "sqrt"))
                own()
                nc.vector.reciprocal(std[:], std[:]).then_inc(dve_t.done("rstd"), 1)
                own()
                nc.vector.tensor_tensor(xn[:], cent[:], std[:].unsqueeze(1).to_broadcast([P, H, CHUNK]),
                                        ALU.mult).then_inc(dve_t.done("norm"), 1)
                nc.vector.tensor_scalar(keep_id[:], ident[:], keep_sb[:, bass.ds(t, 1)], None, ALU.mult).then_inc(dve_t.done("keep_id"), 1)
                v.wait_ge(pe_t.sem, pe_t.upto(t, "sim"))
                nc.vector.tensor_scalar(sim[:], bank[0:HEADS, 0], qks[:], None, ALU.mult).then_inc(dve_t.done("sim"), 1)
                v.wait_ge(act_t.sem, act_t.upto(t, "vnorm"))
                nc.vector.tensor_scalar_max(norms[:], norms[:], TINY).then_inc(dve_t.done("floor"), 1)
                own()
                nc.vector.reciprocal(norms[:], norms[:]).then_inc(dve_t.done("inv"), 1)
                for h in range(H):
                    v.wait_ge(pe_t.sem, pe_t.upto(t, f"ks{h}"))
                    nc.vector.tensor_tensor(K[:, h], K[:, h], bank[:, h], ALU.mult).then_inc(dve_t.done(f"kh{h}"), 1)
                for h in range(H):
                    v.wait_ge(pe_t.sem, pe_t.upto(t, f"vs{h}"))
                    nc.vector.tensor_tensor(V[:, h], V[:, h], bank[:, 2 if h == 0 else 0], ALU.mult).then_inc(dve_t.done(f"vh{h}"), 1)
                own()
                for h in range(H):
                    v.wait_ge(pe_t.sem, pe_t.upto(t, f"wg{h}"))
                    nc.vector.tensor_tensor(gp[:, h], K[:, h], bank[:, 1 + h], ALU.mult).then_inc(dve_t.done(f"gp{h}"), 1)
                v.wait_ge(act_t.sem, act_t.upto(t, "gsq"))
                nc.vector.tensor_scalar_add(gate[:], gate[:], GATE_EPS).then_inc(dve_t.done("gate"), 1)
                for h in range(H):
                    v.wait_ge(pe_t.sem, pe_t.upto(t, f"gs{h}"))
                    nc.vector.tensor_tensor(GK[:, h], K[:, h], bank[:, 1 + h], ALU.mult).then_inc(dve_t.done(f"gk{h}"), 1)
                kt, rt = keep_sb[0:HEADS, bass.ds(t, 1)], restart_sb[0:HEADS, bass.ds(t, 1)]
                nc.vector.tensor_scalar(most[:, 0:1], most[:, CHUNK:CHUNK + 1], kt, rt, ALU.mult, ALU.add).then_inc(dve_t.done("most0"), 1)
                nc.vector.tensor_scalar(s_car[:], s_run[:, CHUNK - 1:CHUNK], kt, None, ALU.mult).then_inc(dve_t.done("s_car"), 1)
                nc.vector.tensor_scalar(g_car[:], g_run[:, CHUNK - 1:CHUNK], kt, None, ALU.mult).then_inc(dve_t.done("g_car"), 1)
                own()
                nc.vector.tensor_tensor_scan(most[:, 1:], sim[:], sim[:], most[:, 0:1], ALU.max, ALU.max).then_inc(dve_t.done("most"), 1)
                own()
                nc.vector.tensor_tensor(expo[:, 0], most[:, 0:CHUNK], most[:, 1:], ALU.subtract).then_inc(dve_t.done("fall"), 1)
                nc.vector.tensor_tensor(expo[:, 1], sim[:], most[:, 1:], ALU.subtract).then_inc(dve_t.done("rise"), 1)
                v.wait_ge(act_t.sem, act_t.upto(t, "exp"))
                nc.vector.tensor_tensor_scan(s_run[:], expo[:, 0], expo[:, 1], s_car[:], ALU.mult, ALU.add).then_inc(dve_t.done("s_run"), 1)
                nc.vector.tensor_tensor_scan(g_run[:], ones_row[:], gate[:], g_car[:], ALU.mult, ALU.add).then_inc(dve_t.done("g_run"), 1)
                own()
                nc.vector.tensor_scalar_add(wrow[:], s_run[:], GATE_EPS).then_inc(dve_t.done("s_eps"), 1)
                own()
                nc.vector.reciprocal(wrow[:], wrow[:]).then_inc(dve_t.done("s_inv"), 1)
                own()
                nc.vector.tensor_tensor(wrow[:], expo[:, 1], wrow[:], ALU.mult).then_inc(dve_t.done("w"), 1)
                v.wait_ge(act_t.sem, act_t.upto(t, "silu"))
                nc.vector.tensor_scalar_add(erow[:], erow[:], 1.0).then_inc(dve_t.done("e1"), 1)
                own()
                nc.vector.reciprocal(erow[:], erow[:]).then_inc(dve_t.done("e_inv"), 1)
                own()
                nc.vector.tensor_tensor(wrow[:], wrow[:], erow[:], ALU.mult).then_inc(dve_t.done("sw"), 1)
                nc.vector.tensor_scalar_add(crow[:], g_run[:], GATE_EPS).then_inc(dve_t.done("g_eps"), 1)
                own()
                nc.vector.reciprocal(crow[:], crow[:]).then_inc(dve_t.done("g_inv"), 1)
                own()
                nc.vector.scalar_tensor_tensor(crow[:], wrow[:], 1.0, crow[:], ALU.add, ALU.mult).then_inc(dve_t.done("c"), 1)
                v.wait_ge(pe_t.sem, pe_t.upto(t, "seed"))
                for i in range(G):
                    h, far = i // GROUP, i % GROUP
                    if i:
                        v.wait_ge(pe_t.sem, pe_t.upto(t, f"grow{i - 1}"))
                    own()
                    nc.vector.tensor_tensor(sz[:, i % 2].rearrange("p h e -> p (h e)"), state[:, 0:H * P],
                                            s_blk[:].rearrange("p h e -> p (h e)"), ALU.mult).then_inc(dve_t.done(f"sz{i}"), 1)
                    v.wait_ge(pe_t.sem, pe_t.upto(t, f"pair{i}"))
                    gk_part = GK[:, h].rearrange("p (g n) -> p g n", n=GROUP)[:, :, 0:GROUP - far]
                    dst = acc[:, h] if far == 0 else weighed[:, i % 2, :, 0:GROUP - far]
                    nc.vector.tensor_tensor(dst, gk_part, paired[:, i % 2, 0:G * (GROUP - far)].rearrange("p (g n) -> p g n", g=G),
                                            ALU.mult).then_inc(dve_t.done(f"weigh{i}"), 1)
                    if far:
                        own()
                        nc.vector.tensor_tensor(acc[:, h, :, far:], acc[:, h, :, far:], dst, ALU.add).then_inc(dve_t.done(f"add{i}"), 1)
                v.wait_ge(pe_t.sem, pe_t.upto(t, f"grow{G - 1}"))
                own()
                nc.vector.tensor_copy(state_sb[:], state[:, 0:H * P]).then_inc(dve_t.done("keep_state"), 1)
                flat = acc[:].rearrange("p h g n -> p h (g n)")
                nc.vector.tensor_tensor(flat, flat, inter[:], ALU.add).then_inc(dve_t.done("inter"), 1)
                v.wait_ge(pe_t.sem, pe_t.upto(t, "c1"))
                own()
                for h in range(H):
                    nc.vector.tensor_tensor(ctxt[:, h], flat[:, h], bank[:, h], ALU.mult).then_inc(dve_t.done(f"ctxt{h}"), 1)
                v.wait_ge(act_t.sem, act_t.upto(t, "o1"))
                v.wait_ge(stored_t.sem, stored_t.last_turn(t, "stored"))
                own()
                nc.vector.tensor_tensor(res[:], proj[:], x_sb[:], ALU.add).then_inc(dve_t.done("res"), 1)
        return


def ffn_phase(nc, x_dram, out_dram, gate_w, gate_b, w1, b1, w2, b2, ones_mean, identity):
    E, M, H = EXPERTS, 4, HALVES
    blocks = CHUNK // P
    turns = BATCH * CHUNKS
    with ExitStack() as ctx:
        def sb(name, shape):
            return ctx.enter_context(nc.sbuf_tensor("ffn_" + name, shape, F32))

        def psum(name, shape):
            return ctx.enter_context(nc.psum_tensor("ffn_" + name, shape, F32))

        w1_sb = sb("w1", [P, E, H, 512])
        w2_sb = sb("w2", [P, E, M, 256])
        b1_sb = sb("b1", [P, E, M])
        b2_sb = sb("b2", [E, 256])
        gw_sb = sb("gw", [P, H, E])
        gb_sb = sb("gb", [P, E])
        ones_sb = sb("ones", [P, P])
        ident = sb("ident", [P, P])
        pick = sb("pick", [E, E, P])
        x_sb = sb("x", [P, H, CHUNK])
        cent = sb("cent", [P, H, CHUNK])
        sq = sb("sq", [P, H, CHUNK])
        std = sb("std", [P, CHUNK])
        xn = sb("xn", [P, H, CHUNK])
        logit = sb("logit", [P, blocks, E])
        top = sb("top", [P, blocks])
        total = sb("total", [P, blocks])
        probs = sb("probs", [P, blocks, 2 * E])
        sorted8 = sb("sorted8", [P, blocks, E])
        first2 = sb("first2", [P, blocks, E])
        marked = sb("marked", [P, blocks, 2 * E])
        cw = sb("cw", [P, blocks, E])
        cw_rows = sb("cw_rows", [E, CHUNK])
        act_out = sb("act_out", [P, 2, M, CHUNK])
        scaled = sb("scaled", [P, 2, M, CHUNK])
        res = sb("res", [P, H, CHUNK])
        small = psum("small", [P, 512])
        spread = psum("spread", [P, 512])
        hid = psum("hid", [P, M, 512])
        y = psum("y", [P, H, 512])

        pe_order = ["mean", "var", "router", "cw_rows", "cwb0"] + [f"h0_{m}" for m in range(M)]
        act_order = ["square", "sqrt", "exp", "cw_rows"]
        dve_order = ["center", "var_eps", "rstd", "norm", "logit", "top", "shift", "total", "inv", "prob"]
        dve_order += [f"sort{b}" for b in range(blocks)] + ["first2"] + [f"mark{b}" for b in range(blocks)]
        dve_order += ["chosen", "cw"]
        for e in range(E):
            act_order += [f"gelu{e}_{m}" for m in range(M)]
            dve_order += [f"scale{e}_{m}" for m in range(M)]
            if e + 1 < E:
                pe_order += [f"h{e + 1}_{m}" for m in range(M)]
            pe_order += [f"y{e}"]
            if e + 1 < E:
                pe_order += [f"cwb{e + 1}"]
        dve_order += ["res"]
        pe_t = Track(ctx, nc, "ffn_pe", pe_order)
        act_t = Track(ctx, nc, "ffn_act", act_order)
        dve_t = Track(ctx, nc, "ffn_dve", dve_order)
        stored_t = Track(ctx, nc, "ffn_res_stored", ["stored"])
        ready = ctx.enter_context(nc.semaphore("ffn_constants"))
        filled = ctx.enter_context(nc.semaphore("ffn_filled"))
        sentinels = ctx.enter_context(nc.semaphore("ffn_sentinels"))
        passed = ctx.enter_context(nc.semaphore("ffn_passed"))
        loads = Loads(ctx, nc, "ffn_x_loaded")
        stores = Loads(ctx, nc, "ffn_stored")
        consts = [(w1_sb, w1), (w2_sb, w2), (b1_sb, b1), (b2_sb, b2), (gw_sb, gate_w), (gb_sb, gate_b),
                  (ones_sb, ones_mean), (ident, identity)]
        block = ctx.enter_context(nc.Block())

        @block.sync
        def _(sp):
            for dst, src in consts:
                sp.dma_start(dst[:], src).then_inc(ready, 16)
            with sp.Fori(0, turns) as t:
                sp.wait_ge(dve_t.sem, dve_t.last_turn(t, "res"))
                sp.dma_start(x_sb[:], chunk_of(x_dram, t)).then_inc(loads.sem, 16)

        @block.gpsimd
        def _(pool):
            stored_t.credit(pool)
            pool.wait_ge(ready, 16 * len(consts))
            nc.gpsimd.tensor_copy(pick[:], ident[0:E, 0:E].unsqueeze(2).to_broadcast([E, E, P])).then_inc(filled, 1)
            with pool.Fori(0, turns) as t:
                pool.wait_ge(dve_t.sem, dve_t.upto(t, "res"))
                pool.dma_start(chunk_of(out_dram, t), res[:]).then_inc(stores.sem, 16)
                pool.wait_ge(stores.sem, stores.upto(t))
                pool.sem_inc(stored_t.done("stored"), 1)

        @block.tensor
        def _(pe):
            pe_t.credit(pe)
            pe.wait_ge(ready, 16 * len(consts))
            pe.wait_ge(filled, 1)

            def hidden(t, e):
                for m in range(M):
                    pe.wait_ge(act_t.sem, act_t.upto(t, f"gelu{e - 1}_{m}") if e else act_t.last_turn(t, f"gelu{E - 1}_{m}"))
                    for k in range(H):
                        mm = nc.tensor.matmul(hid[:, m], w1_sb[:, e, k, m * P:(m + 1) * P], xn[:, k],
                                              start=(k == 0), stop=(k == H - 1))
                    mm.then_inc(pe_t.done(f"h{e}_{m}"), 1)

            def spread_weight(t, e):
                pe.wait_ge(dve_t.sem, dve_t.upto(t, f"scale{e - 1}_{M - 1}") if e else dve_t.last_turn(t, f"scale{E - 1}_{M - 1}"))
                nc.tensor.matmul(spread[:], pick[:, e], cw_rows[:], start=True, stop=True).then_inc(pe_t.done(f"cwb{e}"), 1)

            with pe.Fori(0, turns) as t:
                pe.wait_ge(loads.sem, loads.upto(t))
                for k in range(H):
                    mm = nc.tensor.matmul(small[:], ones_sb[:], x_sb[:, k], start=(k == 0), stop=(k == H - 1))
                mm.then_inc(pe_t.done("mean"), 1)
                pe.wait_ge(act_t.sem, act_t.upto(t, "square"))
                for k in range(H):
                    mm = nc.tensor.matmul(small[:], ones_sb[:], sq[:, k], start=(k == 0), stop=(k == H - 1))
                mm.then_inc(pe_t.done("var"), 1)
                pe.wait_ge(dve_t.sem, dve_t.upto(t, "norm"))
                for b in range(blocks):
                    for k in range(H):
                        mm = nc.tensor.matmul(small[:, b * E:(b + 1) * E], xn[:, k, b * P:(b + 1) * P], gw_sb[:, k],
                                              start=(k == 0), stop=(k == H - 1))
                mm.then_inc(pe_t.done("router"), 1)
                pe.wait_ge(dve_t.sem, dve_t.upto(t, "cw"))
                for b in range(blocks):
                    mm = nc.tensor.transpose(small[0:E, b * P:(b + 1) * P], cw[:, b], ident[:])
                mm.then_inc(pe_t.done("cw_rows"), 1)
                pe.wait_ge(act_t.sem, act_t.upto(t, "cw_rows"))
                spread_weight(t, 0)
                hidden(t, 0)
                for e in range(E):
                    if e + 1 < E:
                        hidden(t, e + 1)
                    for m in range(M):
                        pe.wait_ge(dve_t.sem, dve_t.upto(t, f"scale{e}_{m}"))
                        for d in range(H):
                            mm = nc.tensor.matmul(y[:, d], w2_sb[:, e, m, d * P:(d + 1) * P], scaled[:, e % 2, m],
                                                  start=(e == 0 and m == 0), stop=False, skip_group_check=True)
                    if e == E - 1:
                        for d in range(H):
                            mm = nc.tensor.matmul(y[:, d], b2_sb[:, d * P:(d + 1) * P], cw_rows[:],
                                                  start=False, stop=True, skip_group_check=True)
                    mm.then_inc(pe_t.done(f"y{e}"), 1)
                    if e + 1 < E:
                        spread_weight(t, e + 1)

        @block.scalar
        def _(act):
            act_t.credit(act)
            act.wait_ge(ready, 16 * len(consts))
            with act.Fori(0, turns) as t:
                act.wait_ge(dve_t.sem, dve_t.upto(t, "center"))
                nc.scalar.activation(sq[:], cent[:], ACT.Square).then_inc(act_t.done("square"), 1)
                act.wait_ge(dve_t.sem, dve_t.upto(t, "var_eps"))
                nc.scalar.activation(std[:], std[:], ACT.Sqrt).then_inc(act_t.done("sqrt"), 1)
                act.wait_ge(dve_t.sem, dve_t.upto(t, "shift"))
                nc.scalar.activation(logit[:], logit[:], ACT.Exp).then_inc(act_t.done("exp"), 1)
                act.wait_ge(pe_t.sem, pe_t.upto(t, "cw_rows"))
                nc.scalar.copy(cw_rows[:], small[0:E]).then_inc(act_t.done("cw_rows"), 1)
                for e in range(E):
                    for m in range(M):
                        act.wait_ge(pe_t.sem, pe_t.upto(t, f"h{e}_{m}"))
                        if e >= 2:
                            act.wait_ge(dve_t.sem, dve_t.upto(t, f"scale{e - 2}_{m}"))
                        nc.scalar.activation(act_out[:, e % 2, m], hid[:, m], ACT.Gelu,
                                             bias=b1_sb[:, e, m:m + 1]).then_inc(act_t.done(f"gelu{e}_{m}"), 1)

        @block.vector
        def _(v):
            dve_t.credit(v)
            nc.vector.memset(probs[:], -1.0).then_inc(sentinels, 1)
            nc.vector.memset(first2[:], -1.0).then_inc(sentinels, 1)
            v.wait_ge(sentinels, 2)
            v.wait_ge(ready, 16 * len(consts))
            with v.Fori(0, turns) as t:
                def own():
                    v.wait_ge(dve_t.sem, dve_t.so_far(t))
                v.wait_ge(pe_t.sem, pe_t.upto(t, "mean"))
                own()
                nc.vector.tensor_tensor(cent[:], x_sb[:], small[:].unsqueeze(1).to_broadcast([P, H, CHUNK]),
                                        ALU.subtract).then_inc(dve_t.done("center"), 1)
                v.wait_ge(pe_t.sem, pe_t.upto(t, "var"))
                own()
                nc.vector.tensor_scalar_add(std[:], small[:], LN_EPS).then_inc(dve_t.done("var_eps"), 1)
                v.wait_ge(act_t.sem, act_t.upto(t, "sqrt"))
                own()
                nc.vector.reciprocal(std[:], std[:]).then_inc(dve_t.done("rstd"), 1)
                own()
                nc.vector.tensor_tensor(xn[:], cent[:], std[:].unsqueeze(1).to_broadcast([P, H, CHUNK]),
                                        ALU.mult).then_inc(dve_t.done("norm"), 1)
                v.wait_ge(pe_t.sem, pe_t.upto(t, "router"))
                own()
                nc.vector.tensor_tensor(logit[:], small[:, 0:blocks * E].rearrange("p (b e) -> p b e", e=E),
                                        gb_sb[:].unsqueeze(1).to_broadcast([P, blocks, E]), ALU.add).then_inc(dve_t.done("logit"), 1)
                own()
                nc.vector.tensor_reduce(top[:], logit[:], AX.X, ALU.max).then_inc(dve_t.done("top"), 1)
                own()
                nc.vector.tensor_tensor(logit[:], logit[:], top[:].unsqueeze(2).to_broadcast([P, blocks, E]),
                                        ALU.subtract).then_inc(dve_t.done("shift"), 1)
                v.wait_ge(act_t.sem, act_t.upto(t, "exp"))
                own()
                nc.vector.tensor_reduce(total[:], logit[:], AX.X, ALU.add).then_inc(dve_t.done("total"), 1)
                own()
                nc.vector.reciprocal(total[:], total[:]).then_inc(dve_t.done("inv"), 1)
                own()
                nc.vector.tensor_tensor(probs[:, :, 0:E], logit[:], total[:].unsqueeze(2).to_broadcast([P, blocks, E]),
                                        ALU.mult).then_inc(dve_t.done("prob"), 1)
                own()
                v.sem_inc(passed, 1)
                for b in range(blocks):
                    nc.vector.max(sorted8[:, b], probs[:, b, 0:E]).then_inc(dve_t.done(f"sort{b}"), 1)
                own()
                nc.vector.tensor_copy(first2[:, :, 0:2], sorted8[:, :, 0:2]).then_inc(dve_t.done("first2"), 1)
                own()
                v.sem_inc(passed, 1)
                for b in range(blocks):
                    nc.vector.match_replace(marked[:, b], first2[:, b], probs[:, b], -2.0).then_inc(dve_t.done(f"mark{b}"), 1)
                own()
                nc.vector.tensor_tensor(marked[:, :, 0:E], marked[:, :, 0:E], probs[:, :, 0:E],
                                        ALU.not_equal).then_inc(dve_t.done("chosen"), 1)
                own()
                nc.vector.tensor_tensor(cw[:], marked[:, :, 0:E], probs[:, :, 0:E], ALU.mult).then_inc(dve_t.done("cw"), 1)
                for e in range(E):
                    v.wait_ge(pe_t.sem, pe_t.upto(t, f"cwb{e}"))
                    for m in range(M):
                        v.wait_ge(act_t.sem, act_t.upto(t, f"gelu{e}_{m}"))
                        if e >= 2 and m == 0:
                            v.wait_ge(pe_t.sem, pe_t.upto(t, f"y{e - 2}"))
                        nc.vector.tensor_tensor(scaled[:, e % 2, m], act_out[:, e % 2, m], spread[:],
                                                ALU.mult).then_inc(dve_t.done(f"scale{e}_{m}"), 1)
                v.wait_ge(pe_t.sem, pe_t.upto(t, f"y{E - 1}"))
                v.wait_ge(stored_t.sem, stored_t.last_turn(t, "stored"))
                own()
                nc.vector.tensor_tensor(res[:], y[:], x_sb[:], ALU.add).then_inc(dve_t.done("res"), 1)
        return


def conv_arrays(i, pre=""):
    g = lambda n: i[pre + n]
    blocks = lambda m, k: m.T.reshape(k, P, m.shape[0]).transpose(1, 0, 2)
    halves = lambda v: v.reshape(HALVES, P).T
    lane, t, a = np.meshgrid(np.arange(P) // POINTS, np.arange(ROWPAIRS), np.arange(CELLS), indexing="ij")
    coords = np.stack([lane // 2 * CELLS + a, 2 * t + lane % 2], 1).reshape(P, 2, -1).astype(np.float32)
    parts = np.array([(0, 0), (0, 1), (1, 0), (1, 1), (0, 2), (2, 0), (1, 2), (2, 1)])
    minus = -np.repeat(np.stack([parts >= 1, parts >= 2], 2), QC, 0).astype(np.float32)
    return {
        "high": g("high_feature").reshape(BATCH, HALVES, P, 1024).transpose(0, 2, 1, 3),
        "w1": blocks(g("W1"), 4), "w2": blocks(g("W2"), 2), "b1": g("b1").reshape(P, 1), "b2": g("b2").reshape(P, 1),
        "wq": np.tile(g("Wq").T, (1, 8)), "wk": np.tile(g("Wk").T, (1, 8)), "wv": g("Wv").T,
        "bq": np.tile(g("bq").reshape(QC, 1), (8, 1)), "bk": np.tile(g("bk").reshape(QC, 1), (8, 1)), "minus": minus,
        "bv": np.broadcast_to(g("bv"), (P, P)),
        "woff": g("Woff").reshape(POINTS, 2, P).transpose(2, 1, 0),
        "boff": np.tile(g("boff").reshape(POINTS, 2), (LANES, 1)),
        "wbv": g("Wb")[:, :P].T, "wbh": blocks(g("Wb")[:, P:], 2),
        "gamma": halves(g("gamma")), "beta": halves(g("beta")), "rmean": halves(g("rmean")), "rvar": halves(g("rvar")),
        "gmean": np.kron(np.eye(P // 8), np.full((8, 8), 1 / 8)).astype(np.float32),
        "coords": coords, "ramp": np.broadcast_to(np.arange(SIDE, dtype=np.float32), (P, SIDE)),
        "id": np.eye(P, dtype=np.float32),
    }


def attn_arrays(i, pre=""):
    g = lambda n: i[pre + n]
    head_rows = np.zeros((P, HALVES, HEADS), np.float32)
    for p in range(P):
        for h in range(HALVES):
            head_rows[p, h, h * 4 + p // 32] = 1.0
    keep = np.ones((P, BATCH * CHUNKS), np.float32)
    keep[:, ::CHUNKS] = 0.0
    restart = np.zeros((P, BATCH * CHUNKS), np.float32)
    restart[:, ::CHUNKS] = -3e38
    tok = np.arange(P)
    a = {}
    for n in "qkvo":
        a["a_w" + n] = g(f"w{n}_w").T.reshape(HALVES, P, 256).transpose(1, 0, 2)
        a["a_b" + n] = g(f"w{n}_b").reshape(HALVES, P).T
    a["a_wg"] = g("wg_w").reshape(32, 32)
    a["a_wgb"] = np.broadcast_to(g("wg_b").reshape(1, 1), (HEADS, 1))
    a["a_kvs"] = g("kv_norm_scale").reshape(HEADS, 32, 32)
    a["a_qks"] = g("qk_norm_scale").reshape(HEADS, 1)
    a["c_ones"] = np.full((P, P), 1 / 256, np.float32)
    a["c_id"] = np.eye(P, dtype=np.float32)
    a["c_hr"] = head_rows
    a["c_hc"] = head_rows.transpose(2, 1, 0)
    a["c_mask"] = np.stack([(tok % 32 // GROUP == m) for m in range(2)], 1).astype(np.float32)
    a["c_keep"] = keep
    a["c_restart"] = restart
    return a


def chunked(x):
    return x.reshape(BATCH, HALVES, P, CHUNKS, CHUNK).transpose(0, 3, 2, 1, 4).reshape(-1, P, HALVES, CHUNK)


def unchunked(x):
    return np.ascontiguousarray(x.reshape(BATCH, CHUNKS, P, HALVES, CHUNK).transpose(0, 3, 2, 1, 4).reshape(BATCH, 256, 64, 64))


ATTN_ARGS = ["a_wq", "a_wk", "a_wv", "a_wo", "a_bq", "a_bk", "a_bv", "a_bo", "a_wg", "a_wgb", "a_kvs", "a_qks",
             "c_ones", "c_id", "c_hr", "c_hc", "c_mask", "c_keep", "c_restart"]


def ffn_arrays(i, pre=""):
    g = lambda n: i[pre + n]
    return {
        "f_gw": g("gate_w").reshape(HALVES, P, EXPERTS).transpose(1, 0, 2),
        "f_gb": np.broadcast_to(g("gate_b"), (P, EXPERTS)),
        "f_w1": g("W1").reshape(EXPERTS, HALVES, P, 512).transpose(2, 0, 1, 3),
        "f_b1": g("b1").reshape(EXPERTS, 4, P).transpose(2, 0, 1),
        "f_w2": g("W2").reshape(EXPERTS, 4, P, 256).transpose(2, 0, 1, 3),
        "f_b2": g("b2"),
    }


FFN_ARGS = ["f_gw", "f_gb", "f_w1", "f_b1", "f_w2", "f_b2", "c_ones", "c_id"]


def build(nc, arrays):
    d = {k: nc.dram_tensor(f"in_{k}", a.shape, F32, kind="ExternalInput").ap() for k, a in arrays.items()}
    shape = (BATCH * CHUNKS, P, HALVES, CHUNK)
    base, x1, x2 = (nc.dram_tensor(n, shape, F32, kind="Internal").ap() for n in ("base", "after_conv", "after_attention"))
    out = nc.dram_tensor("out", shape, F32, kind="ExternalOutput").ap()
    conv_layer(nc, d["x_in"], base, x1, d)
    attn_phase(nc, x1, x2, *[d[n] for n in ATTN_ARGS])
    ffn_phase(nc, x2, out, *[d[n] for n in FFN_ARGS])


def kernel(**inputs):
    import concourse.bacc as bacc
    from concourse.bass_utils import run_bass_kernel_spmd as run

    i = {k: np.asarray(v) for k, v in inputs.items()}
    arrays = {"x_in": chunked(i["x"])}
    arrays.update(conv_arrays(i, "L0_conv_"))
    arrays.update(attn_arrays(i, "L1_attn_"))
    arrays.update(ffn_arrays(i, "L1_ffn_"))
    arrays = {k: np.ascontiguousarray(a) for k, a in arrays.items()}
    nc = bacc.Bacc("TRN2", target_bir_lowering=False, num_devices=1)
    build(nc, arrays)
    r = run(nc, [{f"in_{k}": a for k, a in arrays.items()}], core_ids=[0])
    return unchunked(r.results[0]["out"])
```

```python
from contextlib import ExitStack

import numpy as np
import concourse.bass as bass
from concourse import mybir

ALU = mybir.AluOpType
ACT = mybir.ActivationFunctionType
AX = mybir.AxisListType
F32 = mybir.dt.float32
BF16 = mybir.dt.bfloat16

P = 128
BATCH = 2
HALVES = 2
CHUNK = 512
CHUNKS = 8
TOKENS = CHUNK * CHUNKS
HEADS = 8
EXPERTS = 8
LN_EPS = 1e-5


class Track:

    def __init__(self, ctx, nc, name, steps):
        self.sem = ctx.enter_context(nc.semaphore(name))
        self.steps = steps
        self.place = {s: i + 1 for i, s in enumerate(steps)}
        assert len(self.place) == len(steps), name
        self.per = len(steps)
        self.emitted = 0

    def credit(self, eng):
        eng.sem_inc(self.sem, self.per)

    def done(self, step):
        assert self.steps[self.emitted % self.per] == step, (step, self.steps[self.emitted % self.per])
        self.emitted += 1
        return self.sem

    def upto(self, t, step):
        return t * self.per + (self.per + self.place[step])

    def last_turn(self, t, step):
        return t * self.per + self.place[step]

    def so_far(self, t):
        return t * self.per + (self.per + self.emitted % self.per)


class Loads:

    def __init__(self, ctx, nc, name, per=1):
        self.sem = ctx.enter_context(nc.semaphore(name))
        self.per = per

    def upto(self, t):
        return t * (16 * self.per) + 16 * self.per


def chunk_of(dram, index):
    return dram[bass.ds(index, 1)].rearrange("o p k n -> (o p) k n")


SIDE = 64
POINTS = 32
ROWPAIRS = SIDE // 2
LANES = 4
CELLS = SIDE // 2
QC = 16


def norm_phase(nc, x_dram, group_mean, gamma, beta, rmean, rvar, gn, bn):
    n = BATCH * HALVES
    with ExitStack() as ctx:
        def sb(name, shape):
            return ctx.enter_context(nc.sbuf_tensor("gn_" + name, shape, F32))
        x_sb = sb("x", [P, BATCH * CHUNKS, HALVES, CHUNK])
        avg = sb("avg", [P, P])
        stats = sb("stats", [P, n, CHUNKS, 6])
        mv = sb("mv", [P, n, 2])
        off = sb("off", [P, n])
        spread = sb("spread", [P, n])
        par = sb("par", [P, 4, HALVES])
        means = ctx.enter_context(nc.psum_tensor("gn_means", [P, n], F32))
        variances = ctx.enter_context(nc.psum_tensor("gn_vars", [P, n], F32))
        ready = ctx.enter_context(nc.semaphore("gn_constants"))
        parts = [Loads(ctx, nc, f"gn_x_loaded{i}") for i in range(4)]
        dve_t = Track(ctx, nc, "gn_dve", [f"stats{i}" for i in range(n * CHUNKS)] + [f"mv{i}" for i in range(n)]
                      + "off offsq spread eps inv shift rv_eps rv_inv scale bias0 bias".split())
        pe_t = Track(ctx, nc, "gn_pe", ["mean", "var"])
        act_t = Track(ctx, nc, "gn_act", ["std", "rv_std"])
        block = ctx.enter_context(nc.Block())

        @block.sync
        def _(sp):
            for i in range(4):
                sp.dma_start(x_sb[:, 4 * i:4 * i + 4], x_dram[4 * i:4 * i + 4].rearrange("c p k n -> p c k n")).then_inc(parts[i].sem, 16)
            sp.dma_start(avg[:], group_mean).then_inc(ready, 16)
            for i, src in enumerate((gamma, beta, rmean, rvar)):
                sp.dma_start(par[:, i], src).then_inc(ready, 16)

        @block.tensor
        def _(pe):
            pe_t.credit(pe)
            pe.wait_ge(ready, 80)
            pe.wait_ge(dve_t.sem, dve_t.upto(0, f"mv{n - 1}"))
            nc.tensor.matmul(means[:], avg[:], mv[:, :, 0], start=True, stop=True).then_inc(pe_t.done("mean"), 1)
            pe.wait_ge(dve_t.sem, dve_t.upto(0, "spread"))
            nc.tensor.matmul(variances[:], avg[:], spread[:], start=True, stop=True).then_inc(pe_t.done("var"), 1)

        @block.scalar
        def _(act):
            act_t.credit(act)
            act.wait_ge(dve_t.sem, dve_t.upto(0, "eps"))
            nc.scalar.activation(gn[:, :, 0], gn[:, :, 0], ACT.Sqrt).then_inc(act_t.done("std"), 1)
            act.wait_ge(dve_t.sem, dve_t.upto(0, "rv_eps"))
            nc.scalar.activation(bn[:, :, 0], bn[:, :, 0], ACT.Sqrt).then_inc(act_t.done("rv_std"), 1)

        @block.vector
        def _(v):
            dve_t.credit(v)

            def own():
                v.wait_ge(dve_t.sem, dve_t.so_far(0))
            i = 0
            for c in range(BATCH * CHUNKS):
                if c % 4 == 0:
                    v.wait_ge(parts[c // 4].sem, 16)
                for h in range(HALVES):
                    nc.vector.bn_stats(stats[:, c // CHUNKS * HALVES + h, c % CHUNKS], x_sb[:, c, h]).then_inc(dve_t.done(f"stats{i}"), 1)
                    i += 1
            own()
            for i in range(n):
                nc.vector.bn_aggr(mv[:, i], stats[:, i].rearrange("p c s -> p (c s)")).then_inc(dve_t.done(f"mv{i}"), 1)
            v.wait_ge(pe_t.sem, pe_t.upto(0, "mean"))
            own()
            nc.vector.tensor_tensor(off[:], mv[:, :, 0], means[:], ALU.subtract).then_inc(dve_t.done("off"), 1)
            own()
            nc.vector.tensor_tensor(off[:], off[:], off[:], ALU.mult).then_inc(dve_t.done("offsq"), 1)
            own()
            nc.vector.tensor_tensor(spread[:], off[:], mv[:, :, 1], ALU.add).then_inc(dve_t.done("spread"), 1)
            v.wait_ge(pe_t.sem, pe_t.upto(0, "var"))
            nc.vector.tensor_scalar_add(gn[:, :, 0], variances[:], LN_EPS).then_inc(dve_t.done("eps"), 1)
            v.wait_ge(act_t.sem, act_t.upto(0, "std"))
            nc.vector.reciprocal(gn[:, :, 0], gn[:, :, 0]).then_inc(dve_t.done("inv"), 1)
            own()
            nc.vector.scalar_tensor_tensor(gn[:, :, 1], means[:], -1.0, gn[:, :, 0], ALU.mult, ALU.mult).then_inc(dve_t.done("shift"), 1)
            v.wait_ge(ready, 80)
            nc.vector.tensor_scalar_add(bn[:, :, 0], par[:, 3], LN_EPS).then_inc(dve_t.done("rv_eps"), 1)
            v.wait_ge(act_t.sem, act_t.upto(0, "rv_std"))
            nc.vector.reciprocal(bn[:, :, 0], bn[:, :, 0]).then_inc(dve_t.done("rv_inv"), 1)
            own()
            nc.vector.tensor_tensor(bn[:, :, 0], bn[:, :, 0], par[:, 0], ALU.mult).then_inc(dve_t.done("scale"), 1)
            own()
            nc.vector.tensor_tensor(bn[:, :, 1], par[:, 2], bn[:, :, 0], ALU.mult).then_inc(dve_t.done("bias0"), 1)
            own()
            nc.vector.tensor_tensor(bn[:, :, 1], par[:, 1], bn[:, :, 1], ALU.subtract).then_inc(dve_t.done("bias"), 1)


def upsample_phase(nc, b, high, up):
    S = SIDE // 2
    with ExitStack() as ctx:
        bufs = []
        for h in range(HALVES):
            def sb(name, shape):
                return ctx.enter_context(nc.sbuf_tensor(f"up{b}{h}_{name}", shape, F32))
            bufs.append((sb("in", [P, S, S]), sb("q", [P, S, S + 2]), sb("t", [P, S, S]), sb("wide", [P, S, S, 2])))
        tall_q = ctx.enter_context(nc.sbuf_tensor(f"up{b}_tq", [P, S + 2, SIDE], F32))
        tall_t = ctx.enter_context(nc.sbuf_tensor(f"up{b}_tt", [P, S, SIDE], F32))
        loaded = [ctx.enter_context(nc.semaphore(f"up{b}_loaded{h}")) for h in range(HALVES)]
        wide_steps = "q q_left q_right t even odd".split()
        tall_steps = "tq tq_top tq_bottom tt rows_even rows_odd".split()
        wide_t = [Track(ctx, nc, f"up{b}_wide{h}", wide_steps) for h in range(HALVES)]
        tall_t_ = Track(ctx, nc, f"up{b}_tall", [f"{s}{h}" for h in range(HALVES) for s in tall_steps])
        block = ctx.enter_context(nc.Block())

        def widen(eng, ops, h):
            tr = wide_t[h]
            tr.credit(eng)
            src, q, t, wide = bufs[h]
            eng.wait_ge(loaded[h], 16)
            ops.tensor_scalar(q[:, :, 1:S + 1], src[:], 0.25, None, ALU.mult).then_inc(tr.done("q"), 1)
            ops.tensor_scalar(q[:, :, 0:1], src[:, :, 0:1], 0.25, None, ALU.mult).then_inc(tr.done("q_left"), 1)
            ops.tensor_scalar(q[:, :, S + 1:], src[:, :, S - 1:], 0.25, None, ALU.mult).then_inc(tr.done("q_right"), 1)
            ops.tensor_scalar(t[:], src[:], 0.75, None, ALU.mult).then_inc(tr.done("t"), 1)
            eng.wait_ge(tr.sem, tr.upto(0, "t"))
            ops.tensor_tensor(wide[:, :, :, 0], q[:, :, 0:S], t[:], ALU.add).then_inc(tr.done("even"), 1)
            ops.tensor_tensor(wide[:, :, :, 1], q[:, :, 2:], t[:], ALU.add).then_inc(tr.done("odd"), 1)

        @block.sync
        def _(sp):
            for h in range(HALVES):
                sp.dma_start(bufs[h][0][:], high[b, :, h].rearrange("p (y x) -> p y x", x=S)).then_inc(loaded[h], 16)

        @block.gpsimd
        def _(pool):
            widen(pool, nc.gpsimd, 1)

        @block.vector
        def _(v):
            widen(v, nc.vector, 0)
            tr = tall_t_
            tr.credit(v)
            for h in range(HALVES):
                wide = bufs[h][3][:].rearrange("p y x e -> p y (x e)")
                rows = up[:, h].rearrange("p (y e x) -> p y e x", e=2, x=SIDE)
                v.wait_ge(wide_t[h].sem, wide_t[h].upto(0, "odd"))
                v.wait_ge(tr.sem, tr.so_far(0))
                nc.vector.tensor_scalar(tall_q[:, 1:S + 1], wide, 0.25, None, ALU.mult).then_inc(tr.done(f"tq{h}"), 1)
                nc.vector.tensor_scalar(tall_q[:, 0:1], wide[:, 0:1], 0.25, None, ALU.mult).then_inc(tr.done(f"tq_top{h}"), 1)
                nc.vector.tensor_scalar(tall_q[:, S + 1:], wide[:, S - 1:], 0.25, None, ALU.mult).then_inc(tr.done(f"tq_bottom{h}"), 1)
                nc.vector.tensor_scalar(tall_t[:], wide, 0.75, None, ALU.mult).then_inc(tr.done(f"tt{h}"), 1)
                v.wait_ge(tr.sem, tr.so_far(0))
                nc.vector.tensor_tensor(rows[:, :, 0], tall_q[:, 0:S], tall_t[:], ALU.add).then_inc(tr.done(f"rows_even{h}"), 1)
                nc.vector.tensor_tensor(rows[:, :, 1], tall_q[:, 2:], tall_t[:], ALU.add).then_inc(tr.done(f"rows_odd{h}"), 1)


def features_phase(nc, b, x_dram, base_dram, w, gn, up, qf, vf):
    with ExitStack() as ctx:
        def sb(name, shape):
            return ctx.enter_context(nc.sbuf_tensor(f"fe{b}_{name}", shape, F32))
        w1 = sb("w1", [P, 4, P])
        w2 = sb("w2", [P, HALVES, P])
        wb = sb("wb", [P, HALVES, 256])
        b1 = sb("b1", [P, 1])
        b2 = sb("b2", [P, 1])
        x_sb = sb("x", [P, HALVES, CHUNK])
        xg = sb("xg", [P, HALVES, CHUNK])
        base = sb("base", [P, HALVES, CHUNK])
        ps = ctx.enter_context(nc.psum_tensor(f"fe{b}_ps", [P, 2, 512], F32))
        ps_base = ctx.enter_context(nc.psum_tensor(f"fe{b}_psb", [P, HALVES, 512], F32))
        ready = ctx.enter_context(nc.semaphore(f"fe{b}_constants"))
        loads = Loads(ctx, nc, f"fe{b}_x_loaded")
        stores = Loads(ctx, nc, f"fe{b}_stored")
        pe_t = Track(ctx, nc, f"fe{b}_pe", ["vf", "base", "qf"])
        act_t = Track(ctx, nc, f"fe{b}_act", ["gn0", "gn1", "qf"])
        dve_t = Track(ctx, nc, f"fe{b}_dve", ["vf", "base"])
        stored_t = Track(ctx, nc, f"fe{b}_base_stored", ["stored"])
        consts = [(w1, w["w1"]), (w2, w["w2"]), (wb, w["wbh"]), (b1, w["b1"]), (b2, w["b2"])]
        block = ctx.enter_context(nc.Block())

        @block.sync
        def _(sp):
            for dst, src in consts:
                sp.dma_start(dst[:], src).then_inc(ready, 16)
            with sp.Fori(0, CHUNKS) as t:
                sp.wait_ge(act_t.sem, act_t.last_turn(t, "gn1"))
                sp.dma_start(x_sb[:], chunk_of(x_dram, t + b * CHUNKS)).then_inc(loads.sem, 16)

        @block.gpsimd
        def _(pool):
            stored_t.credit(pool)
            with pool.Fori(0, CHUNKS) as t:
                pool.wait_ge(dve_t.sem, dve_t.upto(t, "base"))
                pool.dma_start(chunk_of(base_dram, t + b * CHUNKS), base[:]).then_inc(stores.sem, 16)
                pool.wait_ge(stores.sem, stores.upto(t))
                pool.sem_inc(stored_t.done("stored"), 1)

        @block.tensor
        def _(pe):
            pe_t.credit(pe)
            pe.wait_ge(ready, 16 * len(consts))
            with pe.Fori(0, CHUNKS) as t:
                u = [up[:, k, bass.ds(t * CHUNK, CHUNK)] for k in range(HALVES)]
                pe.wait_ge(dve_t.sem, dve_t.last_turn(t, "vf"))
                for k in range(HALVES):
                    mm = nc.tensor.matmul(ps[:, 1], w2[:, k], u[k], start=(k == 0), stop=(k == 1))
                mm.then_inc(pe_t.done("vf"), 1)
                pe.wait_ge(dve_t.sem, dve_t.last_turn(t, "base"))
                for h in range(HALVES):
                    for k in range(HALVES):
                        mm = nc.tensor.matmul(ps_base[:, h], wb[:, k, h * P:(h + 1) * P], u[k], start=(k == 0), stop=(k == 1))
                mm.then_inc(pe_t.done("base"), 1)
                pe.wait_ge(act_t.sem, act_t.upto(t, "gn1"))
                for k in range(4):
                    mm = nc.tensor.matmul(ps[:, 0], w1[:, k], u[k] if k < 2 else xg[:, k - 2], start=(k == 0), stop=(k == 3))
                mm.then_inc(pe_t.done("qf"), 1)

        @block.scalar
        def _(act):
            act_t.credit(act)
            act.wait_ge(ready, 16 * len(consts))
            with act.Fori(0, CHUNKS) as t:
                act.wait_ge(loads.sem, loads.upto(t))
                act.wait_ge(pe_t.sem, pe_t.last_turn(t, "qf"))
                for h in range(HALVES):
                    g = b * HALVES + h
                    nc.scalar.activation(xg[:, h], x_sb[:, h], ACT.Identity, bias=gn[:, g, 1:2], scale=gn[:, g, 0:1]).then_inc(act_t.done(f"gn{h}"), 1)
                act.wait_ge(pe_t.sem, pe_t.upto(t, "qf"))
                nc.scalar.activation(qf[:, bass.ds(t * CHUNK, CHUNK)], ps[:, 0], ACT.Identity, bias=b1[:]).then_inc(act_t.done("qf"), 1)

        @block.vector
        def _(v):
            dve_t.credit(v)
            v.wait_ge(ready, 16 * len(consts))
            with v.Fori(0, CHUNKS) as t:
                v.wait_ge(pe_t.sem, pe_t.upto(t, "vf"))
                nc.vector.tensor_scalar(vf[:, bass.ds(t * CHUNK, CHUNK)], ps[:, 1], b2[:], None, ALU.add).then_inc(dve_t.done("vf"), 1)
                v.wait_ge(pe_t.sem, pe_t.upto(t, "base"))
                v.wait_ge(stored_t.sem, stored_t.last_turn(t, "stored"))
                nc.vector.tensor_copy(base[:], ps_base[:]).then_inc(dve_t.done("base"), 1)


def tables_phase(nc, b, w, coords, qf, vf, q_parts, k_parts, v_table, where):
    with ExitStack() as ctx:
        def sb(name, shape, dt=F32):
            return ctx.enter_context(nc.sbuf_tensor(f"ta{b}_{name}", shape, dt))
        wq, wk, wv, woff = sb("wq", [P, P]), sb("wk", [P, P]), sb("wv", [P, P]), sb("woff", [P, 2, POINTS])
        bq, bk, bv, boff = sb("bq", [P, 1]), sb("bk", [P, 1]), sb("bv", [P, P]), sb("boff", [P, 2])
        minus = sb("minus", [P, 2, 2])
        xy = sb("xy", [P, 2, ROWPAIRS * CELLS])
        whole = sb("whole", [P, 2, CHUNK])
        part = sb("part", [P, 2, CHUNK], BF16)
        ring = ctx.enter_context(nc.psum_tensor(f"ta{b}_ring", [P, 4, 512], F32))
        ready = ctx.enter_context(nc.semaphore(f"ta{b}_constants"))
        splits = [f"{n}{c}" for c in range(8) for n in "qk"]
        groups = splits + [f"v{g}" for g in range(8)] + [f"off{i}" for i in range(4)]
        pe_t = Track(ctx, nc, f"ta{b}_pe", groups)
        act_order, dve_order = [], []
        for i in range(len(splits) + 1):
            if i < len(splits):
                act_order += [f"whole_{splits[i]}", f"first_{splits[i]}"]
                dve_order += [f"rest_{splits[i]}"]
            if i:
                act_order += [f"second_{splits[i - 1]}", f"third_{splits[i - 1]}"]
                dve_order += [f"last_{splits[i - 1]}"]
        act_t = Track(ctx, nc, f"ta{b}_act", act_order)
        dve_t = Track(ctx, nc, f"ta{b}_dve", dve_order + [f"v{g}" for g in range(8)]
                      + [f"{s}{i}" for i in range(4) for s in ("off", "clamp")])
        consts = [(wq, w["wq"]), (wk, w["wk"]), (wv, w["wv"]), (woff, w["woff"]), (bq, w["bq"]), (bk, w["bk"]),
                  (bv, w["bv"]), (boff, w["boff"]), (xy, coords), (minus, w["minus"])]
        block = ctx.enter_context(nc.Block())

        @block.sync
        def _(sp):
            for dst, src in consts:
                sp.dma_start(dst[:], src).then_inc(ready, 16)

        @block.tensor
        def _(pe):
            pe_t.credit(pe)
            pe.wait_ge(ready, 16 * len(consts))
            for i, name in enumerate(groups):
                kind, n = name.rstrip("0123456789"), int(name.lstrip("qkvof"))
                dst = ring[:, i % 4]
                if i >= 4:
                    last = groups[i - 4]
                    if last[0] in "qk":
                        pe.wait_ge(act_t.sem, act_t.upto(0, f"whole_{last}"))
                    else:
                        pe.wait_ge(dve_t.sem, dve_t.upto(0, last))
                if kind in "qk":
                    src = qf if kind == "q" else vf
                    mm = nc.tensor.matmul(dst, (wq if kind == "q" else wk)[:], src[:, n * CHUNK:(n + 1) * CHUNK], start=True, stop=True)
                elif kind == "v":
                    cols = vf[:].rearrange("p (y x) -> p x y", x=SIDE)
                    for j in range(4):
                        for h in range(2):
                            mm = nc.tensor.matmul(dst[64 * h:64 * h + 64, j * P:(j + 1) * P], cols[:, 32 * h + 4 * n + j], wv[:],
                                                  start=True, stop=True)
                else:
                    cells = qf[:].rearrange("p (t r h a) -> p t r h a", r=2, h=2, a=CELLS)
                    half = slice(n % 2 * 16, n % 2 * 16 + 16)
                    for lane in range(LANES):
                        mm = nc.tensor.matmul(dst[32 * lane:32 * lane + 32], woff[:, n // 2], cells[:, half, lane % 2, lane // 2],
                                              start=True, stop=True)
                mm.then_inc(pe_t.done(name), 1)

        @block.scalar
        def _(act):
            act_t.credit(act)
            act.wait_ge(ready, 16 * len(consts))
            for i in range(len(splits) + 1):
                if i < len(splits):
                    name = splits[i]
                    act.wait_ge(pe_t.sem, pe_t.upto(0, name))
                    if i >= 2:
                        act.wait_ge(act_t.sem, act_t.upto(0, f"third_{splits[i - 2]}"))
                    nc.scalar.activation(whole[:, i % 2], ring[:, i % 4], ACT.Identity, bias=(bq if name[0] == "q" else bk)[:]
                                         ).then_inc(act_t.done(f"whole_{name}"), 1)
                    act.wait_ge(act_t.sem, act_t.so_far(0))
                    if i >= 2:
                        act.wait_ge(dve_t.sem, dve_t.upto(0, f"last_{splits[i - 2]}"))
                    nc.scalar.copy(part[:, i % 2], whole[:, i % 2]).then_inc(act_t.done(f"first_{name}"), 1)
                if i:
                    name, j = splits[i - 1], (i - 1) % 2
                    c = int(name[1:])
                    act.wait_ge(dve_t.sem, dve_t.upto(0, f"rest_{name}"))
                    nc.scalar.copy(part[:, j], whole[:, j]).then_inc(act_t.done(f"second_{name}"), 1)
                    act.wait_ge(dve_t.sem, dve_t.upto(0, f"last_{name}"))
                    if name[0] == "q":
                        dst, src = q_parts[:, c * CHUNK:(c + 1) * CHUNK], whole[:, j]
                    else:
                        dst, src = k_parts[:, :, 8 * c:8 * c + 8], whole[:, j].rearrange("p (y x) -> p x y", x=SIDE)
                    nc.scalar.copy(dst, src).then_inc(act_t.done(f"third_{name}"), 1)

        @block.vector
        def _(v):
            dve_t.credit(v)
            v.wait_ge(ready, 16 * len(consts))

            def take_off(step, after, name, j, which):
                v.wait_ge(act_t.sem, act_t.upto(0, f"{after}_{name}"))
                which = minus[:, "qk".index(name[0]), which:which + 1]
                nc.vector.scalar_tensor_tensor(whole[:, j], part[:, j], which, whole[:, j], ALU.mult, ALU.add
                                               ).then_inc(dve_t.done(f"{step}_{name}"), 1)

            for i in range(len(splits) + 1):
                if i < len(splits):
                    take_off("rest", "first", splits[i], i % 2, 0)
                if i:
                    take_off("last", "second", splits[i - 1], (i - 1) % 2, 1)
            for g in range(8):
                v.wait_ge(pe_t.sem, pe_t.upto(0, f"v{g}"))
                nc.vector.tensor_tensor(v_table[:, 4 * g:4 * g + 4], ring[:, (16 + g) % 4].rearrange("p (x c) -> p x c", c=P),
                                        bv[:].unsqueeze(1).to_broadcast([P, 4, P]), ALU.add).then_inc(dve_t.done(f"v{g}"), 1)
            for i in range(4):
                v.wait_ge(pe_t.sem, pe_t.upto(0, f"off{i}"))
                piece = where[:, i // 2, i % 2 * 512:i % 2 * 512 + 512]
                nc.vector.scalar_tensor_tensor(piece, ring[:, i % 4], boff[:, i // 2:i // 2 + 1], xy[:, i // 2, i % 2 * 512:i % 2 * 512 + 512],
                                               ALU.add, ALU.add).then_inc(dve_t.done(f"off{i}"), 1)
                v.wait_ge(dve_t.sem, dve_t.upto(0, f"off{i}"))
                nc.vector.tensor_scalar(piece, piece, 0.0, float(SIDE - 1), ALU.max, ALU.min).then_inc(dve_t.done(f"clamp{i}"), 1)


def sample_phase(nc, b, ramp, identity, q_parts, k_parts, v_table, where, val):
    C, G8, HS = CELLS, 8, SIDE // 2
    with ExitStack() as ctx:
        def sb(name, shape, dt=F32):
            return ctx.enter_context(nc.sbuf_tensor(f"sa{b}_{name}", shape, dt))
        ramp_sb = sb("ramp", [P, SIDE])
        ident = sb("ident", [P, P])
        qt = sb("qt", [P, P], BF16)
        scores = sb("scores", [P, SIDE, SIDE])
        hx = sb("hx", [P, 2, C, SIDE])
        hx_own = sb("hx_own", [P, C, 2, LANES, HS])
        hy = sb("hy", [P, 2, C, SIDE])
        ahy = sb("ahy", [P, C, SIDE])
        hy_t = sb("hy_t", [P, C, P])
        A = sb("A", [P, HS, P])
        logit, logit_t, probs, attn_t, attn = (sb(n, [P, 32]) for n in ("logit", "logit_t", "probs", "attn_t", "attn"))
        most, total = sb("most", [P, 1]), sb("total", [P, 1])
        ring = ctx.enter_context(nc.psum_tensor(f"sa{b}_ring", [P, 3, 1024], F32))
        out_ps = ctx.enter_context(nc.psum_tensor(f"sa{b}_out", [P, 512], F32))
        ready = ctx.enter_context(nc.semaphore(f"sa{b}_constants"))
        zeroed = ctx.enter_context(nc.semaphore(f"sa{b}_zeroed"))
        passed = ctx.enter_context(nc.semaphore(f"sa{b}_passed"))
        passed_pool = ctx.enter_context(nc.semaphore(f"sa{b}_passed_pool"))
        fills = [f"s{k}" for k in range(8)] + [f"tr{g}" for g in range(4)] + [f"l{k}" for k in range(4)] + [f"a{k}" for k in range(4)]
        by_act = ["s0", "s1", "s3", "s4", "s6", "s7", "tr1", "tr3"]
        by_dve = ["s2", "s5", "tr0", "tr2"]
        place = {name: i % 3 for i, name in enumerate(fills)}
        first_a = fills.index("a0")
        pe_t = Track(ctx, nc, f"sa{b}_pe", fills[:first_a] + ["out"] + fills[first_a:])
        act_t = Track(ctx, nc, f"sa{b}_act", ["qt"] + [n + r for n in by_act for r in "ab"] + "exp out".split())
        dve_t = Track(ctx, nc, f"sa{b}_dve", [n for k, name in enumerate(by_dve) for n in [name + "a", name + "b"] + ([f"own{k + 1}"] if k < 3 else [])]
                      + [f"{s}{k}{h}" for k in range(4) for s, h in (("l", "a"), ("l", "b"), ("logit", ""))]
                      + "logit_t most neg inv attn_t attn ahy0 ahy1 ahy2 ahy3".split() + [f"a{k}" for k in range(4)])
        pool_t = Track(ctx, nc, f"sa{b}_pool", ["own0"])
        act_hat = Track(ctx, nc, f"sa{b}_act_hat", ["abs_y", "hat_y", "abs_x", "hat_x"])
        pool_hat = Track(ctx, nc, f"sa{b}_pool_hat", ["dist_y", "dist_x"])
        tail_pe = Track(ctx, nc, f"sa{b}_tail_pe", ["out"])
        tail_act = Track(ctx, nc, f"sa{b}_tail_act", ["out"])
        block = ctx.enter_context(nc.Block())

        def schedule(eng, turn):
            with eng.Fori(0, ROWPAIRS // 2) as u:
                turn(u * 2, 0)
                turn(u * 2 + 1, 1)

        def own_lane(p, lane):
            s = slice(POINTS * lane, POINTS * lane + POINTS)
            return hx_own[s].rearrange("q a h l x -> q (a h) l x")[:, :, lane], hx[s, p].rearrange("q a (h x) -> q (a h) x", h=2)

        @block.sync
        def _(sp):
            sp.dma_start(ramp_sb[:], ramp).then_inc(ready, 16)
            sp.dma_start(ident[:], identity).then_inc(ready, 16)

        @block.gpsimd
        def _(pool):
            pool_t.credit(pool)
            pool_hat.credit(pool)
            pool.wait_ge(ready, 32)
            grid = ramp_sb[:].unsqueeze(1).to_broadcast([P, C, SIDE])

            def distances(t, p):
                places = where[:, :, bass.ds(t * C, C)]
                for k, (buf, c) in ((1, (hy, "y")), (0, (hx, "x"))):
                    nc.gpsimd.tensor_tensor(buf[:, p], grid, places[:, k].unsqueeze(2).to_broadcast([P, C, SIDE]),
                                            ALU.subtract).then_inc(pool_hat.done(f"dist_{c}"), 1)
            distances(0, 0)
            nc.gpsimd.memset(A[:], 0.0).then_inc(zeroed, 1)
            pool.wait_ge(zeroed, 3)

            def turn(t, p):
                pool.wait_ge(dve_t.sem, dve_t.last_turn(t, "ahy3"))
                pool.wait_ge(pool_t.sem, pool_t.last_turn(t, "own0"))
                pool.wait_ge(pool_hat.sem, pool_hat.upto(t, "dist_x"))
                distances(t + 1, 1 - p)
                pool.wait_ge(pe_t.sem, pe_t.last_turn(t, "a3"))
                pool.wait_ge(act_hat.sem, act_hat.upto(t, "hat_x"))
                pool.wait_ge(pool_hat.sem, pool_hat.upto(t + 1, "dist_x"))
                pool.sem_inc(passed_pool, 1)
                nc.gpsimd.tensor_copy(*own_lane(p, 0)).then_inc(pool_t.done("own0"), 1)
            schedule(pool, turn)

        @block.tensor
        def _(pe):
            pe_t.credit(pe)
            pe.wait_ge(ready, 32)
            pe.wait_ge(zeroed, 3)

            def free(t, i):
                last = i >= 3
                name = fills[i - 3 if last else i + 3 * ((len(fills) - 1 - i) // 3)]
                if name in by_act:
                    tr, step = act_t, name + "b"
                else:
                    tr, step = dve_t, name if name[0] == "a" else name + "b"
                pe.wait_ge(tr.sem, tr.upto(t, step) if last else tr.last_turn(t, step))

            def weighted_values(tr):
                for x in range(HS):
                    mm = nc.tensor.matmul(out_ps[:, 0:P], v_table[:, x], A[:, x], start=(x == 0), stop=(x == HS - 1))
                mm.then_inc(tr.done("out"), 1)

            def turn(t, p):
                for i, name in enumerate(fills):
                    pair = ring[:, place[name]]
                    n = int(name.lstrip("trsla"))
                    if name == "s0":
                        pe.wait_ge(act_t.sem, act_t.upto(t, "qt"))
                    if name == "tr0":
                        pe.wait_ge(act_hat.sem, act_hat.upto(t, "hat_y"))
                    if name == "l0":
                        pe.wait_ge(act_t.sem, act_t.upto(t, "tr3b"))
                        pe.wait_ge(dve_t.sem, dve_t.upto(t, "tr2b"))
                    if name == "a0":
                        pe.wait_ge(dve_t.sem, dve_t.last_turn(t, "a3"))
                        pe.wait_ge(act_t.sem, act_t.last_turn(t, "out"))
                        weighted_values(pe_t)
                        pe.wait_ge(pool_t.sem, pool_t.upto(t, "own0"))
                    if name in ("a0", "a1", "a2"):
                        pe.wait_ge(dve_t.sem, dve_t.upto(t, f"ahy{n}"))
                    else:
                        free(t, i)
                    if name[0] == "t":
                        pe.sem_inc(passed, 1)
                        for j in range(G8):
                            mm = nc.tensor.transpose(pair[0:64, j * P:(j + 1) * P], hy[:, p, G8 * n + j], ident[:])
                    elif name[0] == "s":
                        for j in range(G8):
                            mm = nc.tensor.matmul(pair[0:64, j * P:(j + 1) * P], k_parts[:, n * G8 + j], qt[:], start=True, stop=True)
                    elif name[0] == "l":
                        own_rows = scores[:].rearrange("q (h a) x -> q a h x", h=2)
                        for j in range(G8):
                            mm = nc.tensor.matmul(pair[:, j * P:(j + 1) * P], hy_t[:, n * G8 + j], own_rows[:, n * G8 + j],
                                                  start=True, stop=True)
                    else:
                        for j in range(G8):
                            for h in range(2):
                                a = n * G8 + j
                                mm = nc.tensor.matmul(pair[64 * h:64 * h + 64, j * P:(j + 1) * P], ahy[:, a],
                                                      hx_own[:, a, h].rearrange("q l x -> q (l x)"), start=True, stop=True)
                    mm.then_inc(pe_t.done(name), 1)
            schedule(pe, turn)

            tail_pe.credit(pe)
            pe.wait_ge(dve_t.sem, dve_t.last_turn(ROWPAIRS, "a3"))
            pe.wait_ge(act_t.sem, act_t.last_turn(ROWPAIRS, "out"))
            weighted_values(tail_pe)

        def take(copy, name, r):
            mine, n, src = slice(64 * r, 64 * r + 64), int(name.lstrip("str")), ring[0:64, place[name]]
            if name[0] == "s":
                return copy(scores[mine, :, n * G8:(n + 1) * G8].rearrange("q n x -> q x n"),
                            src.rearrange("q (x r n) -> q r x n", r=2, n=SIDE)[:, r])
            dst = hy_t[mine, G8 * n:G8 * n + G8].rearrange("q a (h r p) -> q (a h) r p", h=2, r=2)
            return copy(dst[:, :, r], src.rearrange("q (i r p) -> q i r p", r=2, p=POINTS)[:, :, r])

        @block.scalar
        def _(act):
            act_t.credit(act)

            def keep_values(slot, tr):
                nc.scalar.copy(slot.rearrange("p (r h a) -> p r h a", r=2, h=2),
                               out_ps[:, 0:P].rearrange("p (a h r) -> p r h a", h=2, r=2)).then_inc(tr.done("out"), 1)

            def hats(t, p):
                for buf, c in ((hy, "y"), (hx, "x")):
                    act.wait_ge(pool_hat.sem, pool_hat.upto(t, f"dist_{c}"))
                    nc.scalar.activation(buf[:, p], buf[:, p], ACT.Abs).then_inc(act_hat.done(f"abs_{c}"), 1)
                    act.wait_ge(act_hat.sem, act_hat.so_far(t))
                    nc.scalar.activation(buf[:, p], buf[:, p], ACT.Relu, bias=1.0, scale=-1.0).then_inc(act_hat.done(f"hat_{c}"), 1)
            act_hat.credit(act)
            hats(0, 0)
            act.wait_ge(zeroed, 3)

            def turn(t, p):
                act.wait_ge(pe_t.sem, pe_t.last_turn(t, "l3"))
                nc.scalar.copy(qt[:], q_parts[:, bass.ds(t * P, P)]).then_inc(act_t.done("qt"), 1)
                for name in by_act:
                    act.wait_ge(pe_t.sem, pe_t.upto(t, name))
                    for r in range(2):
                        take(nc.scalar.copy, name, r).then_inc(act_t.done(name + "ab"[r]), 1)
                hats(t + 1, 1 - p)
                act.wait_ge(dve_t.sem, dve_t.upto(t, "neg"))
                nc.scalar.activation(probs[:], logit_t[:], ACT.Exp, bias=most[:], scale=0.25, accum_out=total[:]).then_inc(act_t.done("exp"), 1)
                act.wait_ge(pe_t.sem, pe_t.upto(t, "out"))
                keep_values(val[:, bass.ds(t * P, P)], act_t)
            schedule(act, turn)
            tail_act.credit(act)
            act.wait_ge(tail_pe.sem, tail_pe.upto(0, "out"))
            keep_values(val[:, ROWPAIRS * P:], tail_act)

        @block.vector
        def _(v):
            dve_t.credit(v)
            nc.vector.memset(hy_t[:], 0.0).then_inc(zeroed, 1)
            nc.vector.memset(hx_own[:], 0.0).then_inc(zeroed, 1)
            v.wait_ge(zeroed, 3)
            def turn(t, p):
                def own():
                    v.wait_ge(dve_t.sem, dve_t.so_far(t))
                v.wait_ge(act_hat.sem, act_hat.upto(t, "hat_x"))
                for k, name in enumerate(by_dve):
                    v.wait_ge(pe_t.sem, pe_t.upto(t, name))
                    for r in range(2):
                        take(nc.vector.tensor_copy, name, r).then_inc(dve_t.done(name + "ab"[r]), 1)
                    if k < 3:
                        nc.vector.tensor_copy(*own_lane(p, k + 1)).then_inc(dve_t.done(f"own{k + 1}"), 1)
                for k in range(4):
                    cells = slice(k * G8, (k + 1) * G8)
                    v.wait_ge(pe_t.sem, pe_t.upto(t, f"l{k}"))
                    for h in range(2):
                        s = slice(64 * h, 64 * h + 64)
                        src = ring[s, place[f"l{k}"]].rearrange("p (a h x) -> p h a x", h=2, x=SIDE)[:, h]
                        nc.vector.tensor_tensor(ahy[s, cells], hx[s, p, cells], src, ALU.mult).then_inc(dve_t.done(f"l{k}{'ab'[h]}"), 1)
                    own()
                    nc.vector.tensor_reduce(logit[:, cells], ahy[:, cells], AX.X, ALU.add).then_inc(dve_t.done(f"logit{k}"), 1)
                own()
                nc.vector.transpose(logit_t[:], logit[:]).then_inc(dve_t.done("logit_t"), 1)
                own()
                nc.vector.tensor_reduce(most[:], logit_t[:], AX.X, ALU.max).then_inc(dve_t.done("most"), 1)
                own()
                nc.vector.tensor_scalar(most[:], most[:], -0.25, None, ALU.mult).then_inc(dve_t.done("neg"), 1)
                v.wait_ge(act_t.sem, act_t.upto(t, "exp"))
                nc.vector.reciprocal(total[:], total[:]).then_inc(dve_t.done("inv"), 1)
                own()
                nc.vector.tensor_scalar(attn_t[:], probs[:], total[:], None, ALU.mult).then_inc(dve_t.done("attn_t"), 1)
                own()
                nc.vector.transpose(attn[:], attn_t[:]).then_inc(dve_t.done("attn"), 1)
                own()
                for k in range(4):
                    cells = slice(k * G8, (k + 1) * G8)
                    nc.vector.tensor_tensor(ahy[:, cells], hy[:, p, cells], attn[:, cells].unsqueeze(2).to_broadcast([P, G8, SIDE]),
                                            ALU.mult).then_inc(dve_t.done(f"ahy{k}"), 1)
                v.wait_ge(pe_t.sem, pe_t.upto(t, "out"))
                for k in range(4):
                    v.wait_ge(pe_t.sem, pe_t.upto(t, f"a{k}"))
                    nc.vector.tensor_copy(A[:, :, k * 32:(k + 1) * 32].rearrange("q x n -> q n x"),
                                          ring[:, place[f"a{k}"]].rearrange("q (n x) -> q n x", x=HS)).then_inc(dve_t.done(f"a{k}"), 1)
            schedule(v, turn)


def merge_phase(nc, b, x_dram, base_dram, out_dram, wbv, bn, val):
    H = HALVES
    with ExitStack() as ctx:
        def sb(name, shape):
            return ctx.enter_context(nc.sbuf_tensor(f"me{b}_{name}", shape, F32))
        w_sb = sb("w", [P, 256])
        x_sb, base, tmp, res = (sb(n, [P, 2, H, CHUNK]) for n in ("x", "base", "tmp", "res"))
        ps = ctx.enter_context(nc.psum_tensor(f"me{b}_ps", [P, 2, H, 512], F32))
        ready = ctx.enter_context(nc.semaphore(f"me{b}_constants"))
        x_loads, base_loads, stores = ([Loads(ctx, nc, f"me{b}_{n}{c}") for c in range(2)] for n in ("x_loaded", "base_loaded", "stored"))
        pe_t = Track(ctx, nc, f"me{b}_pe", ["conv0", "conv1"])
        act_t = Track(ctx, nc, f"me{b}_act", [f"relu{c}{h}" for c in range(2) for h in range(H)])
        dve_t = Track(ctx, nc, f"me{b}_dve", ["sum0", "sum1", "res0", "res1"])
        stored_t = Track(ctx, nc, f"me{b}_res_stored", ["stored0", "stored1"])
        block = ctx.enter_context(nc.Block())

        @block.sync
        def _(sp):
            sp.dma_start(w_sb[:], wbv).then_inc(ready, 16)
            with sp.Fori(0, CHUNKS // 2) as t:
                for c in range(2):
                    sp.wait_ge(dve_t.sem, dve_t.last_turn(t, f"sum{c}"))
                    sp.dma_start(base[:, c], chunk_of(base_dram, t * 2 + (b * CHUNKS + c))).then_inc(base_loads[c].sem, 16)
                for c in range(2):
                    sp.wait_ge(dve_t.sem, dve_t.last_turn(t, f"res{c}"))
                    sp.dma_start(x_sb[:, c], chunk_of(x_dram, t * 2 + (b * CHUNKS + c))).then_inc(x_loads[c].sem, 16)

        @block.gpsimd
        def _(pool):
            stored_t.credit(pool)
            with pool.Fori(0, CHUNKS // 2) as t:
                for c in range(2):
                    pool.wait_ge(dve_t.sem, dve_t.upto(t, f"res{c}"))
                    two = out_dram[bass.ds(t * 4 + 2 * c, 2)].rearrange("u p h (b n) -> b p h u n", b=BATCH)[b]
                    pool.dma_start(two, res[:, c].rearrange("p h (u n) -> p h u n", u=2)).then_inc(stores[c].sem, 16)
                for c in range(2):
                    pool.wait_ge(stores[c].sem, stores[c].upto(t))
                    pool.sem_inc(stored_t.done(f"stored{c}"), 1)

        @block.tensor
        def _(pe):
            pe_t.credit(pe)
            pe.wait_ge(ready, 16)
            with pe.Fori(0, CHUNKS // 2) as t:
                for c in range(2):
                    pe.wait_ge(dve_t.sem, dve_t.last_turn(t, f"sum{c}"))
                    for h in range(H):
                        mm = nc.tensor.matmul(ps[:, c, h], w_sb[:, h * P:(h + 1) * P], val[:, bass.ds(t * 2 * CHUNK + (c * CHUNK + P), CHUNK)],
                                              start=True, stop=True)
                    mm.then_inc(pe_t.done(f"conv{c}"), 1)

        @block.scalar
        def _(act):
            act_t.credit(act)
            with act.Fori(0, CHUNKS // 2) as t:
                for c in range(2):
                    act.wait_ge(dve_t.sem, dve_t.upto(t, f"sum{c}"))
                    for h in range(H):
                        nc.scalar.activation(tmp[:, c, h], tmp[:, c, h], ACT.Relu, bias=bn[:, h, 1:2], scale=bn[:, h, 0:1]
                                             ).then_inc(act_t.done(f"relu{c}{h}"), 1)

        @block.vector
        def _(v):
            dve_t.credit(v)
            with v.Fori(0, CHUNKS // 2) as t:
                for c in range(2):
                    v.wait_ge(pe_t.sem, pe_t.upto(t, f"conv{c}"))
                    v.wait_ge(base_loads[c].sem, base_loads[c].upto(t))
                    v.wait_ge(dve_t.sem, dve_t.so_far(t))
                    nc.vector.tensor_tensor(tmp[:, c], base[:, c], ps[:, c], ALU.add).then_inc(dve_t.done(f"sum{c}"), 1)
                for c in range(2):
                    v.wait_ge(act_t.sem, act_t.upto(t, f"relu{c}1"))
                    v.wait_ge(x_loads[c].sem, x_loads[c].upto(t))
                    v.wait_ge(stored_t.sem, stored_t.last_turn(t, f"stored{c}"))
                    nc.vector.tensor_tensor(res[:, c], tmp[:, c], x_sb[:, c], ALU.add).then_inc(dve_t.done(f"res{c}"), 1)


def conv_layer(nc, x_dram, base_dram, out_dram, w):
    with ExitStack() as ctx:
        def sb(name, shape, dt=F32):
            return ctx.enter_context(nc.sbuf_tensor("cl_" + name, shape, dt))
        gn = sb("gn", [P, BATCH * HALVES, 2])
        bn = sb("bn", [P, HALVES, 2])
        norm_phase(nc, x_dram, w["gmean"], w["gamma"], w["beta"], w["rmean"], w["rvar"], gn, bn)
        q_parts = sb("q_parts", [P, TOKENS], BF16)
        k_parts = sb("k_parts", [P, SIDE, SIDE], BF16)
        v_table = sb("v_table", [P, SIDE // 2, P])
        where = sb("where", [P, 2, (ROWPAIRS + 1) * CELLS])
        with nc.semaphore("cl_where_end") as cleared, nc.Block() as block:
            @block.gpsimd
            def _(pool):
                nc.gpsimd.memset(where[:, :, ROWPAIRS * CELLS:], 0.0).then_inc(cleared, 1)
                pool.wait_ge(cleared, 1)
        for b in range(BATCH):
            with ExitStack() as inner:
                qf = inner.enter_context(nc.sbuf_tensor(f"qf{b}", [P, TOKENS], F32))
                vf = inner.enter_context(nc.sbuf_tensor(f"vf{b}", [P, TOKENS], F32))
                with nc.sbuf_tensor(f"resized{b}", [P, HALVES, TOKENS], F32) as up:
                    upsample_phase(nc, b, w["high"], up)
                    features_phase(nc, b, x_dram, base_dram, w, gn, up, qf, vf)
                tables_phase(nc, b, w, w["coords"], qf, vf, q_parts, k_parts, v_table, where)
            with nc.sbuf_tensor(f"values{b}", [P, (ROWPAIRS + 1) * P], F32) as val:
                sample_phase(nc, b, w["ramp"], w["id"], q_parts, k_parts, v_table, where, val)
                merge_phase(nc, b, x_dram, base_dram, out_dram, w["wbv"], bn, val)


UNIT = 256
UNITS = TOKENS // UNIT
GROUP = 16
GROUPS = BATCH * UNIT // GROUP
STEPS = UNIT // GROUP
ROWS = BATCH * HEADS
TINY = 1e-12
GATE_EPS = 1e-5
LEAST = -3e38


def attn_phase(nc, x_dram, out_dram, wq, wk, wv, wo, qb, kb, vb, ob, gate_weight, gate_bias, kv_scale, qk_scale,
               ones_mean, identity, head_rows, head_cols, group_mask):
    H, G, blocks = HALVES, GROUPS, CHUNK // P
    last = UNITS - 1
    with ExitStack() as ctx:
        def sb(name, shape):
            return ctx.enter_context(nc.sbuf_tensor("at_" + name, shape, F32))

        def psum(name, shape):
            return ctx.enter_context(nc.psum_tensor("at_" + name, shape, F32))

        w_sb = {n: sb("w" + n, [P, H, 256]) for n in "qkvo"}
        bias = {n: sb("b" + n, [P, H]) for n in "qkvo"}
        ones_sb = sb("ones", [P, P])
        ident = sb("ident", [P, P])
        to_rows = sb("to_rows", [P, H, BATCH, ROWS])
        to_cols = sb("to_cols", [ROWS, H, BATCH, P])
        mask = sb("mask", [P, 2])
        s_blk = sb("s_blk", [P, H, P])
        wg_blk = sb("wg_blk", [P, H, P])
        qks = sb("qks", [ROWS, 1])
        wgb = sb("wgb", [ROWS, 1])
        x_sb, cent, sq, xn, K, qk, ksq, vsq, gp, ctxt, res, x_again = (
            sb(n, [P, H, CHUNK]) for n in "x cent sq xn k qk ksq vsq gp ctxt res x_again".split())
        std = sb("std", [P, CHUNK])
        Q, V, GK = (sb(n, [P, 2, H, CHUNK]) for n in ("q", "v", "gk"))
        VT = sb("vt", [P, 2, H, blocks, P])
        GT = sb("gt", [P, 2, 2, H, blocks, P])
        spaced = sb("spaced", [P, 2, H, G * 2 * GROUP + GROUP])
        acc = sb("acc", [P, 2, H, G, GROUP])
        crow = sb("crow", [ROWS, 2, UNIT])
        pair = sb("pair", [P, 2, G, GROUP])
        weighed = sb("weighed", [P, 2, G, GROUP])
        sz = sb("sz", [P, 2, BATCH, H, P])
        before = sb("before", [P, H, blocks, P])
        sim, gate, g_norm, norm_inv, s_run, g_run, wrow, erow, spread_row, ones_row = (
            sb(n, [ROWS, UNIT]) for n in "sim gate g_norm norm_inv s_run g_run wrow erow spread_row ones_row".split())
        norms = sb("norms", [ROWS, 2, UNIT])
        expo = sb("expo", [ROWS, 2, UNIT])
        most = sb("most", [ROWS, UNIT + 1])
        s_car, g_car = sb("s_car", [ROWS, 1]), sb("g_car", [ROWS, 1])
        bank = psum("bank", [P, 3, 512])
        state = psum("state", [P, BATCH, H, P])
        before_ps = psum("before_ps", [P, H, blocks, P])
        paired = psum("paired", [P, 2, 512])

        fills = [tuple(f.split(":")) for f in
                 ("it0:c it1:c mean:a c0:c c1:c var:a o0:c o1:c q0:a q1:a k0:a k1:a v0:a v1:a nrm:a sim:a wg0:a wg1:a "
                  "tv0:a tv1:a glog:a gs0:a gs1:a tg0:a tg1:a").split()]
        pe_a, pe_c = (Track(ctx, nc, f"at_pe_{p}", [n for n, part in fills if part == p]) for p in "ac")
        pe_b = Track(ctx, nc, "at_pe_b", [f"{s}{i}" for i in range(STEPS) for s in ("paira", "pairb", "apply", "grow")])
        act_a = Track(ctx, nc, "at_act_a", "square sqrt q0 q1 k0 k1 ksq v0 v1 vsq norms exp vt0 vt1 silu gt00 gt01 gt10 gt11".split())
        act_c = Track(ctx, nc, "at_act_c", ["before0", "before1"])
        dve_a = Track(ctx, nc, "at_dve_a", ("center var_eps rstd norm floor inv sim norm_inv most0 s_car g_car most gp0 gp1 fall rise "
                                            "s_run s_eps s_inv w glog g_relu g_square gate g_norm gk0 gk1 g_run "
                                            "e1 e_inv sw g_eps g_inv c").split())
        dve_b = Track(ctx, nc, "at_dve_b", [f"{s}{i}" for i in range(STEPS) for s in ("sz", "weigha", "adda", "weighb", "addb")
                                            if s != "adda" or 2 * i % GROUP])
        dve_c = Track(ctx, nc, "at_dve_c", "inter0 inter1 ctxt0 ctxt1 res0 res1".split())
        pool_a = Track(ctx, nc, "at_pool_a", ["qk", "spaced"])
        pool_b = Track(ctx, nc, "at_pool_b", [f"pair{j}" for j in range(G)])
        stored_t = Track(ctx, nc, "at_res_stored", ["stored"])
        ready = ctx.enter_context(nc.semaphore("at_constants"))
        zeroed = ctx.enter_context(nc.semaphore("at_zeroed"))
        scaled = ctx.enter_context(nc.semaphore("at_gate_weight"))
        seeded = ctx.enter_context(nc.semaphore("at_state_zero"))
        passed = ctx.enter_context(nc.semaphore("at_passed"))
        passed_pool = ctx.enter_context(nc.semaphore("at_passed_pool"))
        x_loads = Loads(ctx, nc, "at_x_loaded")
        again_loads = Loads(ctx, nc, "at_x_again_loaded")
        stores = Loads(ctx, nc, "at_stored")
        readers = {"it0": (dve_c, "inter0"), "it1": (dve_c, "inter1"), "mean": (dve_a, "center"), "c0": (dve_c, "ctxt0"),
                   "c1": (dve_c, "ctxt1"), "var": (dve_a, "var_eps"), "o0": (dve_c, "res0"), "o1": (dve_c, "res1"),
                   "nrm": (act_a, "norms"), "sim": (dve_a, "sim"), "wg0": (dve_a, "gp0"), "wg1": (dve_a, "gp1"),
                   "tv0": (act_a, "vt0"), "tv1": (act_a, "vt1"), "glog": (dve_a, "glog"), "gs0": (dve_a, "gk0"),
                   "gs1": (dve_a, "gk1"), "tg0": (act_a, "gt01"), "tg1": (act_a, "gt11")}
        readers.update({n: (act_a, n) for n in ("q0", "q1", "k0", "k1", "v0", "v1")})
        names = [n for n, _ in fills]
        in_bank = {n: i % 3 for i, n in enumerate(names)}
        consts = [(w_sb["q"], wq), (w_sb["k"], wk), (w_sb["v"], wv), (w_sb["o"], wo), (bias["q"], qb), (bias["k"], kb),
                  (bias["v"], vb), (bias["o"], ob), (ones_sb, ones_mean), (ident, identity), (to_rows, head_rows),
                  (to_cols, head_cols), (mask, group_mask), (qks, qk_scale), (wgb, gate_bias)]
        n_consts = len(consts) + 2 * HEADS
        n_zeroed = 8
        block = ctx.enter_context(nc.Block())

        def schedule(eng, turn):
            turn(-1, 1, b=False, c=False)
            turn(0, 0, c=False)
            with eng.Fori(0, (UNITS - 2) // 2) as u:
                turn(u * 2 + 1, 1)
                turn(u * 2 + 2, 0)
            turn(last, last % 2, a=False)
            turn(last + 1, (last + 1) % 2, a=False, b=False)

        @block.sync
        def _(sp):
            stored_t.credit(sp)
            sp.wait_ge(zeroed, n_zeroed)
            for dst, src in consts:
                sp.dma_start(dst[:], src).then_inc(ready, 16)
            for h in range(HEADS):
                r = slice(32 * (h % 4), 32 * (h % 4) + 32)
                sp.dma_start(s_blk[r, h // 4, r], kv_scale[h]).then_inc(ready, 16)
                sp.dma_start(wg_blk[r, h // 4, r], gate_weight).then_inc(ready, 16)

            def turn(t, p, a=True, b=True, c=True):
                if a:
                    sp.wait_ge(dve_a.sem, dve_a.last_turn(t + 1, "center"))
                    sp.dma_start(x_sb[:], chunk_of(x_dram, t + 1)).then_inc(x_loads.sem, 16)
                if c:
                    sp.wait_ge(dve_c.sem, dve_c.last_turn(t - 1, "res1"))
                    sp.dma_start(x_again[:], chunk_of(x_dram, t - 1)).then_inc(again_loads.sem, 16)
                    sp.wait_ge(dve_c.sem, dve_c.upto(t - 1, "res1"))
                    sp.dma_start(chunk_of(out_dram, t - 1), res[:]).then_inc(stores.sem, 16)
                    sp.wait_ge(stores.sem, stores.upto(t - 1))
                    sp.sem_inc(stored_t.done("stored"), 1)
            schedule(sp, turn)

        @block.gpsimd
        def _(pool):
            pool_a.credit(pool)
            pool_b.credit(pool)
            nc.gpsimd.memset(spaced[:], 0.0).then_inc(zeroed, 1)
            pool.wait_ge(zeroed, n_zeroed)

            def make_qk(a, n):
                pool.wait_ge(act_a.sem, act_a.upto(a, "k1"))
                pool.wait_ge(pe_a.sem, pe_a.last_turn(a, "sim"))
                nc.gpsimd.tensor_tensor(qk[:], Q[:, n], K[:], ALU.mult).then_inc(pool_a.done("qk"), 1)

            def make_spaced(a, n):
                pool.wait_ge(act_a.sem, act_a.upto(a, "q1"))
                pool.sem_inc(passed_pool, 1)
                groups = spaced[:, n, :, 0:2 * GROUP * G].rearrange("p h (g z n) -> p h g z n", z=2, n=GROUP)[:, :, :, 1]
                nc.gpsimd.tensor_copy(groups, Q[:, n].rearrange("p h (g n) -> p h g n", n=GROUP)).then_inc(pool_a.done("spaced"), 1)

            def turn(t, p, a=True, b=True, c=True):
                if b:
                    for j in range(G):
                        if j == 14 and a:
                            make_qk(t + 1, 1 - p)
                        if j == 24 and a:
                            make_spaced(t + 1, 1 - p)
                        h, far = j // GROUP, j % GROUP
                        if j >= 2:
                            pool.wait_ge(pe_b.sem, pe_b.upto(t, f"pair{'ab'[j % 2]}{j // 2 - 1}"))
                        else:
                            pool.wait_ge(pe_b.sem, pe_b.last_turn(t, f"pair{'ab'[j % 2]}{STEPS - 1}"))
                            pool.wait_ge(act_a.sem, act_a.upto(t, "v1"))
                        q_part = Q[:, p, h].rearrange("p (g n) -> p g n", n=GROUP)[:, :, far:]
                        v_part = V[:, p, h].rearrange("p (g n) -> p g n", n=GROUP)[:, :, 0:GROUP - far]
                        nc.gpsimd.tensor_tensor(pair[:, j % 2, :, 0:GROUP - far], q_part, v_part, ALU.mult).then_inc(pool_b.done(f"pair{j}"), 1)
                elif a:
                    make_qk(t + 1, 1 - p)
                    make_spaced(t + 1, 1 - p)
            schedule(pool, turn)

        @block.tensor
        def _(pe):
            for tr in (pe_a, pe_b, pe_c):
                tr.credit(pe)
            pe.wait_ge(ready, 16 * n_consts)
            pe.wait_ge(scaled, 1)
            pe.wait_ge(zeroed, n_zeroed)
            nc.tensor.matmul(state[:].rearrange("p b h e -> p (b h e)"), sz[:, 0, 0, 0], sz[:, 0].rearrange("p b h e -> p (b h e)"),
                             start=True, stop=False, skip_group_check=True).then_inc(seeded, 1)
            pe.wait_ge(seeded, 1)

            def turn(t, p, a=True, b=True, c=True):
                n = 1 - p
                first = not (b or c)

                def into(name, implied=False):
                    if implied:
                        return in_bank[name]
                    i = names.index(name)
                    here = [k for k in range(i % 3, i, 3) if (a if fills[k][1] == "a" else c)]
                    if here:
                        k, back = here[-1], 0
                    else:
                        k, back = [k for k in range(i % 3, len(fills), 3) if fills[k][1] == ("a" if a or b else "c")][-1], 1
                    tr, step = readers[names[k]]
                    index = (t + 1 if fills[k][1] == "a" else t - 1) - back
                    if not (first and back):
                        pe.wait_ge(tr.sem, tr.upto(index, step))
                    return in_bank[name]

                def both(name, lhs, rhs, implied=False):
                    dst = bank[:, into(name, implied)]
                    for k in range(H):
                        mm = nc.tensor.matmul(dst, lhs[k], rhs[k], start=(k == 0), stop=(k == H - 1))
                    return mm

                def rows(dst, src):
                    for k in range(H):
                        for im in range(BATCH):
                            mm = nc.tensor.matmul(dst, to_rows[:, k, im], src[:, k, im * UNIT:(im + 1) * UNIT],
                                                  start=(k == 0 and im == 0), stop=(k == H - 1 and im == BATCH - 1))
                    return mm

                def cols(name, h, src):
                    dst = bank[:, into(name)]
                    for im in range(BATCH):
                        mm = nc.tensor.matmul(dst[:, im * UNIT:(im + 1) * UNIT], to_cols[:, h, im], src, start=True, stop=True)
                    return mm

                def flip(name, src, implied=False):
                    dst = bank[:, into(name, implied)]
                    pe.sem_inc(passed, 1)
                    for blk in range(blocks):
                        mm = nc.tensor.transpose(dst[:, blk * P:(blk + 1) * P], src(blk), ident[:])
                    return mm

                def project(name):
                    h = int(name[1])
                    both(name, [w_sb[name[0]][:, k, h * P:(h + 1) * P] for k in range(H)], [xn[:, 0], xn[:, 1]]).then_inc(pe_a.done(name), 1)

                def side(i):
                    if i == 0:
                        if c:
                            pe.wait_ge(act_c.sem, act_c.upto(t - 1, "before1"))
                            for h in range(H):
                                flip(f"it{h}", lambda blk: before[:, h, blk]).then_inc(pe_c.done(f"it{h}"), 1)
                        if a:
                            pe.wait_ge(x_loads.sem, x_loads.upto(t + 1))
                            both("mean", [ones_sb[:]] * 2, [x_sb[:, 0], x_sb[:, 1]]).then_inc(pe_a.done("mean"), 1)
                    if i == 1:
                        if c:
                            pe.wait_ge(dve_a.sem, dve_a.upto(t - 1, "c"))
                            for h in range(H):
                                cols(f"c{h}", h, crow[:, n]).then_inc(pe_c.done(f"c{h}"), 1)
                        if a:
                            pe.wait_ge(act_a.sem, act_a.upto(t + 1, "square"))
                            both("var", [ones_sb[:]] * 2, [sq[:, 0], sq[:, 1]]).then_inc(pe_a.done("var"), 1)
                    if i == 2 and c:
                        pe.wait_ge(dve_c.sem, dve_c.upto(t - 1, "ctxt1"))
                        for h in range(H):
                            both(f"o{h}", [w_sb["o"][:, k, h * P:(h + 1) * P] for k in range(H)],
                                 [ctxt[:, 0], ctxt[:, 1]], implied=True).then_inc(pe_c.done(f"o{h}"), 1)
                    if not a:
                        return
                    if i == 3:
                        pe.wait_ge(dve_a.sem, dve_a.upto(t + 1, "norm"))
                        project("q0")
                    if i == 4:
                        project("q1")
                        project("k0")
                    if i == 5:
                        project("k1")
                        project("v0")
                    if i == 6:
                        project("v1")
                    if i == 7:
                        pe.wait_ge(act_a.sem, act_a.upto(t + 1, "ksq"))
                        dst = bank[0:ROWS, into("nrm", implied=True)]
                        rows(dst[:, 0:UNIT], ksq)
                        pe.wait_ge(act_a.sem, act_a.upto(t + 1, "vsq"))
                        rows(dst[:, UNIT:], vsq).then_inc(pe_a.done("nrm"), 1)
                    if i == 8:
                        pe.wait_ge(pool_a.sem, pool_a.upto(t + 1, "qk"))
                        rows(bank[0:ROWS, into("sim")][:, 0:UNIT], qk).then_inc(pe_a.done("sim"), 1)
                    if i == 9:
                        for h in range(H):
                            nc.tensor.matmul(bank[:, into(f"wg{h}")], wg_blk[:, h], V[:, n, h], start=True, stop=True).then_inc(pe_a.done(f"wg{h}"), 1)
                    if i == 10:
                        for h in range(H):
                            flip(f"tv{h}", lambda blk: V[:, n, h, blk * P:(blk + 1) * P]).then_inc(pe_a.done(f"tv{h}"), 1)
                    if i == 11:
                        pe.wait_ge(dve_a.sem, dve_a.upto(t + 1, "gp1"))
                        rows(bank[0:ROWS, into("glog", implied=True)][:, 0:UNIT], gp).then_inc(pe_a.done("glog"), 1)
                    if i == 13:
                        pe.wait_ge(dve_a.sem, dve_a.upto(t + 1, "g_norm"))
                        for h in range(H):
                            cols(f"gs{h}", h, g_norm[:]).then_inc(pe_a.done(f"gs{h}"), 1)
                    if i == 14:
                        for h in range(H):
                            pe.wait_ge(dve_a.sem, dve_a.upto(t + 1, f"gk{h}"))
                            flip(f"tg{h}", lambda blk: GK[:, n, h, blk * P:(blk + 1) * P], implied=True).then_inc(pe_a.done(f"tg{h}"), 1)

                for i in range(STEPS):
                    if b:
                        for j in (2 * i, 2 * i + 1):
                            h, far, s = j // GROUP, j % GROUP, "ab"[j % 2]
                            pe.wait_ge(pool_b.sem, pool_b.upto(t, f"pair{j}"))
                            pe.wait_ge(dve_b.sem, dve_b.upto(t, f"weigh{s}{i - 1}") if i else dve_b.last_turn(t, f"weigh{s}{STEPS - 1}"))
                            nc.tensor.matmul(paired[:, j % 2, 0:G * (GROUP - far)], s_blk[:, h], pair[:, j % 2, :, 0:GROUP - far],
                                             start=True, stop=True).then_inc(pe_b.done(f"pair{s}{i}"), 1)
                        if i == 0:
                            pe.wait_ge(act_c.sem, act_c.last_turn(t, "before1"))
                            pe.wait_ge(pool_a.sem, pool_a.upto(t, "spaced"))
                            pe.wait_ge(act_a.sem, act_a.upto(t, "gt11"))
                        pe.wait_ge(dve_b.sem, dve_b.upto(t, f"sz{i}"))
                        r, m = slice(32 * (i % 8 // 2), 32 * (i % 8 // 2) + 32), i % 2
                        for im in range(BATCH):
                            g = im * STEPS + i
                            start = g * 2 * GROUP + (0 if m else GROUP)
                            for k in range(H):
                                mm = nc.tensor.matmul(before_ps[r, k, g // 8], spaced[:, p, k, start:start + 2 * GROUP], sz[:, i % 2, im, k],
                                                      start=(m == 0 and im == 0), stop=(m == 1), skip_group_check=True)
                        mm.then_inc(pe_b.done(f"apply{i}"), 1)
                        for im in range(BATCH):
                            blk = im * 2 + i // 8
                            for k in range(H):
                                mm = nc.tensor.matmul(state[:, im, k], VT[r, p, k, blk], GT[r, p, m, k, blk],
                                                      start=False, stop=False, skip_group_check=True)
                        mm.then_inc(pe_b.done(f"grow{i}"), 1)
                    side(i)
            schedule(pe, turn)

        @block.scalar
        def _(act):
            act_a.credit(act)
            act_c.credit(act)
            act.wait_ge(ready, 16 * n_consts)

            def turn(t, p, a=True, b=True, c=True):
                n = 1 - p
                A = t + 1

                def step(name, ins):
                    ins.then_inc(act_a.done(name), 1)

                if c:
                    act.wait_ge(pe_b.sem, pe_b.upto(t - 1, f"grow{STEPS - 1}"))
                    act.wait_ge(pe_c.sem, pe_c.last_turn(t - 1, "it1"))
                    for h in range(H):
                        nc.scalar.copy(before[:, h], before_ps[:, h]).then_inc(act_c.done(f"before{h}"), 1)
                if not a:
                    return
                act.wait_ge(dve_a.sem, dve_a.upto(A, "center"))
                step("square", nc.scalar.activation(sq[:], cent[:], ACT.Square))
                act.wait_ge(dve_a.sem, dve_a.upto(A, "var_eps"))
                step("sqrt", nc.scalar.activation(std[:], std[:], ACT.Sqrt))
                for name, dst in (("q", Q[:, n]), ("k", K), ("v", V[:, n])):
                    for h in range(H):
                        act.wait_ge(pe_a.sem, pe_a.upto(A, f"{name}{h}"))
                        step(f"{name}{h}", nc.scalar.activation(dst[:, h], bank[:, in_bank[f"{name}{h}"]], ACT.Identity, bias=bias[name][:, h:h + 1]))
                    if name == "k":
                        act.wait_ge(act_a.sem, act_a.so_far(A))
                        step("ksq", nc.scalar.activation(ksq[:], K[:], ACT.Square))
                act.wait_ge(act_a.sem, act_a.so_far(A))
                step("vsq", nc.scalar.activation(vsq[:], V[:, n], ACT.Square))
                act.wait_ge(pe_a.sem, pe_a.upto(A, "nrm"))
                act.wait_ge(dve_a.sem, dve_a.last_turn(A, "norm_inv"))
                step("norms", nc.scalar.activation(norms[:].rearrange("r k n -> r (k n)"), bank[0:ROWS, in_bank["nrm"]], ACT.Sqrt))
                act.wait_ge(dve_a.sem, dve_a.upto(A, "rise"))
                step("exp", nc.scalar.activation(expo[:], expo[:], ACT.Exp))
                for h in range(H):
                    act.wait_ge(pe_a.sem, pe_a.upto(A, f"tv{h}"))
                    step(f"vt{h}", nc.scalar.copy(VT[:, n, h], bank[:, in_bank[f"tv{h}"]].rearrange("p (b c) -> p b c", c=P)))
                act.wait_ge(dve_a.sem, dve_a.upto(A, "w"))
                step("silu", nc.scalar.activation(erow[:], wrow[:], ACT.Exp, scale=-1.0))
                for h in range(H):
                    act.wait_ge(pe_a.sem, pe_a.upto(A, f"tg{h}"))
                    for m in range(2):
                        step(f"gt{h}{m}", nc.scalar.activation(GT[:, n, m, h], bank[:, in_bank[f"tg{h}"]].rearrange("p (b c) -> p b c", c=P),
                                                               ACT.Copy, scale=mask[:, m:m + 1]))
            schedule(act, turn)

        @block.vector
        def _(v):
            for tr in (dve_a, dve_b, dve_c):
                tr.credit(v)
            for z in (s_blk, wg_blk, s_run, g_run):
                nc.vector.memset(z[:], 0.0).then_inc(zeroed, 1)
            nc.vector.memset(sz[:, 0], 0.0).then_inc(zeroed, 1)
            nc.vector.memset(ones_row[:], 1.0).then_inc(zeroed, 1)
            nc.vector.memset(most[:], LEAST).then_inc(zeroed, 1)
            v.wait_ge(ready, 16 * n_consts)
            nc.vector.tensor_tensor(wg_blk[:], wg_blk[:], s_blk[:], ALU.mult).then_inc(scaled, 1)
            v.wait_ge(scaled, 1)
            v.wait_ge(zeroed, n_zeroed)
            v.wait_ge(seeded, 1)

            def turn(t, p, a=True, b=True, c=True):
                n = 1 - p
                A = t + 1

                def own(tr, index):
                    v.wait_ge(tr.sem, tr.so_far(index))

                def step(name, ins):
                    ins.then_inc(dve_a.done(name), 1)

                def side(i):
                    if i == 0:
                        if c:
                            for h in range(H):
                                v.wait_ge(pe_c.sem, pe_c.upto(t - 1, f"it{h}"))
                                own(dve_b, t)
                                flat = acc[:, n, h].rearrange("p g n -> p (g n)")
                                nc.vector.tensor_tensor(flat, flat, bank[:, in_bank[f"it{h}"]], ALU.add).then_inc(dve_c.done(f"inter{h}"), 1)
                        if a:
                            v.wait_ge(pe_a.sem, pe_a.upto(A, "mean"))
                            v.wait_ge(act_a.sem, act_a.last_turn(A, "square"))
                            own(dve_a, A)
                            step("center", nc.vector.tensor_tensor(cent[:], x_sb[:], bank[:, in_bank["mean"]].unsqueeze(1).to_broadcast([P, H, CHUNK]),
                                                                   ALU.subtract))
                    if i == 1:
                        if c:
                            for h in range(H):
                                v.wait_ge(pe_c.sem, pe_c.upto(t - 1, f"c{h}"))
                                own(dve_c, t - 1)
                                nc.vector.tensor_tensor(ctxt[:, h], acc[:, n, h].rearrange("p g n -> p (g n)"), bank[:, in_bank[f"c{h}"]],
                                                        ALU.mult).then_inc(dve_c.done(f"ctxt{h}"), 1)
                        if a:
                            v.wait_ge(pe_a.sem, pe_a.upto(A, "var"))
                            own(dve_a, A)
                            step("var_eps", nc.vector.tensor_scalar_add(std[:], bank[:, in_bank["var"]], LN_EPS))
                    if i == 2:
                        if a:
                            v.wait_ge(act_a.sem, act_a.upto(A, "sqrt"))
                            step("rstd", nc.vector.reciprocal(std[:], std[:]))
                            v.wait_ge(pe_a.sem, pe_a.last_turn(A, "v1"))
                            own(dve_a, A)
                            step("norm", nc.vector.tensor_tensor(xn[:], cent[:], std[:].unsqueeze(1).to_broadcast([P, H, CHUNK]), ALU.mult))
                    if i == 3 and c:
                        v.wait_ge(again_loads.sem, again_loads.upto(t - 1))
                        v.wait_ge(stored_t.sem, stored_t.last_turn(t - 1, "stored"))
                        for h in range(H):
                            v.wait_ge(pe_c.sem, pe_c.upto(t - 1, f"o{h}"))
                            nc.vector.scalar_tensor_tensor(res[:, h], bank[:, in_bank[f"o{h}"]], bias["o"][:, h:h + 1], x_again[:, h],
                                                           ALU.add, ALU.add).then_inc(dve_c.done(f"res{h}"), 1)
                    if not a:
                        return
                    if i == 8:
                        v.wait_ge(act_a.sem, act_a.upto(A, "norms"))
                        step("floor", nc.vector.tensor_scalar_max(norms[:], norms[:], TINY))
                        own(dve_a, A)
                        step("inv", nc.vector.reciprocal(norms[:], norms[:]))
                    if i == 9:
                        v.wait_ge(pe_a.sem, pe_a.upto(A, "sim"))
                        own(dve_a, A)
                        step("sim", nc.vector.tensor_scalar(sim[:], bank[0:ROWS, in_bank["sim"], 0:UNIT], qks[:], None, ALU.mult))
                        step("norm_inv", nc.vector.tensor_tensor(norm_inv[:], norms[:, 0], norms[:, 1], ALU.mult))
                        step("most0", nc.vector.tensor_copy(most[:, 0:1], most[:, UNIT:UNIT + 1]))
                        step("s_car", nc.vector.tensor_copy(s_car[:], s_run[:, UNIT - 1:UNIT]))
                        step("g_car", nc.vector.tensor_copy(g_car[:], g_run[:, UNIT - 1:UNIT]))
                        own(dve_a, A)
                        step("most", nc.vector.tensor_tensor_scan(most[:, 1:], sim[:], sim[:], most[:, 0:1], ALU.max, ALU.max))
                    if i == 10:
                        for h in range(H):
                            v.wait_ge(pe_a.sem, pe_a.upto(A, f"wg{h}"))
                            step(f"gp{h}", nc.vector.tensor_tensor(gp[:, h], K[:, h], bank[:, in_bank[f"wg{h}"]], ALU.mult))
                        own(dve_a, A)
                        v.wait_ge(act_a.sem, act_a.last_turn(A, "exp"))
                        step("fall", nc.vector.tensor_tensor(expo[:, 0], most[:, 0:UNIT], most[:, 1:], ALU.subtract))
                        step("rise", nc.vector.tensor_tensor(expo[:, 1], sim[:], most[:, 1:], ALU.subtract))
                    if i == 11:
                        v.wait_ge(act_a.sem, act_a.upto(A, "exp"))
                        step("s_run", nc.vector.tensor_tensor_scan(s_run[:], expo[:, 0], expo[:, 1], s_car[:], ALU.mult, ALU.add))
                        own(dve_a, A)
                        step("s_eps", nc.vector.tensor_scalar_add(wrow[:], s_run[:], GATE_EPS))
                        own(dve_a, A)
                        step("s_inv", nc.vector.reciprocal(wrow[:], wrow[:]))
                        own(dve_a, A)
                        step("w", nc.vector.tensor_tensor(wrow[:], expo[:, 1], wrow[:], ALU.mult))
                    if i == 12:
                        v.wait_ge(pe_a.sem, pe_a.upto(A, "glog"))
                        own(dve_a, A)
                        step("glog", nc.vector.tensor_tensor(gate[:], bank[0:ROWS, in_bank["glog"], 0:UNIT], norm_inv[:], ALU.mult))
                        own(dve_a, A)
                        step("g_relu", nc.vector.tensor_scalar(gate[:], gate[:], wgb[:], 0.0, ALU.add, ALU.max))
                        own(dve_a, A)
                        step("g_square", nc.vector.tensor_tensor(gate[:], gate[:], gate[:], ALU.mult))
                        own(dve_a, A)
                        step("gate", nc.vector.tensor_scalar_add(gate[:], gate[:], GATE_EPS))
                        own(dve_a, A)
                        step("g_norm", nc.vector.tensor_tensor(g_norm[:], gate[:], norm_inv[:], ALU.mult))
                    if i == 13:
                        for h in range(H):
                            v.wait_ge(pe_a.sem, pe_a.upto(A, f"gs{h}"))
                            step(f"gk{h}", nc.vector.tensor_tensor(GK[:, n, h], K[:, h], bank[:, in_bank[f"gs{h}"]], ALU.mult))
                        step("g_run", nc.vector.tensor_tensor_scan(g_run[:], ones_row[:], gate[:], g_car[:], ALU.mult, ALU.add))
                    if i == 14:
                        v.wait_ge(act_a.sem, act_a.upto(A, "silu"))
                        own(dve_a, A)
                        step("e1", nc.vector.tensor_scalar_add(erow[:], erow[:], 1.0))
                        own(dve_a, A)
                        step("e_inv", nc.vector.reciprocal(erow[:], erow[:]))
                        own(dve_a, A)
                        step("sw", nc.vector.tensor_tensor(erow[:], wrow[:], erow[:], ALU.mult))
                    if i == 15:
                        step("g_eps", nc.vector.tensor_scalar_add(spread_row[:], g_run[:], GATE_EPS))
                        own(dve_a, A)
                        step("g_inv", nc.vector.reciprocal(spread_row[:], spread_row[:]))
                        own(dve_a, A)
                        if b:
                            v.wait_ge(pe_c.sem, pe_c.last_turn(t, "c1"))
                        step("c", nc.vector.scalar_tensor_tensor(crow[:, n], erow[:], 1.0, spread_row[:], ALU.add, ALU.mult))

                for i in range(STEPS):
                    if b:
                        if i:
                            v.wait_ge(pe_b.sem, pe_b.upto(t, f"grow{i - 1}"))
                        else:
                            v.wait_ge(pe_b.sem, pe_b.last_turn(t, f"grow{STEPS - 1}"))
                            v.wait_ge(dve_a.sem, dve_a.upto(t, "gk1"))
                            if c:
                                own(dve_c, t - 1)
                        own(dve_b, t)
                        nc.vector.tensor_tensor(sz[:, i % 2], state[:], s_blk[:].unsqueeze(1).to_broadcast([P, BATCH, H, P]),
                                                ALU.mult).then_inc(dve_b.done(f"sz{i}"), 1)
                        for j in (2 * i, 2 * i + 1):
                            h, far, s = j // GROUP, j % GROUP, "ab"[j % 2]
                            v.wait_ge(pe_b.sem, pe_b.upto(t, f"pair{s}{i}"))
                            gk_part = GK[:, p, h].rearrange("p (g n) -> p g n", n=GROUP)[:, :, 0:GROUP - far]
                            dst = acc[:, p, h] if far == 0 else weighed[:, j % 2, :, 0:GROUP - far]
                            nc.vector.tensor_tensor(dst, gk_part, paired[:, j % 2, 0:G * (GROUP - far)].rearrange("p (g n) -> p g n", g=G),
                                                    ALU.mult).then_inc(dve_b.done(f"weigh{s}{i}"), 1)
                            if far:
                                own(dve_b, t)
                                nc.vector.tensor_tensor(acc[:, p, h, :, far:], acc[:, p, h, :, far:], dst, ALU.add).then_inc(dve_b.done(f"add{s}{i}"), 1)
                    side(i)
            schedule(v, turn)


def ffn_phase(nc, x_dram, out_dram, gate_w, gate_b, w1, b1, w2, b2, ones_mean, identity, expert_rows):
    E, M, H = EXPERTS, 4, HALVES
    R = 3 * E
    blocks = CHUNK // P
    turns = BATCH * CHUNKS
    with ExitStack() as ctx:
        def sb(name, shape, dt=F32):
            return ctx.enter_context(nc.sbuf_tensor("ffn_" + name, shape, dt))

        def psum(name, shape):
            return ctx.enter_context(nc.psum_tensor("ffn_" + name, shape, F32))

        w1_sb = sb("w1", [P, E, H, 512])
        w2_sb = sb("w2", [P, E, M, 256])
        b1_sb = sb("b1", [P, E, M])
        b2_sb = sb("b2", [R, 256])
        gw_sb = sb("gw", [P, H, E])
        gb_sb = sb("gb", [P, E])
        ones_sb = sb("ones", [P, P])
        ident = sb("ident", [P, P])
        rows_sb = sb("rows", [R, E])
        pick = sb("pick", [R, E, P], BF16)
        x_sb = sb("x", [P, H, CHUNK])
        cent = sb("cent", [P, H, CHUNK])
        sq = sb("sq", [P, H, CHUNK])
        std = sb("std", [P, CHUNK])
        x_again = sb("x_again", [P, H, CHUNK])
        xn = sb("xn", [P, 2, H, CHUNK])
        logit = sb("logit", [P, blocks, E])
        top = sb("top", [P, blocks])
        total = sb("total", [P, blocks])
        probs = sb("probs", [P, blocks, 2 * E])
        sorted8 = sb("sorted8", [P, blocks, E])
        first2 = sb("first2", [P, blocks, E])
        marked = sb("marked", [P, blocks, 2 * E])
        cw = sb("cw", [P, blocks, E])
        rest = sb("rest", [P, blocks, E])
        part = sb("part", [P, 2, blocks, E], BF16)
        cw_parts = sb("cw_parts", [P, blocks, 3, E])
        cw_rows = sb("cw_rows", [R, 2, CHUNK])
        cw_short = sb("cw_short", [R, 2, CHUNK], BF16)
        act_out = sb("act_out", [P, 2, M, CHUNK])
        scaled = sb("scaled", [P, 2, M, CHUNK])
        res = sb("res", [P, H, CHUNK])
        small = psum("small", [P, 512])
        spread = psum("spread", [P, 512])
        hid = psum("hid", [P, M, 512])
        y = psum("y", [P, H, 512])

        pe_a = Track(ctx, nc, "ffn_pe_a", ["mean", "var", "router", "cw_rows"] + [f"h0_{m}" for m in range(M)] + ["cwb0"])
        act_a = Track(ctx, nc, "ffn_act_a", ["square", "sqrt", "exp", "cw_rows", "cw_short"])
        dve_a = Track(ctx, nc, "ffn_dve_a", ["center", "var_eps", "rstd", "norm", "logit", "top", "shift", "total", "inv", "prob"]
                      + [f"sort{b}" for b in range(blocks)] + ["first2"] + [f"mark{b}" for b in range(blocks)] + ["chosen", "cw", "part0", "keep0", "rest", "part1", "keep1", "keep2"])
        pe_b = Track(ctx, nc, "ffn_pe_b", [s for e in range(E) for s in
                                           ([f"h{e + 1}_{m}" for m in range(M)] if e + 1 < E else []) + [f"y{e}"]
                                           + ([f"cwb{e + 1}"] if e + 1 < E else [])])
        act_b = Track(ctx, nc, "ffn_act_b", [f"gelu{e}_{m}" for e in range(E) for m in range(M)])
        dve_b = Track(ctx, nc, "ffn_dve_b", [f"scale{e}_{m}" for e in range(E) for m in range(M)] + ["res"])
        stored_t = Track(ctx, nc, "ffn_res_stored", ["stored"])
        ready = ctx.enter_context(nc.semaphore("ffn_constants"))
        weights = ctx.enter_context(nc.semaphore("ffn_weights"))
        filled = ctx.enter_context(nc.semaphore("ffn_filled"))
        sentinels = ctx.enter_context(nc.semaphore("ffn_sentinels"))
        passed = ctx.enter_context(nc.semaphore("ffn_passed"))
        passed_v = ctx.enter_context(nc.semaphore("ffn_passed_v"))
        loads = Loads(ctx, nc, "ffn_x_loaded")
        again_loads = Loads(ctx, nc, "ffn_x_again_loaded")
        stores = Loads(ctx, nc, "ffn_stored")
        consts = [(b1_sb, b1), (b2_sb, b2), (gw_sb, gate_w), (gb_sb, gate_b),
                  (ones_sb, ones_mean), (ident, identity), (rows_sb, expert_rows)]
        block = ctx.enter_context(nc.Block())

        def schedule(eng, turn):
            turn(-1, 1, b=False)
            turn(0, 0)
            with eng.Fori(0, (turns - 2) // 2) as u:
                turn(u * 2 + 1, 1)
                turn(u * 2 + 2, 0)
            turn(turns - 1, (turns - 1) % 2, a=False)

        @block.sync
        def _(sp):
            stored_t.credit(sp)
            for dst, src in consts:
                sp.dma_start(dst[:], src).then_inc(ready, 16)

            def turn(t, p, a=True, b=True):
                if a:
                    sp.wait_ge(dve_a.sem, dve_a.last_turn(t + 1, "center"))
                    sp.dma_start(x_sb[:], chunk_of(x_dram, t + 1)).then_inc(loads.sem, 16)
                if not b:
                    sp.dma_start(w1_sb[:], w1).then_inc(weights, 16)
                    sp.dma_start(w2_sb[:], w2).then_inc(weights, 16)
                if b:
                    sp.wait_ge(dve_b.sem, dve_b.last_turn(t, "res"))
                    sp.dma_start(x_again[:], chunk_of(x_dram, t)).then_inc(again_loads.sem, 16)
                    sp.wait_ge(dve_b.sem, dve_b.upto(t, "res"))
                    sp.dma_start(chunk_of(out_dram, t), res[:]).then_inc(stores.sem, 16)
                    sp.wait_ge(stores.sem, stores.upto(t))
                    sp.sem_inc(stored_t.done("stored"), 1)
            schedule(sp, turn)

        @block.gpsimd
        def _(pool):
            pool.wait_ge(ready, 16 * len(consts))
            nc.gpsimd.tensor_copy(pick[:], rows_sb[:].unsqueeze(2).to_broadcast([R, E, P])).then_inc(filled, 1)

        @block.tensor
        def _(pe):
            pe_a.credit(pe)
            pe_b.credit(pe)
            pe.wait_ge(ready, 16 * len(consts))
            pe.wait_ge(filled, 1)

            def turn(t, p, a=True, b=True):
                n = 1 - p

                def hidden(tr, e, q):
                    for m in range(M):
                        if e:
                            pe.wait_ge(act_b.sem, act_b.upto(t, f"gelu{e - 1}_{m}"))
                        elif b:
                            pe.wait_ge(act_b.sem, act_b.upto(t, f"gelu{E - 1}_{m}"))
                        for k in range(H):
                            mm = nc.tensor.matmul(hid[:, m], w1_sb[:, e, k, m * P:(m + 1) * P], xn[:, q, k],
                                                  start=(k == 0), stop=(k == H - 1))
                        mm.then_inc(tr.done(f"h{e}_{m}"), 1)

                def spread_weight(tr, e, q):
                    if e or b:
                        pe.wait_ge(dve_b.sem, dve_b.upto(t, f"scale{(e - 1) % E}_{M - 1}"))
                    nc.tensor.matmul(spread[:], pick[:, e], cw_short[:, q], start=True, stop=True).then_inc(tr.done(f"cwb{e}"), 1)

                def side(e):
                    if e == 0:
                        pe.wait_ge(loads.sem, loads.upto(t + 1))
                        pe.wait_ge(act_a.sem, act_a.last_turn(t + 1, "cw_short"))
                        for k in range(H):
                            mm = nc.tensor.matmul(small[:], ones_sb[:], x_sb[:, k], start=(k == 0), stop=(k == H - 1))
                        mm.then_inc(pe_a.done("mean"), 1)
                    if e == 2:
                        pe.wait_ge(act_a.sem, act_a.upto(t + 1, "square"))
                        for k in range(H):
                            mm = nc.tensor.matmul(small[:], ones_sb[:], sq[:, k], start=(k == 0), stop=(k == H - 1))
                        mm.then_inc(pe_a.done("var"), 1)
                    if e == 4:
                        pe.wait_ge(dve_a.sem, dve_a.upto(t + 1, "norm"))
                        for blk in range(blocks):
                            for k in range(H):
                                mm = nc.tensor.matmul(small[:, blk * E:(blk + 1) * E], xn[:, n, k, blk * P:(blk + 1) * P], gw_sb[:, k],
                                                      start=(k == 0), stop=(k == H - 1))
                        mm.then_inc(pe_a.done("router"), 1)
                    if e == 6:
                        pe.wait_ge(dve_a.sem, dve_a.upto(t + 1, "keep2"))
                        pe.sem_inc(passed, 1)
                        for blk in range(blocks):
                            mm = nc.tensor.transpose(small[0:R, blk * P:(blk + 1) * P], cw_parts[:, blk].rearrange("p k e -> p (k e)"), ident[:])
                        mm.then_inc(pe_a.done("cw_rows"), 1)

                for e in range(E):
                    if b and e + 1 < E:
                        hidden(pe_b, e + 1, p)
                    if a and e + 1 == E:
                        if not b:
                            pe.wait_ge(weights, 32)
                        hidden(pe_a, 0, n)
                    if b:
                        for m in range(M):
                            pe.wait_ge(dve_b.sem, dve_b.upto(t, f"scale{e}_{m}"))
                            for d in range(H):
                                mm = nc.tensor.matmul(y[:, d], w2_sb[:, e, m, d * P:(d + 1) * P], scaled[:, e % 2, m],
                                                      start=(e == 0 and m == 0), stop=False, skip_group_check=True)
                        if e == E - 1:
                            for d in range(H):
                                mm = nc.tensor.matmul(y[:, d], b2_sb[:, d * P:(d + 1) * P], cw_rows[:, p],
                                                      start=False, stop=True, skip_group_check=True)
                        mm.then_inc(pe_b.done(f"y{e}"), 1)
                    if b and e + 1 < E:
                        spread_weight(pe_b, e + 1, p)
                    if a and e + 1 == E:
                        pe.wait_ge(act_a.sem, act_a.upto(t + 1, "cw_short"))
                        spread_weight(pe_a, 0, n)
                    if a:
                        side(e)
            schedule(pe, turn)

        @block.scalar
        def _(act):
            act_a.credit(act)
            act_b.credit(act)
            act.wait_ge(ready, 16 * len(consts))

            def turn(t, p, a=True, b=True):
                n = 1 - p
                A = t + 1

                def side(e):
                    if e == 1:
                        act.wait_ge(dve_a.sem, dve_a.upto(A, "center"))
                        nc.scalar.activation(sq[:], cent[:], ACT.Square).then_inc(act_a.done("square"), 1)
                    if e == 3:
                        act.wait_ge(dve_a.sem, dve_a.upto(A, "var_eps"))
                        nc.scalar.activation(std[:], std[:], ACT.Sqrt).then_inc(act_a.done("sqrt"), 1)
                    if e == 5:
                        act.wait_ge(dve_a.sem, dve_a.upto(A, "shift"))
                        nc.scalar.activation(logit[:], logit[:], ACT.Exp).then_inc(act_a.done("exp"), 1)
                    if e == 7:
                        act.wait_ge(pe_a.sem, pe_a.upto(A, "cw_rows"))
                        nc.scalar.copy(cw_rows[:, n], small[0:R]).then_inc(act_a.done("cw_rows"), 1)
                        nc.scalar.copy(cw_short[:, n], small[0:R]).then_inc(act_a.done("cw_short"), 1)

                for e in range(E):
                    if b:
                        for m in range(M):
                            tr = pe_b if e else pe_a
                            act.wait_ge(tr.sem, tr.upto(t, f"h{e}_{m}"))
                            act.wait_ge(dve_b.sem, dve_b.upto(t, f"scale{e - 2}_{m}") if e >= 2 else dve_b.last_turn(t, f"scale{e + E - 2}_{m}"))
                            nc.scalar.activation(act_out[:, e % 2, m], hid[:, m], ACT.Gelu,
                                                 bias=b1_sb[:, e, m:m + 1]).then_inc(act_b.done(f"gelu{e}_{m}"), 1)
                    if a:
                        side(e)
            schedule(act, turn)

        @block.vector
        def _(v):
            dve_a.credit(v)
            dve_b.credit(v)
            nc.vector.memset(probs[:], -1.0).then_inc(sentinels, 1)
            nc.vector.memset(first2[:], -1.0).then_inc(sentinels, 1)
            v.wait_ge(sentinels, 2)
            v.wait_ge(ready, 16 * len(consts))

            def turn(t, p, a=True, b=True):
                n = 1 - p
                A = t + 1

                def own():
                    v.wait_ge(dve_a.sem, dve_a.so_far(A))

                def side(e):
                    if e == 0:
                        v.wait_ge(pe_a.sem, pe_a.upto(A, "mean"))
                        v.wait_ge(act_a.sem, act_a.last_turn(A, "square"))
                        own()
                        nc.vector.tensor_tensor(cent[:], x_sb[:], small[:].unsqueeze(1).to_broadcast([P, H, CHUNK]),
                                                ALU.subtract).then_inc(dve_a.done("center"), 1)
                    if e == 2:
                        v.wait_ge(pe_a.sem, pe_a.upto(A, "var"))
                        own()
                        nc.vector.tensor_scalar_add(std[:], small[:], LN_EPS).then_inc(dve_a.done("var_eps"), 1)
                    if e == 3:
                        v.wait_ge(act_a.sem, act_a.upto(A, "sqrt"))
                        nc.vector.reciprocal(std[:], std[:]).then_inc(dve_a.done("rstd"), 1)
                        own()
                        nc.vector.tensor_tensor(xn[:, n], cent[:], std[:].unsqueeze(1).to_broadcast([P, H, CHUNK]),
                                                ALU.mult).then_inc(dve_a.done("norm"), 1)
                    if e == 4:
                        v.wait_ge(pe_a.sem, pe_a.upto(A, "router"))
                        own()
                        nc.vector.tensor_tensor(logit[:], small[:, 0:blocks * E].rearrange("p (b e) -> p b e", e=E),
                                                gb_sb[:].unsqueeze(1).to_broadcast([P, blocks, E]), ALU.add).then_inc(dve_a.done("logit"), 1)
                        own()
                        nc.vector.tensor_reduce(top[:], logit[:], AX.X, ALU.max).then_inc(dve_a.done("top"), 1)
                        own()
                        nc.vector.tensor_tensor(logit[:], logit[:], top[:].unsqueeze(2).to_broadcast([P, blocks, E]),
                                                ALU.subtract).then_inc(dve_a.done("shift"), 1)
                    if e == 5:
                        v.wait_ge(act_a.sem, act_a.upto(A, "exp"))
                        nc.vector.tensor_reduce(total[:], logit[:], AX.X, ALU.add).then_inc(dve_a.done("total"), 1)
                        own()
                        nc.vector.reciprocal(total[:], total[:]).then_inc(dve_a.done("inv"), 1)
                        own()
                        nc.vector.tensor_tensor(probs[:, :, 0:E], logit[:], total[:].unsqueeze(2).to_broadcast([P, blocks, E]),
                                                ALU.mult).then_inc(dve_a.done("prob"), 1)
                        own()
                        v.sem_inc(passed_v, 1)
                        for blk in range(blocks):
                            nc.vector.max(sorted8[:, blk], probs[:, blk, 0:E]).then_inc(dve_a.done(f"sort{blk}"), 1)
                        own()
                        nc.vector.tensor_copy(first2[:, :, 0:2], sorted8[:, :, 0:2]).then_inc(dve_a.done("first2"), 1)
                        own()
                        v.sem_inc(passed_v, 1)
                        for blk in range(blocks):
                            nc.vector.match_replace(marked[:, blk], first2[:, blk], probs[:, blk], -2.0).then_inc(dve_a.done(f"mark{blk}"), 1)
                        own()
                        nc.vector.tensor_tensor(marked[:, :, 0:E], marked[:, :, 0:E], probs[:, :, 0:E],
                                                ALU.not_equal).then_inc(dve_a.done("chosen"), 1)
                        own()
                        nc.vector.tensor_tensor(cw[:], marked[:, :, 0:E], probs[:, :, 0:E], ALU.mult).then_inc(dve_a.done("cw"), 1)
                        own()
                        nc.vector.tensor_copy(part[:, 0], cw[:]).then_inc(dve_a.done("part0"), 1)
                        own()
                        nc.vector.tensor_copy(cw_parts[:, :, 0], part[:, 0]).then_inc(dve_a.done("keep0"), 1)
                        nc.vector.tensor_tensor(rest[:], cw[:], part[:, 0], ALU.subtract).then_inc(dve_a.done("rest"), 1)
                        own()
                        nc.vector.tensor_copy(part[:, 1], rest[:]).then_inc(dve_a.done("part1"), 1)
                        own()
                        nc.vector.tensor_copy(cw_parts[:, :, 1], part[:, 1]).then_inc(dve_a.done("keep1"), 1)
                        nc.vector.tensor_tensor(cw_parts[:, :, 2], rest[:], part[:, 1], ALU.subtract).then_inc(dve_a.done("keep2"), 1)

                for e in range(E):
                    if b:
                        tr = pe_b if e else pe_a
                        v.wait_ge(tr.sem, tr.upto(t, f"cwb{e}"))
                        for m in range(M):
                            v.wait_ge(act_b.sem, act_b.upto(t, f"gelu{e}_{m}"))
                            if m == 0:
                                v.wait_ge(pe_b.sem, pe_b.upto(t, f"y{e - 2}") if e >= 2 else pe_b.last_turn(t, f"y{e + E - 2}"))
                            nc.vector.tensor_tensor(scaled[:, e % 2, m], act_out[:, e % 2, m], spread[:],
                                                    ALU.mult).then_inc(dve_b.done(f"scale{e}_{m}"), 1)
                    if a:
                        side(e)
                if b:
                    v.wait_ge(pe_b.sem, pe_b.upto(t, f"y{E - 1}"))
                    v.wait_ge(again_loads.sem, again_loads.upto(t))
                    v.wait_ge(stored_t.sem, stored_t.last_turn(t, "stored"))
                    nc.vector.tensor_tensor(res[:], y[:], x_again[:], ALU.add).then_inc(dve_b.done("res"), 1)
            schedule(v, turn)


def conv_arrays(i, pre=""):
    g = lambda n: i[pre + n]
    blocks = lambda m, k: m.T.reshape(k, P, m.shape[0]).transpose(1, 0, 2)
    halves = lambda v: v.reshape(HALVES, P).T
    lane, t, a = np.meshgrid(np.arange(P) // POINTS, np.arange(ROWPAIRS), np.arange(CELLS), indexing="ij")
    coords = np.stack([lane // 2 * CELLS + a, 2 * t + lane % 2], 1).reshape(P, 2, -1).astype(np.float32)
    parts = np.array([(0, 0), (0, 1), (1, 0), (1, 1), (0, 2), (2, 0), (1, 2), (2, 1)])
    minus = -np.repeat(np.stack([parts >= 1, parts >= 2], 2), QC, 0).astype(np.float32)
    return {
        "high": g("high_feature").reshape(BATCH, HALVES, P, 1024).transpose(0, 2, 1, 3),
        "w1": blocks(g("W1"), 4), "w2": blocks(g("W2"), 2), "b1": g("b1").reshape(P, 1), "b2": g("b2").reshape(P, 1),
        "wq": np.tile(g("Wq").T, (1, 8)), "wk": np.tile(g("Wk").T, (1, 8)), "wv": g("Wv").T,
        "bq": np.tile(g("bq").reshape(QC, 1), (8, 1)), "bk": np.tile(g("bk").reshape(QC, 1), (8, 1)), "minus": minus,
        "bv": np.broadcast_to(g("bv"), (P, P)),
        "woff": g("Woff").reshape(POINTS, 2, P).transpose(2, 1, 0),
        "boff": np.tile(g("boff").reshape(POINTS, 2), (LANES, 1)),
        "wbv": g("Wb")[:, :P].T, "wbh": blocks(g("Wb")[:, P:], 2),
        "gamma": halves(g("gamma")), "beta": halves(g("beta")), "rmean": halves(g("rmean")), "rvar": halves(g("rvar")),
        "gmean": np.kron(np.eye(P // 8), np.full((8, 8), 1 / 8)).astype(np.float32),
        "coords": coords, "ramp": np.broadcast_to(np.arange(SIDE, dtype=np.float32), (P, SIDE)),
        "id": np.eye(P, dtype=np.float32),
    }


def units(x):
    return x.reshape(BATCH, HALVES, P, UNITS, UNIT).transpose(3, 2, 1, 0, 4).reshape(UNITS, P, HALVES, BATCH * UNIT)


def ununits(x):
    return np.ascontiguousarray(x.reshape(UNITS, P, HALVES, BATCH, UNIT).transpose(3, 2, 1, 0, 4).reshape(BATCH, 256, 64, 64))


def attn_arrays(i, pre=""):
    g = lambda n: i[pre + n]
    head_rows = np.zeros((P, HALVES, BATCH, ROWS), np.float32)
    for p in range(P):
        for h in range(HALVES):
            for b in range(BATCH):
                head_rows[p, h, b, b * HEADS + h * 4 + p // 32] = 1.0
    tok = np.arange(P)
    a = {}
    for n in "qkvo":
        a["a_w" + n] = g(f"w{n}_w").T.reshape(HALVES, P, 256).transpose(1, 0, 2)
        a["a_b" + n] = g(f"w{n}_b").reshape(HALVES, P).T
    a["a_wg"] = g("wg_w").reshape(32, 32)
    a["a_wgb"] = np.broadcast_to(g("wg_b").reshape(1, 1), (ROWS, 1))
    a["a_kvs"] = g("kv_norm_scale").reshape(HEADS, 32, 32)
    a["a_qks"] = np.tile(g("qk_norm_scale").reshape(HEADS, 1), (BATCH, 1))
    a["c_ones"] = np.full((P, P), 1 / 256, np.float32)
    a["c_id"] = np.eye(P, dtype=np.float32)
    a["c_hr"] = head_rows
    a["c_hc"] = head_rows.transpose(3, 1, 2, 0)
    a["c_mask"] = np.stack([(tok % 32 // GROUP == m) for m in range(2)], 1).astype(np.float32)
    return a


def chunked(x):
    return x.reshape(BATCH, HALVES, P, CHUNKS, CHUNK).transpose(0, 3, 2, 1, 4).reshape(-1, P, HALVES, CHUNK)


ATTN_ARGS = ["a_wq", "a_wk", "a_wv", "a_wo", "a_bq", "a_bk", "a_bv", "a_bo", "a_wg", "a_wgb", "a_kvs", "a_qks",
             "c_ones", "c_id", "c_hr", "c_hc", "c_mask"]


def ffn_arrays(i, pre=""):
    g = lambda n: i[pre + n]
    return {
        "f_gw": g("gate_w").reshape(HALVES, P, EXPERTS).transpose(1, 0, 2),
        "f_gb": np.broadcast_to(g("gate_b"), (P, EXPERTS)),
        "f_w1": g("W1").reshape(EXPERTS, HALVES, P, 512).transpose(2, 0, 1, 3),
        "f_b1": g("b1").reshape(EXPERTS, 4, P).transpose(2, 0, 1),
        "f_w2": g("W2").reshape(EXPERTS, 4, P, 256).transpose(2, 0, 1, 3),
        "f_b2": np.tile(g("b2"), (3, 1)),
        "c_rows": np.tile(np.eye(EXPERTS, dtype=np.float32), (3, 1)),
    }


FFN_ARGS = ["f_gw", "f_gb", "f_w1", "f_b1", "f_w2", "f_b2", "c_ones", "c_id", "c_rows"]


def build(nc, arrays):
    d = {k: nc.dram_tensor(f"in_{k}", a.shape, F32, kind="ExternalInput").ap() for k, a in arrays.items()}
    shape = (BATCH * CHUNKS, P, HALVES, CHUNK)
    base, x1, x2 = (nc.dram_tensor(n, shape, F32, kind="Internal").ap() for n in ("base", "after_conv", "after_attention"))
    out = nc.dram_tensor("out", shape, F32, kind="ExternalOutput").ap()
    conv_layer(nc, d["x_in"], base, x1, d)
    attn_phase(nc, x1, x2, *[d[n] for n in ATTN_ARGS])
    ffn_phase(nc, x2, out, *[d[n] for n in FFN_ARGS])


def kernel(**inputs):
    import concourse.bacc as bacc
    from concourse.bass_utils import run_bass_kernel_spmd as run

    i = {k: np.asarray(v) for k, v in inputs.items()}
    arrays = {"x_in": chunked(i["x"])}
    arrays.update(conv_arrays(i, "L0_conv_"))
    arrays.update(attn_arrays(i, "L1_attn_"))
    arrays.update(ffn_arrays(i, "L1_ffn_"))
    arrays = {k: np.ascontiguousarray(a) for k, a in arrays.items()}
    nc = bacc.Bacc("TRN2", target_bir_lowering=False, num_devices=1)
    build(nc, arrays)
    r = run(nc, [{f"in_{k}": a for k, a in arrays.items()}], core_ids=[0])
    return ununits(r.results[0]["out"])
```
